# Optimizing a Trainium2 kernel written in Bass

```python
import numpy as np
import jax
import jax.numpy as jnp

def _softmax(x, axis=-1):
    return jax.nn.softmax(x, axis=axis)

def _gelu(x):
    return jax.nn.gelu(x, approximate=True)

def _silu(x):
    return jax.nn.silu(x)

def _sigmoid(x):
    return jax.nn.sigmoid(x)

def _layernorm(x, axis=-1, eps=1e-05):
    m = jnp.mean(x, axis=axis, keepdims=True)
    v = jnp.var(x, axis=axis, keepdims=True)
    return (x - m) / jnp.sqrt(v + eps)

def _scatter_add(tgt, idx, src, axis=0):
    return tgt.at[idx].add(src)

def _segment_sum(src, seg, n):
    return jax.ops.segment_sum(src, seg, n)
kernel_name = 'mk_decoder_preln_d2_seqx_r8_f12434'

def setup_inputs(seed: int=0):
    np.random.seed(seed)
    _w = jnp.asarray

    def _rec_inputs():
        import jax
        import jax.numpy as jnp
        _rk = jax.random.key(seed)
        x = 7.22e-05 + 1 * jax.random.normal(jax.random.fold_in(_rk, 1), (8, 128, 512), jnp.float32)
        _lenS = 128 - jax.random.randint(jax.random.fold_in(_rk, 7), (8,), 0, max(1, 128 // 4) + 1, jnp.int32)
        _lenS2 = 128 - jax.random.randint(jax.random.fold_in(_rk, 8), (8,), 0, max(1, 128 // 4) + 1, jnp.int32)
        _ctx_4096P = jax.random.normal(jax.random.fold_in(_rk, 11), (8, 16, 512), jnp.float32)
        _ctx_4096c = jax.random.dirichlet(jax.random.fold_in(_rk, 511), 0.3 * jnp.ones((16,), jnp.float32), (8, 128))
        _ctx_4096t = jnp.einsum('bsk,bkd->bsd', _ctx_4096c, _ctx_4096P)
        _ctx_4096t = _ctx_4096t * jax.lax.rsqrt(jnp.mean(jnp.square(_ctx_4096t)) + 1e-12) * 0.953939
        ctx_4096 = 4.13588e-05 + 0.999923 * (_ctx_4096t + 0.3 * jax.random.normal(jax.random.fold_in(_rk, 611), (8, 128, 512), jnp.float32))
        fside_Bx32xSxS2_0 = 1.74963e-06 + 0.0200011 * jax.random.normal(jax.random.fold_in(_rk, 13), (8, 32, 128, 128), jnp.float32)
        _validS = jnp.arange(128)[None, :] < _lenS[:, None]
        _validS2 = jnp.arange(128)[None, :] < _lenS2[:, None]
        _causal = jnp.tril(jnp.ones((128, 128), dtype=bool))
        mask_BxSxS2_bk0 = jnp.logical_not(jnp.broadcast_to(_validS2[:, None, :], (8, 128, 128)))
        return (x, ctx_4096, fside_Bx32xSxS2_0, mask_BxSxS2_bk0)
    x, ctx_4096, fside_Bx32xSxS2_0, mask_BxSxS2_bk0 = _rec_inputs()

    def _L0_attn_setup():
        import jax, jax.numpy as jnp
        import numpy as np
        B, T, H, S, F, G = (2, 256, 512, 128, 1248, 6)
        GRAD_ORDER_MIN = 4
        THD = 2.5
        key = jax.random.key(seed)
        ks = jax.random.split(key, 9)
        sc = 0.02
        hidden_states = jax.random.normal(ks[0], (B, T, H), jnp.float32)
        up_w = jax.random.normal(ks[1], (S, H), jnp.float32) * sc
        gate_w = jax.random.normal(ks[2], (S, H), jnp.float32) / np.sqrt(H)
        local_point = jax.random.normal(ks[3], (S,), jnp.float32)
        local_approx_output = jax.random.normal(ks[4], (H, S), jnp.float32) * sc
        fuse_weight = jax.random.normal(ks[5], (H, S, G), jnp.float32) * sc
        discount_factor = jnp.asarray(np.cumsum(np.log(np.arange(1, G + 1, dtype=np.float64))), jnp.float32)
        ffn_gate_w = jax.random.normal(ks[6], (F, H), jnp.float32) * sc
        ffn_up_w = jax.random.normal(ks[7], (F, H), jnp.float32) * sc
        ffn_down_w = jax.random.normal(ks[8], (H, F), jnp.float32) * sc
        return {'hidden_states': hidden_states, 'up_w': up_w, 'gate_w': gate_w, 'local_point': local_point, 'local_approx_output': local_approx_output, 'fuse_weight': fuse_weight, 'discount_factor': discount_factor, 'ffn_gate_w': ffn_gate_w, 'ffn_up_w': ffn_up_w, 'ffn_down_w': ffn_down_w}
    _L0_attn_all = _L0_attn_setup()
    _L0_attn_in = {k: v for k, v in _L0_attn_all.items() if k in ('up_w', 'gate_w', 'local_point', 'local_approx_output', 'fuse_weight', 'discount_factor', 'ffn_gate_w', 'ffn_up_w', 'ffn_down_w')}
    del _L0_attn_all

    def _L0_xattn_setup():
        import jax, jax.numpy as jnp
        import numpy as np
        B, S, D, H, DH = (2, 128, 512, 32, 128)
        key = jax.random.key(seed)
        ks = jax.random.split(key, 7)
        hidden_q = jax.random.normal(ks[0], (B, S, D), dtype=jnp.float32)
        hidden_kv = jax.random.normal(ks[1], (B, S, D), dtype=jnp.float32)
        attention_mask = jnp.tril(jnp.ones((B, S, S), dtype=bool))
        position_bias = jax.random.normal(ks[2], (B, H, S, S), dtype=jnp.float32) * 0.02
        Wq = jax.random.normal(ks[3], (D, H * DH), dtype=jnp.float32) * 0.02
        Wk = jax.random.normal(ks[4], (D, H * DH), dtype=jnp.float32) * 0.02
        Wv = jax.random.normal(ks[5], (D, H * DH), dtype=jnp.float32) * 0.02
        Wo = jax.random.normal(ks[6], (H * DH, D), dtype=jnp.float32) * 0.02
        return {'hidden_q': hidden_q, 'hidden_kv': hidden_kv, 'attention_mask': attention_mask, 'position_bias': position_bias, 'Wq': Wq, 'Wk': Wk, 'Wv': Wv, 'Wo': Wo}
    _L0_xattn_all = _L0_xattn_setup()
    _L0_xattn_in = {k: v for k, v in _L0_xattn_all.items() if k in ('Wq', 'Wk', 'Wv', 'Wo')}
    del _L0_xattn_all

    def _L0_ffn_setup():
        import jax, jax.numpy as jnp
        import numpy as np
        import math
        B, S, IN, OUT = (4, 256, 512, 512)
        E, R, K = (8, 64, 128)
        SCALE = 64.0 / 64.0
        MULTIPLIER = 1.0
        key = jax.random.key(seed)
        ks = jax.random.split(key, 6)
        return {'x': jax.random.normal(ks[0], (B, S, IN), jnp.float32), 'W_org': jax.random.normal(ks[1], (OUT, IN), jnp.float32) * 0.02, 'lora_down': jax.random.normal(ks[2], (E, IN, R), jnp.float32) * 0.02, 'lora_up': jax.random.normal(ks[3], (E, R, OUT), jnp.float32) * 0.02, 'lora_keys': jax.random.normal(ks[4], (E, K), jnp.float32), 'Wq': jax.random.normal(ks[5], (K, IN), jnp.float32) * 0.02}
    _L0_ffn_all = _L0_ffn_setup()
    _L0_ffn_in = {k: v for k, v in _L0_ffn_all.items() if k in ('W_org', 'lora_down', 'lora_up', 'lora_keys', 'Wq')}
    del _L0_ffn_all

    def _L1_attn_setup():
        import jax, jax.numpy as jnp
        import numpy as np
        BATCH, SEQ, HIDDEN = (2, 512, 512)
        HEADS, HEAD_DIM, BLOCK = (32, 128, 32)
        LAYER_IDX, N_LAYERS = (1, 32)
        EPS = 1e-05

        def _decays():
            base = 1.0 / 2.0 ** (8.0 / HEADS)
            exponent = jnp.arange(HEADS, dtype=jnp.float32) + 1.0
            factor = 1.0 - LAYER_IDX / (N_LAYERS - 1 + 1e-05) + 1e-05
            slope = (base ** exponent * factor)[:, None, None]
            r = jnp.arange(BLOCK, dtype=jnp.float32) + 1.0
            q_decay = jnp.exp(-slope * r[:, None])
            k_decay = jnp.exp(-slope * (BLOCK - r)[:, None])
            diff = r[:, None] - r[None, :]
            diag = slope[None] * diff[None, None]
            diag = jnp.where(diag >= 0, -diag, -jnp.inf)
            diag_decay = jnp.exp(diag)
            block_decay = jnp.exp(-slope * BLOCK)
            return (q_decay, k_decay, diag_decay, block_decay)
        key = jax.random.key(seed)
        ks = jax.random.split(key, 5)
        s = 0.02
        return {'hidden_states': jax.random.normal(ks[0], (BATCH, SEQ, HIDDEN), jnp.float32), 'qkv_w': jax.random.normal(ks[1], (3 * HEADS * HEAD_DIM, HIDDEN), jnp.float32) * s, 'out_w': jax.random.normal(ks[2], (HIDDEN, HEADS * HEAD_DIM), jnp.float32) * s, 'gate_w': jax.random.normal(ks[3], (HEADS * HEAD_DIM, HIDDEN), jnp.float32) * s, 'norm_w': jnp.ones((HEADS * HEAD_DIM,), jnp.float32)}
    _L1_attn_all = _L1_attn_setup()
    _L1_attn_in = {k: v for k, v in _L1_attn_all.items() if k in ('qkv_w', 'out_w', 'gate_w', 'norm_w')}
    del _L1_attn_all

    def _L1_xattn_setup():
        import jax, jax.numpy as jnp
        import numpy as np
        EMBED = 512
        HEADS = 32
        GROUP = 4
        KV_HEADS = HEADS // GROUP
        HEAD_DIM = EMBED // HEADS
        B, S = (2, 256)
        key = jax.random.key(seed)
        ks = jax.random.split(key, 7)
        scale = 0.02
        return {'queries': jax.random.normal(ks[0], (B, S, EMBED), dtype=jnp.float32), 'keys': jax.random.normal(ks[1], (B, S, EMBED), dtype=jnp.float32), 'values': jax.random.normal(ks[2], (B, S, EMBED), dtype=jnp.float32), 'Wq': jax.random.normal(ks[3], (EMBED, EMBED), dtype=jnp.float32) * scale, 'Wk': jax.random.normal(ks[4], (EMBED, KV_HEADS * HEAD_DIM), dtype=jnp.float32) * scale, 'Wv': jax.random.normal(ks[5], (EMBED, KV_HEADS * HEAD_DIM), dtype=jnp.float32) * scale, 'Wo': jax.random.normal(ks[6], (EMBED, EMBED), dtype=jnp.float32) * scale}
    _L1_xattn_all = _L1_xattn_setup()
    _L1_xattn_in = {k: v for k, v in _L1_xattn_all.items() if k in ('Wq', 'Wk', 'Wv', 'Wo')}
    del _L1_xattn_all

    def _L1_ffn_setup():
        import jax, jax.numpy as jnp
        import numpy as np
        GROUP_SIZE = 32
        OUT_FEATURES = 512
        IN_FEATURES = 512

        def _unpack_3bit(p):
            b0, b1, b2 = (p[..., 0], p[..., 1], p[..., 2])
            v0 = b0 & 7
            v1 = b0 >> 3 & 7
            v2 = b0 >> 6 & 3 | (b1 & 1) << 2
            v3 = b1 >> 1 & 7
            v4 = b1 >> 4 & 7
            v5 = b1 >> 7 & 1 | (b2 & 3) << 1
            v6 = b2 >> 2 & 7
            v7 = b2 >> 5 & 7
            return jnp.stack([v0, v1, v2, v3, v4, v5, v6, v7], axis=-1)

        def _block_dequantize_3bit(packed, normalization, group_size=GROUP_SIZE):
            p = packed.astype(jnp.uint8).reshape(-1, group_size // 8, 3)
            q = _unpack_3bit(p).reshape(-1, group_size).astype(jnp.float32)
            n = normalization.astype(jnp.float32)
            x_norm = q / 7.0
            return (x_norm * (2.0 * n) - n).reshape(-1)
        key = jax.random.key(seed)
        k1, k2, k3, k4 = jax.random.split(key, 4)
        n_groups = OUT_FEATURES * IN_FEATURES // GROUP_SIZE
        packed_cols = GROUP_SIZE * 3 // 8
        x = jax.random.normal(k1, (2, 256, IN_FEATURES), dtype=jnp.float32)
        weight_q3 = jax.random.randint(k2, (n_groups, packed_cols), 0, 32, dtype=jnp.int32).astype(jnp.int8)
        weight_norm = jax.random.uniform(k3, (n_groups, 1), dtype=jnp.float32, minval=0.05, maxval=1.0)
        bias = jax.random.normal(k4, (OUT_FEATURES,), dtype=jnp.float32) * 0.02
        return {'x': x, 'weight_q3': weight_q3, 'weight_norm': weight_norm, 'bias': bias}
    _L1_ffn_all = _L1_ffn_setup()
    _L1_ffn_in = {k: v for k, v in _L1_ffn_all.items() if k in ('weight_q3', 'weight_norm', 'bias')}
    del _L1_ffn_all
    return {'x': x, 'ctx_4096': ctx_4096, 'fside_Bx32xSxS2_0': fside_Bx32xSxS2_0, 'mask_BxSxS2_bk0': mask_BxSxS2_bk0, 'L0_attn_up_w': _L0_attn_in['up_w'], 'L0_attn_gate_w': _L0_attn_in['gate_w'], 'L0_attn_local_point': _L0_attn_in['local_point'], 'L0_attn_local_approx_output': _L0_attn_in['local_approx_output'], 'L0_attn_fuse_weight': _L0_attn_in['fuse_weight'], 'L0_attn_discount_factor': _L0_attn_in['discount_factor'], 'L0_attn_ffn_gate_w': _L0_attn_in['ffn_gate_w'], 'L0_attn_ffn_up_w': _L0_attn_in['ffn_up_w'], 'L0_attn_ffn_down_w': _L0_attn_in['ffn_down_w'], 'L0_xattn_Wq': _L0_xattn_in['Wq'], 'L0_xattn_Wk': _L0_xattn_in['Wk'], 'L0_xattn_Wv': _L0_xattn_in['Wv'], 'L0_xattn_Wo': _L0_xattn_in['Wo'], 'L0_ffn_W_org': _L0_ffn_in['W_org'], 'L0_ffn_lora_down': _L0_ffn_in['lora_down'], 'L0_ffn_lora_up': _L0_ffn_in['lora_up'], 'L0_ffn_lora_keys': _L0_ffn_in['lora_keys'], 'L0_ffn_Wq': _L0_ffn_in['Wq'], 'L1_attn_qkv_w': _L1_attn_in['qkv_w'], 'L1_attn_out_w': _L1_attn_in['out_w'], 'L1_attn_gate_w': _L1_attn_in['gate_w'], 'L1_attn_norm_w': _L1_attn_in['norm_w'], 'L1_xattn_Wq': _L1_xattn_in['Wq'], 'L1_xattn_Wk': _L1_xattn_in['Wk'], 'L1_xattn_Wv': _L1_xattn_in['Wv'], 'L1_xattn_Wo': _L1_xattn_in['Wo'], 'L1_ffn_weight_q3': _L1_ffn_in['weight_q3'], 'L1_ffn_weight_norm': _L1_ffn_in['weight_norm'], 'L1_ffn_bias': _L1_ffn_in['bias']}

def reference(x, ctx_4096, fside_Bx32xSxS2_0, mask_BxSxS2_bk0, L0_attn_up_w, L0_attn_gate_w, L0_attn_local_point, L0_attn_local_approx_output, L0_attn_fuse_weight, L0_attn_discount_factor, L0_attn_ffn_gate_w, L0_attn_ffn_up_w, L0_attn_ffn_down_w, L0_xattn_Wq, L0_xattn_Wk, L0_xattn_Wv, L0_xattn_Wo, L0_ffn_W_org, L0_ffn_lora_down, L0_ffn_lora_up, L0_ffn_lora_keys, L0_ffn_Wq, L1_attn_qkv_w, L1_attn_out_w, L1_attn_gate_w, L1_attn_norm_w, L1_xattn_Wq, L1_xattn_Wk, L1_xattn_Wv, L1_xattn_Wo, L1_ffn_weight_q3, L1_ffn_weight_norm, L1_ffn_bias):
    import jax
    import jax.numpy as jnp

    def _L0_attn_ref(hidden_states, up_w, gate_w, local_point, local_approx_output, fuse_weight, discount_factor, ffn_gate_w, ffn_up_w, ffn_down_w):
        import jax, jax.numpy as jnp
        import numpy as np
        B, T, H, S, F, G = (2, 256, 512, 128, 1248, 6)
        GRAD_ORDER_MIN = 4
        THD = 2.5
        approx_up = hidden_states @ up_w.T
        gate_pre = hidden_states @ gate_w.T
        delta = gate_pre - local_point
        neg_factor = jnp.where(delta > 0, 1.0, -1.0).astype(hidden_states.dtype)
        delta_abs = jnp.abs(delta)
        log_delta = jnp.log(delta_abs)
        keep = (delta_abs <= THD).astype(hidden_states.dtype)
        approx_out = approx_up @ local_approx_output.T
        for idx in range(G):
            m = idx + 1
            dterm = jnp.exp(log_delta * m - discount_factor[idx])
            if m % 2 == 1:
                dterm = dterm * neg_factor
            tmp = dterm * approx_up
            if m > GRAD_ORDER_MIN:
                tmp = tmp * keep
            approx_out = approx_out + tmp @ fuse_weight[:, :, idx].T
        ffn_out = jax.nn.silu(hidden_states @ ffn_gate_w.T) * (hidden_states @ ffn_up_w.T) @ ffn_down_w.T
        return approx_out + ffn_out

    def _L0_xattn_ref(hidden_q, hidden_kv, attention_mask, position_bias, Wq, Wk, Wv, Wo):
        import jax, jax.numpy as jnp
        import numpy as np
        B, S, D, H, DH = (2, 128, 512, 32, 128)
        b, lq, _ = hidden_q.shape
        lk = hidden_kv.shape[1]
        h, dh = (H, DH)
        q = (hidden_q @ Wq).reshape(b, lq, h, dh)
        k = (hidden_kv @ Wk).reshape(b, lk, h, dh)
        v = (hidden_kv @ Wv).reshape(b, lk, h, dh)
        scale = 1.0 / jnp.sqrt(jnp.asarray(dh, dtype=q.dtype))
        score = jnp.einsum('bqhd,bkhd->bhqk', q, k) * scale + position_bias
        mask = attention_mask[:, None, :, :]
        neg_inf = jnp.asarray(-jnp.inf, dtype=score.dtype)
        score = jnp.where(mask, score, neg_inf)
        probs = jax.nn.softmax(score, axis=-1)
        probs = jnp.where(mask, probs, jnp.asarray(0, dtype=probs.dtype))
        ctx = jnp.einsum('bhqk,bkhd->bqhd', probs, v).reshape(b, lq, h * dh)
        return ctx @ Wo

    def _L0_ffn_ref(x, W_org, lora_down, lora_up, lora_keys, Wq):
        import jax, jax.numpy as jnp
        import numpy as np
        import math
        B, S, IN, OUT = (4, 256, 512, 512)
        E, R, K = (8, 64, 128)
        SCALE = 64.0 / 64.0
        MULTIPLIER = 1.0
        base = jnp.einsum('bsi,oi->bso', x, W_org)
        q = jnp.einsum('bi,ki->bk', x.mean(axis=1), Wq)
        scores = jnp.einsum('bk,ek->be', q, lora_keys) / math.sqrt(K)
        coeffs = jax.nn.softmax(scores, axis=-1)
        h = jnp.einsum('bsi,eir->bser', x, lora_down)
        delta = jnp.einsum('be,bser,ero->bso', coeffs, h, lora_up)
        return base + delta * (SCALE * MULTIPLIER)

    def _L1_attn_ref(hidden_states, qkv_w, out_w, gate_w, norm_w):
        import jax, jax.numpy as jnp
        import numpy as np
        BATCH, SEQ, HIDDEN = (2, 512, 512)
        HEADS, HEAD_DIM, BLOCK = (32, 128, 32)
        LAYER_IDX, N_LAYERS = (1, 32)
        EPS = 1e-05

        def _decays():
            base = 1.0 / 2.0 ** (8.0 / HEADS)
            exponent = jnp.arange(HEADS, dtype=jnp.float32) + 1.0
            factor = 1.0 - LAYER_IDX / (N_LAYERS - 1 + 1e-05) + 1e-05
            slope = (base ** exponent * factor)[:, None, None]
            r = jnp.arange(BLOCK, dtype=jnp.float32) + 1.0
            q_decay = jnp.exp(-slope * r[:, None])
            k_decay = jnp.exp(-slope * (BLOCK - r)[:, None])
            diff = r[:, None] - r[None, :]
            diag = slope[None] * diff[None, None]
            diag = jnp.where(diag >= 0, -diag, -jnp.inf)
            diag_decay = jnp.exp(diag)
            block_decay = jnp.exp(-slope * BLOCK)
            return (q_decay, k_decay, diag_decay, block_decay)
        b, s, _ = hidden_states.shape
        h, d, bs = (HEADS, HEAD_DIM, BLOCK)
        nb = s // bs
        q_decay, k_decay, diag_decay, block_decay = _decays()
        qkv = jax.nn.silu(hidden_states @ qkv_w.T)
        qkv = qkv.reshape(b, s, h, 3, d)
        q = jnp.moveaxis(qkv[:, :, :, 0], 2, 1)
        k = jnp.moveaxis(qkv[:, :, :, 1], 2, 1)
        v = jnp.moveaxis(qkv[:, :, :, 2], 2, 1)

        def to_blocks(x):
            return jnp.moveaxis(x.reshape(b, h, nb, bs, d), 2, 0)
        qb, kb, vb = (to_blocks(q), to_blocks(k), to_blocks(v))

        def step(kv, blk):
            cq, ck, cv = blk
            scores = jnp.einsum('bhnd,bhmd->bhnm', cq, ck) * diag_decay
            intra = jnp.einsum('bhnm,bhmd->bhnd', scores, cv)
            inter = jnp.einsum('bhnd,bhde->bhne', cq * q_decay, kv)
            kv_next = kv * block_decay + jnp.einsum('bhnd,bhne->bhde', ck * k_decay, cv)
            return (kv_next, intra + inter)
        kv0 = jnp.zeros((b, h, d, d), hidden_states.dtype)
        _, out_blocks = jax.lax.scan(step, kv0, (qb, kb, vb))
        attn = jnp.moveaxis(out_blocks, 0, 2)
        attn = attn.reshape(b, h, s, d).transpose(0, 2, 1, 3).reshape(b, s, h * d)
        xf = attn.astype(jnp.float32)
        xf = xf * jax.lax.rsqrt(jnp.mean(xf * xf, axis=-1, keepdims=True) + EPS)
        normed = norm_w * xf.astype(attn.dtype)
        gate = jax.nn.sigmoid(hidden_states @ gate_w.T)
        return gate * normed @ out_w.T

    def _L1_xattn_ref(queries, keys, values, Wq, Wk, Wv, Wo):
        import jax, jax.numpy as jnp
        import numpy as np
        EMBED = 512
        HEADS = 32
        GROUP = 4
        KV_HEADS = HEADS // GROUP
        HEAD_DIM = EMBED // HEADS
        B, S = (2, 256)
        b, s, _ = queries.shape
        q = (queries @ Wq).reshape(b, s, KV_HEADS, GROUP, HEAD_DIM)
        k = (keys @ Wk).reshape(b, s, KV_HEADS, HEAD_DIM)
        v = (values @ Wv).reshape(b, s, KV_HEADS, HEAD_DIM)
        scale = 1.0 / jnp.sqrt(jnp.asarray(HEAD_DIM, dtype=q.dtype))
        scores = jnp.einsum('bqhgd,bkhd->bhgqk', q, k) * scale
        attn = jax.nn.softmax(scores, axis=-1)
        out = jnp.einsum('bhgqk,bkhd->bqhgd', attn, v)
        out = out.reshape(b, s, EMBED)
        return out @ Wo

    def _L1_ffn_ref(x, weight_q3, weight_norm, bias):
        import jax, jax.numpy as jnp
        import numpy as np
        GROUP_SIZE = 32
        OUT_FEATURES = 512
        IN_FEATURES = 512

        def _unpack_3bit(p):
            b0, b1, b2 = (p[..., 0], p[..., 1], p[..., 2])
            v0 = b0 & 7
            v1 = b0 >> 3 & 7
            v2 = b0 >> 6 & 3 | (b1 & 1) << 2
            v3 = b1 >> 1 & 7
            v4 = b1 >> 4 & 7
            v5 = b1 >> 7 & 1 | (b2 & 3) << 1
            v6 = b2 >> 2 & 7
            v7 = b2 >> 5 & 7
            return jnp.stack([v0, v1, v2, v3, v4, v5, v6, v7], axis=-1)

        def _block_dequantize_3bit(packed, normalization, group_size=GROUP_SIZE):
            p = packed.astype(jnp.uint8).reshape(-1, group_size // 8, 3)
            q = _unpack_3bit(p).reshape(-1, group_size).astype(jnp.float32)
            n = normalization.astype(jnp.float32)
            x_norm = q / 7.0
            return (x_norm * (2.0 * n) - n).reshape(-1)
        w = _block_dequantize_3bit(weight_q3, weight_norm).reshape(OUT_FEATURES, IN_FEATURES)
        return jnp.einsum('bsi,oi->bso', x, w) + bias
    x = x + _L0_attn_ref(_layernorm(x, axis=-1), L0_attn_up_w, L0_attn_gate_w, L0_attn_local_point, L0_attn_local_approx_output, L0_attn_fuse_weight, L0_attn_discount_factor, L0_attn_ffn_gate_w, L0_attn_ffn_up_w, L0_attn_ffn_down_w)
    x = x + _L0_xattn_ref(_layernorm(x, axis=-1), ctx_4096, mask_BxSxS2_bk0, fside_Bx32xSxS2_0, L0_xattn_Wq, L0_xattn_Wk, L0_xattn_Wv, L0_xattn_Wo)
    x = x + _L0_ffn_ref(_layernorm(x, axis=-1), L0_ffn_W_org, L0_ffn_lora_down, L0_ffn_lora_up, L0_ffn_lora_keys, L0_ffn_Wq)
    x = x + _L1_attn_ref(_layernorm(x, axis=-1), L1_attn_qkv_w, L1_attn_out_w, L1_attn_gate_w, L1_attn_norm_w)
    x = x + _L1_xattn_ref(_layernorm(x, axis=-1), ctx_4096, ctx_4096, L1_xattn_Wq, L1_xattn_Wk, L1_xattn_Wv, L1_xattn_Wo)
    x = x + _L1_ffn_ref(_layernorm(x, axis=-1), L1_ffn_weight_q3, L1_ffn_weight_norm, L1_ffn_bias)
    return x

_drawn_inputs = setup_inputs


def setup_inputs(seed=0):
    import zlib

    import numpy as np

    out = dict(_drawn_inputs(seed))
    spreads = {'L1_attn_norm_w': (1.0, 0.2)}
    factors = {'fside_Bx32xSxS2_0': 8.0,
     'L0_ffn_lora_keys': 8.0,
     'L0_ffn_Wq': 8.0,
     'L1_xattn_Wq': 8.0,
     'L1_xattn_Wk': 8.0,
     'L1_ffn_bias': 26.964}
    for name, (base, spread) in spreads.items():
        noise = np.random.default_rng([zlib.crc32(name.encode()), seed]).standard_normal(out[name].shape)
        drawn = base * np.exp(spread * noise) if base else spread * noise
        out[name] = jnp.asarray(drawn.astype(out[name].dtype))
    for name, factor in factors.items():
        out[name] = (out[name] * factor).astype(out[name].dtype)
    return out
```

```python
import numpy as np
import concourse.bass as bass
from concourse import mybir
from contextlib import ExitStack

FP32 = mybir.dt.float32
F32R = mybir.dt.float32r
I32 = mybir.dt.int32
U8 = mybir.dt.uint8
ACT = mybir.ActivationFunctionType
ALU = mybir.AluOpType
AX = mybir.AxisListType

P = 128
B, S, D = 8, 128, 512
T = B * S
KC = D // P
HALF = T // 2
HB = B // 2
NSLOT, PIECE = 5, 1024
TAYLOR = 7
FG = 5
FPAD = FG * 256
HG = 16
E, R = 8, 64
KVH, GQ, HD = 8, 4, 16
VW = HD + 2
EPS = 1e-5
MASKED = 1e30

PJ_PER = dict(ln=B, taylor=4, ffn=FG * 8, l0x=HG * 16, l0f=8, l1a=HG * 20, l1xv=B, l1x=4 * 6, l1f=4)
PJ_ORDER = ["ln0", "taylor", "ffn", "ln1", "l0x", "ln2", "l0f", "ln3", "l1a", "ln4", "l1xv", "l1x", "l1f", "ln5"]
OU_PER = dict(taylor=B, ffn=FG * B, l0x=HG * B, l0f=2 * B, l1a=HG * B, l1x=B, l1f=B)
OU_ORDER = ["taylor", "ffn", "l0x", "l0f", "l1a", "l1x", "l1f"]


CONSTS_IN = ["identity", "local_point", "discount", "bias", "lora_keys", "lora_wq", "expert_rows", "norm_w",
             "one", "block_mask", "q3", "q3_norm"]


def starts(order, per):
    at, out = 0, {}
    for name in order:
        out[name] = at
        at += per["ln" if name[:2] == "ln" else name]
    return out


PJ = starts(PJ_ORDER, PJ_PER)
HI = starts(PJ_ORDER, {k: v if k in ("ln", "l0x", "l1xv", "l1x", "l1f") else 0 for k, v in PJ_PER.items()})
OU = starts(OU_ORDER, OU_PER)
SC = dict(l0x=0, l1a=HG * B, l1x=2 * HG * B)
PV = dict(l0x=0, l1a=HG * B, l1x=2 * HG * B)
TP = dict(l0x=0, l1x=HG * B)
W_T, W_F, W_X, W_L = 0, 1, 1 + FG, 1 + FG + HG
SLOT = dict(
    taylor=[0] * 5,
    ffn=[1, 1, 1],
    l0x=[1 + FG, 1 + FG, 1 + FG, 1],
    l0f=[1 + FG + HG, 1 + FG + HG, 1 + FG + HG, 1 + HG, 1],
    l0f_up=2 + FG + HG,
    l1a=[3 + FG + HG, 2 + FG + HG, 2 + FG + HG, 2 + HG, 2],
    l1x=[3 + FG + 2 * HG, 2 + FG + 2 * HG, 2 + FG + 2 * HG, 2 + 2 * HG, 2 + HG],
    l1x_o=[3 + FG + 2 * HG, 3 + 2 * HG],
)


def build(nc, a):
    ctx = ExitStack()
    with ctx:
        def sb(name, shape, dt=FP32):
            return ctx.enter_context(nc.sbuf_tensor(name, shape, dt))

        def psum(name):
            return ctx.enter_context(nc.psum_tensor(name, [P, 512], FP32))

        def sem(name):
            return ctx.enter_context(nc.semaphore(name))

        RAW = sb("raw", [P, NSLOT, PIECE])
        WH = sb("w_hi", [P, NSLOT, PIECE], F32R)
        WL = sb("w_lo", [P, NSLOT, PIECE], F32R)
        X = sb("x", [P, B, D])
        XTH = sb("xt_hi", [P, KC, T], F32R)
        XTL = sb("xt_lo", [P, KC, T], F32R)
        with ExitStack() as shared:
            Y = shared.enter_context(nc.sbuf_tensor("y", [P, B, D], FP32))
            SQ = shared.enter_context(nc.sbuf_tensor("sumsq", [P, B, 256], FP32))
            G = shared.enter_context(nc.sbuf_tensor("gate", [P, 2, 512], FP32))
            F = shared.enter_context(nc.sbuf_tensor("silu", [P, 2, 512], FP32))
        CH = sb("ctx_hi", [P, KC, T], F32R)
        CL = sb("ctx_lo", [P, KC, T], F32R)
        NA = 3840
        AH = sb("act_hi", [P, NA], F32R)
        AL = sb("act_lo", [P, NA], F32R)
        with ExitStack() as shared:
            FS = shared.enter_context(nc.sbuf_tensor("side", [P, 2, HB, 2, S], FP32))
        KXH = sb("keys_hi", [P, 2, 512], F32R)
        KXL = sb("keys_lo", [P, 2, 512], F32R)
        M = sb("mask_bias", [P, B, S])
        PR = sb("probs", [P, 2, 512])
        DT = sb("decay", [P, 256])
        IDN = sb("identity", [P, P])
        MI = sb("mask_int", [P, B, S // 4], I32)
        BIAS = sb("bias", [P, D])
        Q3 = sb("q3_packed", [P, 4, 16 * 3], I32)
        QN = sb("q3_norm", [P, 4, 16])
        QI = sb("q3_int", [P, 4, 64, 3], I32)
        QT = sb("q3_tmp", [P, 4, 64], I32)
        QU = sb("q3_tmp2", [P, 4, 64], I32)
        QN2 = sb("q3_norm2", [P, 64])
        ST = sb("bn_stats", [P, B, 6])
        MV = sb("bn_mean_var", [P, B, 2])
        VE = sb("var_eps", [P, B])
        SD = sb("std", [P, B])
        RS = sb("rstd", [P, B])
        LP = sb("local_point", [P, 1])
        DC = sb("discount", [P, 6])
        CE = sb("coef_exp", [P, 6])
        MX = sb("row_max", [P, 2, 4])
        NM = sb("neg_max", [P, 2, 4])
        SU = sb("row_sum", [P, 2, 2])
        SM = sb("row_sum_min", [P, 2])
        RC = sb("row_recip", [P, 8])
        KEYS = sb("lora_keys", [P, E])
        LQ = sb("lora_wq", [P, KC, P])
        SEL = sb("expert_rows", [E, KC, P])
        XM = sb("x_sum", [P, KC, B])
        XM2 = sb("x_sum_lo", [P, KC, B])
        XM3 = sb("x_sum_all", [P, KC, B])
        LQT = sb("lora_q", [P, B])
        LS = sb("lora_exp", [B, E])
        LSM = sb("lora_stats", [B, 4])
        LCO = sb("lora_coef", [B, E])
        LCT = sb("lora_coef_t", [E, B])
        LCR = sb("lora_coef_rows", [P, KC, B])
        NW = sb("norm_w", [P, 2 * HG])
        ONE = sb("one", [P, 1])
        BM = sb("block_mask", [P, GQ])
        SS = sb("mean_sq", [P, B])
        SSD = sb("mean_sq_std", [P, B])
        YR = sb("y_scale", [P, B])

        pj = [psum("pj0"), psum("pj1")]
        sc = [psum("sc0"), psum("sc1")]
        tp = psum("tp")
        pv = psum("pv")
        ou = [psum("ou0"), psum("ou1")]

        consts_in, x_in, fs_in, mask_in, out_done = sem("consts_in"), sem("x_in"), [sem("fs_in0"), sem("fs_in1")], sem("mask_in"), sem("out_done")
        dt_in = sem("dt_in")
        w_in = [sem(f"w_in{s}") for s in range(NSLOT)]
        w_scaled = sem("w_scaled")
        w_hi = [sem(f"w_hi{s}") for s in range(NSLOT)]
        w_ready = [sem(f"w_ready{s}") for s in range(NSLOT)]
        pool_gate, dve_gate = sem("pool_gate"), sem("dve_gate")
        c_in, c_hi, c_ready = [sem("c_in0"), sem("c_in1")], sem("c_hi"), sem("c_ready")
        passed = sem("passed")
        ln_stat, ln_aggr, ln_var, ln_std, ln_rstd, ln_x = (sem(n) for n in
            ("ln_stat", "ln_aggr", "ln_var", "ln_std", "ln_rstd", "ln_x"))
        pj_full, pj_hi, pj_done = sem("pj_full"), sem("pj_hi"), sem("pj_done")
        ou_full, x_done = sem("ou_full"), sem("x_done")
        sc_full, sc_done = sem("sc_full"), sem("sc_done")
        tp_full, pt_hi, tp_done = sem("tp_full"), sem("pt_hi"), sem("tp_done")
        pv_full, ct_hi, pv_done = sem("pv_full"), sem("ct_hi"), sem("pv_done")
        ce_ready, ta_u, ta_d, ta_k, ta_t, ta_hi, ta_lo = (sem(n) for n in
            ("ce_ready", "ta_u", "ta_d", "ta_k", "ta_t", "ta_hi", "ta_lo"))
        ff_sg, ff_g, ff_h, ff_hi, ff_lo = (sem(n) for n in ("ff_sg", "ff_g", "ff_h", "ff_hi", "ff_lo"))
        m_ready, fm_ready = sem("m_ready"), [sem("fm_ready0"), sem("fm_ready1")]
        sx_nm, sx_exp, sx_sm, sx_rc, sx_pn = (sem(n) for n in ("sx_nm", "sx_exp", "sx_sm", "sx_rc", "sx_pn"))
        lf_sum, lf_pe, lf_v, lf_a, lf_f, lf_hi, lf_lo = (sem(n) for n in
            ("lf_sum", "lf_pe", "lf_v", "lf_a", "lf_f", "lf_hi", "lf_lo"))
        y_zero, la_sg, la_f, la_hi, la_lo, la_sd, la_sdhi, la_sdlo, la_sq, la_sqa, la_gf, la_gfhi, la_gflo = (
            sem(n) for n in ("y_zero", "la_sg", "la_f", "la_hi", "la_lo", "la_sd", "la_sdhi", "la_sdlo", "la_sq",
                             "la_sqa", "la_gf", "la_gfhi", "la_gflo"))
        la_ss, la_v, la_a, la_y = sem("la_ss"), sem("la_v"), sem("la_a"), sem("la_y")
        v_ones, kr_full, kr_hi, kr_lo, kx_ready, lx_max, lx_nm, lx_exp, lx_rc, lx_on = (sem(n) for n in
            ("v_ones", "kr_full", "kr_hi", "kr_lo", "kx_ready", "lx_max", "lx_nm", "lx_exp", "lx_rc", "lx_on"))
        dq, w_deq, bias_added = sem("dq"), sem("w_deq"), sem("bias_added")

        def f32(ap):
            return ap.bitcast(FP32)

        def wslot(t, s, cols):
            return t[:, s, :].rearrange("p (c n) -> p c n", n=cols)

        def wpair(t, s, cols):
            return t[:, s:s + 2, :].rearrange("p s (c n) -> p (s c) n", n=cols)

        def qk(t, which, h):
            return t[:, (2 * which + h) * 512:(2 * which + h + 1) * 512]

        def vt(t, j):
            return t[:, 2048 + j * 256:2048 + (j + 1) * 256]

        def tile_a(t, n=0):
            return t[:, 3072 + n * 256:3328 + n * 256]

        def tile_b(t):
            return t[:, 3584:3840]

        def grp(t, m):
            return t[:, m * 512:(m + 1) * 512]

        def q1(t, c):
            return t[:, c * 256:(c + 1) * 256]

        V1 = 1024
        PT1 = V1 + B * KVH * VW
        ON1 = PT1 + 1024
        ONT = M[:, :, :].rearrange("p (r c) s -> p r (c s)", r=2)

        FSF = FS[:, :, :, :, :].rearrange("p a b h s -> p (a b h s)")
        TY = [FSF[:, n * 512:(n + 1) * 512] for n in range(4)]
        MF = M[:, :, :].rearrange("p b s -> p (b s)")
        GT = [FSF[:, 0:256], FSF[:, 256:512]]
        SG, HF = MF[:, 0:512], MF[:, 512:1024]

        def nth(base, i, per, j):
            return i * per + (base + j), (base + j) % 2

        block = ctx.enter_context(nc.Block())
        CONSTS = [IDN[:], LP[:], DC[:], BIAS[:], KEYS[:], LQ[:], SEL[:], NW[:], ONE[:], BM[:], Q3[:], QN[:]]

        @block.sync
        def _(sp):
            def load(s, k, src):
                if not isinstance(k, int) or k > 0:
                    sp.wait_ge(w_ready[s], k)
                sp.dma_start(RAW[:, s, :], src).then_inc(w_in[s], 16)

            def load_ctx(n, c):
                if n or c >= 2:
                    sp.wait_ge(c_ready, KC * n + max(c - 1, 0))
                sp.dma_start(FSF[:, (c % 2) * T:(c % 2 + 1) * T], a["ctx_t"][c]).then_inc(c_in[c % 2], 16)

            for n in range(2):
                sp.dma_start(X[:, n * HB:(n + 1) * HB, :],
                             a["x"][n * HB:(n + 1) * HB].rearrange("b p d -> p b d")).then_inc(x_in, 16)
            for dst, name in zip(CONSTS, CONSTS_IN):
                sp.dma_start(dst, a[name]).then_inc(consts_in, 16)
            for s in range(NSLOT):
                load(s, 0, a["taylor_w"][s])
            sp.dma_start(MI[:], a["mask"]).then_inc(mask_in, 16)
            for s in range(3):
                load(s, SLOT["ffn"][s], a["ffn_w"][0, s])
            sp.wait_ge(ta_lo, 2 * TAYLOR)
            load_ctx(0, 0)
            load_ctx(0, 1)
            with sp.Fori(1, FG) as i:
                for s in range(3):
                    load(s, i + SLOT["ffn"][s], a["ffn_w"][bass.ds(i, 1), s].rearrange("a p n -> (a p) n"))
            load_ctx(0, 2)
            load_ctx(0, 3)
            sp.wait_ge(c_ready, KC)
            with sp.Fori(0, HG) as i:
                for s in range(4):
                    load(s, i + SLOT["l0x"][s], a["l0x_w"][bass.ds(i, 1), s].rearrange("a p n -> (a p) n"))
                for hf in range(2):
                    sp.wait_ge(sx_nm, i * B + (hf + 1) * HB)
                    sp.dma_start(FS[:, hf].rearrange("p b h s -> p (b h s)"),
                                 a["side"][bass.ds(i, 1), hf].rearrange("a p n -> (a p) n")).then_inc(fs_in[hf], 16)
            for s in range(NSLOT):
                load(s, SLOT["l0f"][s], a["l0f_w"][s])
            load(0, SLOT["l0f_up"], a["l0f_w"][NSLOT])
            with sp.Fori(0, HG) as i:
                for s in range(NSLOT):
                    load(s, i + SLOT["l1a"][s], a["l1a_w"][bass.ds(i, 1), s].rearrange("a p n -> (a p) n"))
                sp.wait_ge(sc_done, i * B + 2 + SC["l1a"])
                sp.dma_start(DT[:], a["decay"][bass.ds(i, 1)].rearrange("a p n -> (a p) n")).then_inc(dt_in, 16)
            for s in range(NSLOT):
                load(s, SLOT["l1x"][s], a["l1x_w"][s])
            sp.wait_ge(la_gflo, HG * B)
            for c in range(KC):
                load_ctx(1, c)
            for s in range(2):
                load(2 + s, SLOT["l1x_o"][s], a["l1x_w"][NSLOT + s])
            for b in range(B):
                sp.wait_ge(x_done, OU["l1f"] + b + 1)
                sp.dma_start(a["out"][b], X[:, b, :]).then_inc(out_done, 16)
            sp.wait_ge(out_done, 16 * B)

        @block.gpsimd
        def _(pool):
            def hold(*waits):
                for s, v in waits:
                    pool.wait_ge(s, v)
                pool.sem_inc(passed, 1)

            def split(s, k, free=None, scale=None):
                pool.wait_ge(w_in[s], k * 16 + 16)
                if scale is not None:
                    scale()
                hold(*([free] if free else []))
                pool.tensor_tensor(WH[:, s, :], RAW[:, s, :], ONE[:].broadcast_to((P, PIECE)), ALU.mult).then_inc(w_hi[s], 1)
                pool.wait_ge(w_hi[s], k + 1)
                pool.tensor_tensor(WL[:, s, :], RAW[:, s, :], f32(WH[:, s, :]), ALU.subtract).then_inc(w_ready[s], 1)

            def split_ctx(n):
                for c in range(KC):
                    src = FSF[:, (c % 2) * T:(c % 2 + 1) * T]
                    pool.wait_ge(c_in[c % 2], 16 * (2 * n + c // 2 + 1))
                    pool.tensor_tensor(CH[:, c, :], src, ONE[:].broadcast_to((P, T)), ALU.mult).then_inc(c_hi, 1)
                    pool.wait_ge(c_hi, KC * n + c + 1)
                    pool.tensor_tensor(CL[:, c, :], src, f32(CH[:, c, :]), ALU.subtract).then_inc(c_ready, 1)

            def scale_powers(s):
                for j in range(2):
                    m = 2 * (s - 1) + j
                    if 1 <= m < TAYLOR:
                        blk = RAW[:, s, j * 512:(j + 1) * 512]
                        pool.tensor_scalar(blk, blk, CE[:, m - 1:m], None, ALU.mult).then_inc(w_scaled, 1)
                pool.wait_ge(w_scaled, min(2 * s, TAYLOR) - 1)

            pool.wait_ge(consts_in, 16 * len(CONSTS))
            split(0, 0)
            pool.wait_ge(ce_ready, 1)
            for s in range(1, NSLOT):
                split(s, 0, scale=lambda s=s: scale_powers(s))
            for s in range(3):
                split(s, SLOT["ffn"][s], (ou_full, OU["taylor"] + B) if s else (pj_full, PJ["taylor"] + 4))
            with pool.Fori(1, FG) as i:
                split(0, i + SLOT["ffn"][0], (pj_full, i * 8 + (PJ["ffn"] - 1)))
                split(1, i + SLOT["ffn"][1], (pj_full, i * 8 + PJ["ffn"]))
                split(2, i + SLOT["ffn"][2], (ou_full, i * B + OU["ffn"]))
            split_ctx(0)
            pool.wait_ge(m_ready, 1)
            with pool.Fori(0, HG) as i:
                for s, ahead in enumerate((6, 4, 0)):
                    split(s, i + SLOT["l0x"][s], (pj_full, i * 16 + (PJ["l0x"] - ahead)))
                for hf in range(2):
                    pool.wait_ge(fs_in[hf], i * 16 + 16)
                    for h in range(2):
                        pool.tensor_tensor(FS[:, hf, :, h, :], FS[:, hf, :, h, :], M[:, hf * HB:(hf + 1) * HB, :],
                                           ALU.add).then_inc(fm_ready[hf], 1)
                split(3, i + SLOT["l0x"][3], (ou_full, i * B + OU["l0x"]))
            split(0, SLOT["l0f"][0], (pj_full, PJ["l0x"] + HG * 16 - 6))
            split(1, SLOT["l0f"][1], (pj_full, PJ["l0x"] + HG * 16 - 4))
            split(2, SLOT["l0f"][2], (pj_full, PJ["l0x"] + HG * 16))
            split(3, SLOT["l0f"][3], (ou_full, OU["l0x"] + HG * B))
            split(4, SLOT["l0f"][4], (ou_full, OU["taylor"] + B))
            split(0, SLOT["l0f_up"], (ou_full, OU["l0f"] + B))
            pool.memset(Y[:], 0.0).then_inc(y_zero, 1)
            pool.memset(SQ[:], 0.0).then_inc(y_zero, 1)
            pool.wait_ge(ou_full, OU["l0f"] + 2 * B)
            with pool.Fori(0, HG) as i:
                for s, ahead in enumerate((8, 6, 0, 4)):
                    split(s, i + SLOT["l1a"][s], (pj_full, i * 20 + (PJ["l1a"] - ahead)))
                split(4, i + SLOT["l1a"][4], (ou_full, i * B + OU["l1a"]))
            for s, ahead in enumerate((8, 6, 0, 4)):
                split(s, SLOT["l1x"][s], (pj_full, PJ["l1a"] + HG * 20 - ahead))
            split(4, SLOT["l1x"][4], (ou_full, OU["l1a"] + HG * B))
            pool.wait_ge(la_y, B)
            split_ctx(1)
            for s in range(2):
                split(2 + s, SLOT["l1x_o"][s], (kr_full, 2))
            pool.wait_ge(kr_lo, 2)
            with pool.Fori(0, 4) as i:
                for bb in range(2):
                    for c in range(KC):
                        n = bb * KC + c
                        hold((sc_full, i * 16 + (SC["l1x"] + 2 * n - 2)))
                        for t, kx in ((CH, KXH), (CL, KXL)):
                            keys = f32(t[:, c, bass.ds(i * 256 + bb * S, S)])
                            pool.tensor_tensor(kx[:, n % 2, :].rearrange("p (j s) -> p j s", j=GQ),
                                               keys.unsqueeze(1).broadcast_to((P, GQ, S)),
                                               BM[:].unsqueeze(2).broadcast_to((P, GQ, S)),
                                               ALU.mult).then_inc(kx_ready, 1)

        @block.tensor
        def _(pe):
            def mm3(out, w, x, first=True, last=True):
                (wh, wl), (xh, xl) = w, x
                pe.matmul(out, wh, xh, start=first, stop=False)
                pe.matmul(out, wh, xl, start=False, stop=False)
                return pe.matmul(out, wl, xh, start=False, stop=last)

            def pj_free(n):
                if not isinstance(n, int) or n >= 2:
                    pe.wait_ge(pj_done, n - 1)

            def ou_free(n):
                if not isinstance(n, int) or n >= 2:
                    pe.wait_ge(x_done, n - 1)

            def layer_norm(l):
                for b in range(B):
                    n = PJ[f"ln{l}"] + b
                    pe.wait_ge(ln_x, B * l + b + 1)
                    pj_free(n)
                    for c in range(KC):
                        last = pe.transpose(pj[n % 2][:, c * P:(c + 1) * P], PR[:, b % 2, c * P:(c + 1) * P], IDN[:])
                    last.then_inc(pj_full, 1)
                pe.wait_ge(pj_done, PJ[f"ln{l}"] + B)

            def project(fill, w, x, width=512):
                n, bank = fill
                pj_free(n)
                for c in range(KC):
                    last = mm3(pj[bank][:, 0:width], w(c), x(c), c == 0, c == KC - 1)
                last.then_inc(pj_full, 1)

            def both(ts, f):
                return tuple(f(t) for t in ts)

            XT, C, W, A = (XTH, XTL), (CH, CL), (WH, WL), (AH, AL)

            def wide(x, hf):
                return lambda c: both(x, lambda t: t[:, c, hf * HALF:(hf + 1) * HALF])

            def rows(x, b):
                return lambda c: both(x, lambda t: t[:, c, b * S:(b + 1) * S])

            def wcols(s, j, cols=256, width=P):
                return lambda c: both(W, lambda t: wslot(t, s, cols)[:, c, j * width:(j + 1) * width])

            def wrows(s):
                return lambda c: both(W, lambda t: wpair(t, s, 512)[:, c, :])

            def ready(s, k):
                pe.wait_ge(w_ready[s], k + 1)

            pe.wait_ge(consts_in, 16 * len(CONSTS))
            layer_norm(0)
            ready(0, 0)
            for hf in range(2):
                for j in range(2):
                    project(nth(PJ["taylor"], 0, 0, 2 * hf + j), wcols(0, j), wide(XT, hf))
            for s in range(1, NSLOT):
                ready(s, 0)
            for hf in range(2):
                pe.wait_ge(ta_lo, (hf + 1) * TAYLOR)
                for b in range(HB):
                    n, bank = nth(OU["taylor"], 0, 0, hf * HB + b)
                    ou_free(n)
                    for m in range(TAYLOR):
                        w = both(W, lambda t: t[:, 1 + m // 2, (m % 2) * 512:(m % 2 + 1) * 512])
                        x = both(A, lambda t: grp(t, m)[:, b * S:(b + 1) * S])
                        last = mm3(ou[bank][:], x, w, m == 0, m == TAYLOR - 1)
                    last.then_inc(ou_full, 1)

            def ffn_group(i):
                for hf in range(2):
                    for j in range(2):
                        for s in range(2):
                            if hf == 0 and j == 0:
                                ready(s, i + SLOT["ffn"][s])
                            project(nth(PJ["ffn"], i, 8, hf * 4 + 2 * j + s), wcols(s, j), wide(XT, hf))
                    if hf == 0:
                        ready(2, i + SLOT["ffn"][2])
                    pe.wait_ge(ff_lo, i * 4 + (2 * hf + 3))
                    for b in range(HB):
                        n, bank = nth(OU["ffn"], i, B, hf * HB + b)
                        ou_free(n)
                        for j in range(2):
                            last = mm3(ou[bank][:], both(A, lambda t: grp(t, j)[:, b * S:(b + 1) * S]),
                                       wcols(2, 0, 512, 512)(j), j == 0, j == 1)
                        last.then_inc(ou_full, 1)

            with pe.Fori(0, FG) as i:
                ffn_group(i)

            layer_norm(1)
            pe.wait_ge(c_ready, KC)
            with pe.Fori(0, HG) as i:
                for hf in range(2):
                    base = hf * 8
                    for s, x in ((0, XT), (1, C)):
                        if hf == 0:
                            ready(s, i + SLOT["l0x"][s])
                        for h in range(2):
                            project(nth(PJ["l0x"], i, 16, base + 2 * s + h), wcols(s, h), wide(x, hf))
                    if hf == 0:
                        ready(2, i + SLOT["l0x"][2])
                    for j in range(HB):
                        project(nth(PJ["l0x"], i, 16, base + 4 + j), rows(C, hf * HB + j), wcols(2, 0, 256, 256), 256)

                    def scores(j):
                        n, bank = nth(0, i, B, hf * HB + j)
                        pe.wait_ge(sc_done, n + 1)
                        for h in range(2):
                            last = mm3(sc[bank][:, h * S:(h + 1) * S],
                                       both(A, lambda t: qk(t, 0, h)[:, j * S:(j + 1) * S]),
                                       both(A, lambda t: qk(t, 1, h)[:, j * S:(j + 1) * S]))
                        last.then_inc(sc_full, 1)

                    def transposes(j):
                        n, bank = nth(0, i, B, hf * HB + j)
                        pe.wait_ge(sx_pn, n + 1)
                        pe.wait_ge(tp_done, n + 1)
                        for h in range(2):
                            last = pe.transpose(tp[:, h * S:(h + 1) * S], PR[:, bank, h * S:(h + 1) * S], IDN[:])
                        last.then_inc(tp_full, 1)

                    def values(j):
                        n, _ = nth(0, i, B, hf * HB + j)
                        pe.wait_ge(tp_done, n + 2)
                        pe.wait_ge(pv_done, n + 1)
                        for h in range(2):
                            last = mm3(pv[:, h * S:(h + 1) * S],
                                       both(A, lambda t: vt(t, j)[:, h * S:(h + 1) * S]),
                                       both(A, lambda t: tile_a(t)[:, h * S:(h + 1) * S]))
                        last.then_inc(pv_full, 1)

                    def output(j):
                        n, _ = nth(0, i, B, hf * HB + j)
                        m, bank = nth(OU["l0x"], i, B, hf * HB + j)
                        if hf == 0 and j == 0:
                            ready(3, i + SLOT["l0x"][3])
                        pe.wait_ge(pv_done, n + 2)
                        ou_free(m)
                        for h in range(2):
                            last = mm3(ou[bank][:], both(A, lambda t: tile_b(t)[:, h * S:(h + 1) * S]),
                                       wcols(3, 0, 512, 512)(h), h == 0, h == 1)
                        last.then_inc(ou_full, 1)

                    pe.wait_ge(pj_done, i * 16 + (PJ["l0x"] + base + 4))
                    scores(0)
                    for j in range(HB):
                        if j + 1 < HB:
                            scores(j + 1)
                        transposes(j)
                        if j == 0:
                            pe.wait_ge(pj_done, i * 16 + (PJ["l0x"] + base + 8))
                        else:
                            output(j - 1)
                        values(j)
                    output(HB - 1)

            layer_norm(2)
            for s in range(2):
                ready(s, SLOT["l0f"][s])
            for b in range(B):
                n, bank = nth(OU["l0f"], 0, 0, b)
                ou_free(n)
                for c in range(KC):
                    last = mm3(ou[bank][:], rows(XT, b)(c), wrows(0)(c), c == 0, c == KC - 1)
                last.then_inc(ou_full, 1)
            pe.wait_ge(lf_sum, 3)
            for c in range(KC):
                last = pe.matmul(sc[0][:, 0:B], LQ[:, c, :], XM3[:, c, :], start=c == 0, stop=c == KC - 1)
            last.then_inc(lf_pe, 1)
            pe.wait_ge(lf_v, 1)
            pe.matmul(sc[1][0:B, 0:E], LQT[:], KEYS[:], start=True, stop=True).then_inc(lf_pe, 1)
            pe.wait_ge(lf_v, 5)
            pe.transpose(sc[0][0:E, 0:B], LCO[:], IDN[0:B, 0:B]).then_inc(lf_pe, 1)
            pe.wait_ge(lf_v, 6)
            for c in range(KC):
                last = pe.matmul(sc[1][:, c * B:(c + 1) * B], SEL[:, c, :], LCT[:], start=True, stop=True)
            last.then_inc(lf_pe, 1)
            for s in (2, 3, 4):
                ready(s, SLOT["l0f"][s])
            for hf in range(2):
                for e in range(KC):
                    w = lambda c: both(W, lambda t: wpair(t, 2, 512)[:, c, e * P:(e + 1) * P])
                    project(nth(PJ["l0f"], 0, 0, hf * 4 + e), w, wide(XT, hf))
                pe.wait_ge(lf_lo, 4 * hf + 4)
                if hf == 0:
                    ready(0, SLOT["l0f_up"])
                for b in range(HB):
                    n, bank = nth(OU["l0f"], 0, 0, B + hf * HB + b)
                    ou_free(n)
                    for e in range(KC):
                        s = 4 if e < 2 else 0
                        last = mm3(ou[bank][:], both(A, lambda t: grp(t, e)[:, b * S:(b + 1) * S]),
                                   wcols(s, 0, 512, 512)(e % 2), e == 0, e == KC - 1)
                    last.then_inc(ou_full, 1)

            layer_norm(3)
            with pe.Fori(0, HG) as i:
                for hf in range(2):
                    base = hf * 10
                    for f, s in enumerate((0, 1, 3)):
                        if hf == 0:
                            ready(s, i + SLOT["l1a"][s])
                        for h in range(2):
                            project(nth(PJ["l1a"], i, 20, base + 2 * f + h), wcols(s, h), wide(XT, hf))
                    if hf == 0:
                        ready(2, i + SLOT["l1a"][2])
                    for j in range(HB):
                        project(nth(PJ["l1a"], i, 20, base + 6 + j), rows(XT, hf * HB + j), wcols(2, 0, 256, 256), 256)

                    def scores(j):
                        n, bank = nth(SC["l1a"], i, B, hf * HB + j)
                        pe.wait_ge(sc_done, n + 1)
                        for h in range(2):
                            last = mm3(sc[bank][:, h * S:(h + 1) * S],
                                       both(A, lambda t: qk(t, 1, h)[:, j * S:(j + 1) * S]),
                                       both(A, lambda t: qk(t, 0, h)[:, j * S:(j + 1) * S]))
                        last.then_inc(sc_full, 1)

                    def values(j):
                        n, _ = nth(PV["l1a"], i, B, hf * HB + j)
                        pe.wait_ge(la_sdlo, i * B + (hf * HB + j + 1))
                        pe.wait_ge(pv_done, n + 1)
                        for h in range(2):
                            last = mm3(pv[:, h * S:(h + 1) * S],
                                       both(A, lambda t: vt(t, j)[:, h * S:(h + 1) * S]),
                                       both(A, lambda t: tile_a(t, j % 2)[:, h * S:(h + 1) * S]))
                        last.then_inc(pv_full, 1)

                    def output(j):
                        m, bank = nth(OU["l1a"], i, B, hf * HB + j)
                        if hf == 0 and j == 0:
                            ready(4, i + SLOT["l1a"][4])
                        pe.wait_ge(la_gflo, i * B + (hf * HB + j + 1))
                        ou_free(m)
                        for h in range(2):
                            last = mm3(ou[bank][:], both(A, lambda t: tile_b(t)[:, h * S:(h + 1) * S]),
                                       wcols(4, 0, 512, 512)(h), h == 0, h == 1)
                        last.then_inc(ou_full, 1)

                    pe.wait_ge(la_lo, i * 16 + (hf * 8 + 6))
                    scores(0)
                    for j in range(HB):
                        if j + 1 < HB:
                            scores(j + 1)
                        if j == 0:
                            pe.wait_ge(la_lo, i * 16 + (hf * 8 + 10))
                        values(j)
                        if j:
                            output(j - 1)
                    output(HB - 1)
            pe.wait_ge(la_sqa, HG * B)
            for b in range(B):
                for h in range(2):
                    last = pe.matmul(tp[:, b:b + 1], SQ[:, b, h * S:(h + 1) * S], ONE[:], start=h == 0, stop=h == 1)
            last.then_inc(la_ss, 1)

            layer_norm(4)
            ready(4, SLOT["l1x"][4])
            pe.wait_ge(c_ready, 2 * KC)
            for b in range(B):
                project(nth(PJ["l1xv"], 0, 0, b), rows(C, b), lambda c: both(W, lambda t: wslot(t, 4, 256)[:, c, 0:P]), P)
            for s in (2, 3):
                ready(s, SLOT["l1x"][s])
            pe.wait_ge(sc_done, 2 + SC["l1x"])
            pe.wait_ge(x_done, OU["l1x"])
            for hf in range(2):
                if hf:
                    pe.wait_ge(kr_lo, 1)
                for m, bank in enumerate((sc[0], sc[1], ou[0], ou[1])):
                    for c in range(KC):
                        w = both(W, lambda t: wpair(t, 2, 512)[:, c, m * P:(m + 1) * P])
                        last = mm3(bank[:], w, wide(C, hf)(c), c == 0, c == KC - 1)
                last.then_inc(kr_full, 1)
            for s in (0, 1):
                ready(s, SLOT["l1x"][s])
            with pe.Fori(0, 4) as i:
                for c4 in range(KC):
                    w = lambda c: both(W, lambda t: wpair(t, 0, 512)[:, c, c4 * P:(c4 + 1) * P])
                    x = lambda c: both(XT, lambda t: t[:, c, bass.ds(i * 256, 256)])
                    project(nth(PJ["l1x"], i, 6, c4), w, x, 256)
                pe.wait_ge(pj_done, i * 6 + (PJ["l1x"] + 4))

                def scores(m):
                    bb, c, u = m // 8, m // 2 % 4, m % 2
                    n, bank = nth(SC["l1x"], i, 16, m)
                    if u == 0:
                        pe.wait_ge(kx_ready, i * 16 + (2 * (m // 2) + 2))
                    pe.wait_ge(lx_exp, i * 16 + (m + 1))
                    r = slice(64 * u, 64 * u + 64)
                    mm3(sc[bank][:], both(A, lambda t: q1(t, c)[r, bb * S:(bb + 1) * S]),
                        both((KXH, KXL), lambda t: t[r, (m // 2) % 2, :])).then_inc(sc_full, 1)

                def transposes(m):
                    n, bank = nth(TP["l1x"], i, 16, m)
                    pe.wait_ge(lx_exp, i * 16 + (m + 3))
                    pe.wait_ge(tp_done, n + 1)
                    for h in range(GQ):
                        last = pe.transpose(tp[:, h * S:(h + 1) * S], PR[:, bank, h * S:(h + 1) * S], IDN[:])
                    last.then_inc(tp_full, 1)

                def values(m):
                    bb, c, u = m // 8, m // 2 % 4, m % 2
                    n, bank = nth(TP["l1x"], i, 16, m)
                    pe.wait_ge(tp_done, n + 2)
                    if u == 0:
                        pe.wait_ge(pv_done, i * 8 + (PV["l1x"] + m // 2 + 1))
                    at = V1 + (2 * c + u) * VW
                    for h in range(GQ):
                        col = (GQ * u + h) * VW
                        last = mm3(pv[:, col:col + VW],
                                   both(A, lambda t: t[:, PT1 + bank * 512 + h * S:PT1 + bank * 512 + (h + 1) * S]),
                                   both(A, lambda t: t[:, bass.ds(i * (2 * KVH * VW) + (at + bb * KVH * VW), VW)]))
                    last.then_inc(pv_full, 1)

                def turn(bb):
                    n, bank = nth(PJ["l1x"], i, 6, 4 + bb)
                    pe.wait_ge(pv_done, i * 8 + (PV["l1x"] + 4 * bb + 5))
                    pj_free(n)
                    for c in range(KC):
                        last = pe.transpose(pj[bank][:, c * P:(c + 1) * P], ONT[:, bb, c * P:(c + 1) * P], IDN[:])
                    last.then_inc(pj_full, 1)

                def output(bb):
                    n, bank = nth(OU["l1x"], i, 2, bb)
                    pe.wait_ge(pj_done, i * 6 + (PJ["l1x"] + 5 + bb))
                    ou_free(n)
                    for c in range(KC):
                        last = mm3(ou[bank][:], both(A, lambda t: t[:, ON1 + c * P:ON1 + (c + 1) * P]),
                                   wrows(2)(c), c == 0, c == KC - 1)
                    last.then_inc(ou_full, 1)

                scores(0)
                for m in range(16):
                    if m < 15:
                        scores(m + 1)
                    transposes(m)
                    if m:
                        values(m - 1)
                    if m == 10:
                        turn(0)
                    if m == 12:
                        pe.wait_ge(w_ready[3], SLOT["l1x_o"][1] + 1)
                        output(0)
                values(15)
                turn(1)
                output(1)

            pe.wait_ge(w_deq, 1)
            for c in range(KC):
                n, bank = nth(PJ["l1f"], 0, 0, c)
                pj_free(n)
                for o in range(KC):
                    last = pe.transpose(pj[bank][:, o * P:(o + 1) * P], RAW[:, 0:2, :].rearrange("p s (o i) -> p (s o) i", i=512)[:, o, c * P:(c + 1) * P], IDN[:])
                last.then_inc(pj_full, 1)
            layer_norm(5)
            for b in range(B):
                n, bank = nth(OU["l1f"], 0, 0, b)
                ou_free(n)
                for c in range(KC):
                    last = mm3(ou[bank][:], rows(XT, b)(c), wrows(0)(c), c == 0, c == KC - 1)
                last.then_inc(ou_full, 1)

        @block.scalar
        def _(act):
            def hi(fill, dst, src, scale=1.0):
                act.wait_ge(pj_full, fill[0] + 1)
                act.activation(dst, src, ACT.Copy, scale=scale).then_inc(pj_hi, 1)

            def layer_norm(l):
                act.wait_ge(ln_var, l + 1)
                act.activation(SD[:], VE[:], ACT.Sqrt).then_inc(ln_std, 1)
                for b in range(B):
                    n, bank = nth(PJ[f"ln{l}"], 0, 0, b)
                    hi((n, bank), XTH[:, :, b * S:(b + 1) * S], pj[bank][:].rearrange("p (c s) -> p c s", c=KC))

            act.sem_inc(lx_exp, 2)
            act.wait_ge(consts_in, 16 * len(CONSTS))
            act.activation(CE[:], DC[:], ACT.Exp, scale=-1.0).then_inc(ce_ready, 1)
            layer_norm(0)
            for hf in range(2):
                if hf:
                    act.wait_ge(ou_full, OU["taylor"] + HB)
                for m in range(TAYLOR):
                    act.wait_ge(ta_t, hf * TAYLOR + m + 1)
                    act.activation(grp(AH, m), TY[3 * (m % 2)], ACT.Copy).then_inc(ta_hi, 1)

            with act.Fori(0, FG) as i:
                for hf in range(2):
                    for j in range(2):
                        n, bank = nth(PJ["ffn"], i, 8, hf * 4 + 2 * j)
                        act.wait_ge(pj_full, n + 1)
                        act.activation(SG, pj[bank][:], ACT.Sigmoid).then_inc(ff_sg, 1)
                        if j == 0:
                            act.wait_ge(ou_full, i * B + (OU["ffn"] + hf * HB))
                        act.wait_ge(pj_done, n + 2)
                        act.activation(grp(AH, j), HF, ACT.Copy).then_inc(ff_hi, 1)

            layer_norm(1)
            with act.Fori(0, HG) as i:
                for hf in range(2):
                    for f in range(8):
                        fill = nth(PJ["l0x"], i, 16, hf * 8 + f)
                        bank = pj[fill[1]]
                        if f < 4:
                            hi(fill, qk(AH, f // 2, f % 2), bank[:], S ** -0.5 if f < 2 else 1.0)
                        else:
                            hi(fill, vt(AH, f - 4), bank[:, 0:256])

                    def exps(j):
                        n, bank = nth(0, i, B, hf * HB + j)
                        act.wait_ge(sx_nm, n + 9)
                        for h in range(2):
                            t = PR[:, bank, h * S:(h + 1) * S]
                            last = act.activation(t, t, ACT.Exp, bias=NM[:, bank, h:h + 1],
                                                  accum_out=SU[:, bank, h:h + 1])
                        last.then_inc(sx_exp, 1)

                    exps(0)
                    for j in range(HB):
                        n, bank = nth(0, i, B, hf * HB + j)
                        act.wait_ge(tp_full, n + 1)
                        act.activation(tile_a(AH), tp[:, 0:256], ACT.Copy).then_inc(pt_hi, 1)
                        if j + 1 < HB:
                            exps(j + 1)
                        act.wait_ge(pv_full, n + 1)
                        act.wait_ge(ou_full, n + OU["l0x"])
                        act.activation(tile_b(AH), pv[:, 0:256], ACT.Copy).then_inc(ct_hi, 1)

            layer_norm(2)
            act.wait_ge(lf_v, 3)
            act.activation(LS[:], sc[1][0:B, 0:E], ACT.Exp, bias=LSM[:, 1:2], scale=P ** -0.5,
                           accum_out=LSM[:, 2:3]).then_inc(lf_a, 1)
            for hf in range(2):
                if hf:
                    act.wait_ge(ou_full, OU["l0f"] + B + HB)
                for e in range(KC):
                    n, bank = nth(PJ["l0f"], 0, 0, hf * 4 + e)
                    act.wait_ge(pj_done, n + 1)
                    act.activation(grp(AH, e), TY[bank], ACT.Copy).then_inc(lf_hi, 1)

            layer_norm(3)
            act.wait_ge(y_zero, 2)
            with act.Fori(0, HG) as i:
                for hf in range(2):
                    def sigmoid(f):
                        n, bank = nth(PJ["l1a"], i, 20, hf * 10 + f)
                        act.wait_ge(pj_full, n + 1)
                        if f in (4, 5):
                            act.wait_ge(pv_done, i * B + (PV["l1a"] + hf * HB + 1))
                            act.activation(G[:, f - 4, :], pj[bank][:], ACT.Sigmoid).then_inc(la_sg, 1)
                            return
                        x = f if f < 4 else f - 2
                        act.wait_ge(la_lo, i * 16 + (hf * 8 + x + 1))
                        w = 512 if f < 4 else 256
                        act.activation(F[:, x % 2, 0:w], pj[bank][:, 0:w], ACT.Sigmoid).then_inc(la_sg, 1)

                    sigmoid(0)
                    for f in range(10):
                        if f < 9:
                            sigmoid(f + 1)
                        if f in (4, 5):
                            continue
                        x = f if f < 4 else f - 2
                        act.wait_ge(pj_done, i * 20 + (PJ["l1a"] + hf * 10 + f + 1))
                        dst = qk(AH, f // 2, f % 2) if f < 4 else vt(AH, f - 6)
                        act.activation(dst, F[:, x % 2, 0:dst.shape[1]], ACT.Copy).then_inc(la_hi, 1)
                    for j in range(HB):
                        t = i * B + (hf * HB + j)
                        bank = j % 2
                        act.wait_ge(sc_done, t + (SC["l1a"] + 3))
                        act.wait_ge(pv_full, t + (PV["l1a"] - 1))
                        act.activation(tile_a(AH, bank), PR[:, bank, 0:256], ACT.Copy).then_inc(la_sdhi, 1)
                        act.wait_ge(pv_full, t + (PV["l1a"] + 1))
                        act.activation(PR[:, bank, 256:512], pv[:, 0:256], ACT.Square).then_inc(la_sq, 1)
                        act.wait_ge(pv_done, t + (PV["l1a"] + 2))
                        act.wait_ge(ou_full, t + OU["l1a"])
                        act.activation(tile_b(AH), GT[bank], ACT.Copy).then_inc(la_gfhi, 1)
            act.wait_ge(la_v, 1)
            act.activation(SSD[:], SS[:], ACT.Sqrt).then_inc(la_a, 1)

            layer_norm(4)
            act.wait_ge(v_ones, 2)
            for b in range(B):
                fill = nth(PJ["l1xv"], 0, 0, b)
                at = V1 + b * KVH * VW
                hi(fill, AH[:, at:at + KVH * VW].rearrange("p (k w) -> p k w", w=VW)[:, :, 0:HD],
                   pj[fill[1]][:, 0:P].rearrange("p (k w) -> p k w", w=HD))
            for hf in range(2):
                act.wait_ge(kr_full, hf + 1)
                for m, bank in enumerate((sc[0], sc[1], ou[0], ou[1])):
                    last = act.activation(CH[:, m, hf * HALF:(hf + 1) * HALF], bank[:], ACT.Copy)
                last.then_inc(kr_hi, 1)
            with act.Fori(0, 4) as i:
                for c in range(KC):
                    fill = nth(PJ["l1x"], i, 6, c)
                    hi(fill, q1(AH, c), pj[fill[1]][:, 0:256])

                def exps(m):
                    n, bank = nth(0, i, 16, m)
                    act.wait_ge(lx_nm, n + 1)
                    for h in range(GQ):
                        last = act.activation(PR[:, bank, h * S:(h + 1) * S], sc[bank][:, h * S:(h + 1) * S], ACT.Exp,
                                              bias=NM[:, bank, h:h + 1], scale=HD ** -0.5)
                    last.then_inc(lx_exp, 1)

                def turned(bb):
                    fill = nth(PJ["l1x"], i, 6, 4 + bb)
                    act.wait_ge(ou_full, i * 2 + (OU["l1x"] + bb))
                    hi(fill, AH[:, ON1:ON1 + 512], pj[fill[1]][:])

                exps(0)
                for m in range(16):
                    n, bank = nth(TP["l1x"], i, 16, m)
                    act.wait_ge(tp_full, n + 1)
                    act.wait_ge(pv_full, i * 16 + (PV["l1x"] + m - 1))
                    act.activation(AH[:, PT1 + bank * 512:PT1 + (bank + 1) * 512], tp[:], ACT.Copy).then_inc(pt_hi, 1)
                    if m < 15:
                        exps(m + 1)
                    if m == 10:
                        turned(0)
                turned(1)

            for c in range(KC):
                fill = nth(PJ["l1f"], 0, 0, c)
                hi(fill, wpair(WH, 0, 512)[:, c, :], pj[fill[1]][:])
            layer_norm(5)

        @block.vector
        def _(dve):
            def lo(fill, hi_at, dst, src, hi_part, scale=None):
                dve.wait_ge(pj_hi, hi_at + 1)
                if scale is None:
                    dve.tensor_tensor(dst, src, f32(hi_part), ALU.subtract).then_inc(pj_done, 1)
                else:
                    dve.scalar_tensor_tensor(dst, src, scale, f32(hi_part), ALU.mult, ALU.subtract).then_inc(pj_done, 1)

            def add_output(n, bank, dst):
                dve.wait_ge(ou_full, n + 1)
                dve.tensor_tensor(dst, dst, ou[bank][:], ALU.add).then_inc(x_done, 1)

            def layer_norm(l):
                if l == 4:
                    dve.wait_ge(la_y, B)
                elif l:
                    dve.wait_ge(x_done, OU[{1: "l0x", 2: "l0f", 3: "l1a", 5: "l1f"}[l]])
                for b in range(B):
                    last = dve.bn_stats(ST[:, b, :], X[:, b, :])
                last.then_inc(ln_stat, 1)
                dve.wait_ge(ln_stat, l + 1)
                for b in range(B):
                    last = dve.bn_aggr(MV[:, b, :], ST[:, b, :])
                last.then_inc(ln_aggr, 1)
                dve.wait_ge(ln_aggr, l + 1)
                dve.tensor_scalar(VE[:], MV[:, :, 1], EPS, None, ALU.add).then_inc(ln_var, 1)
                dve.wait_ge(ln_std, l + 1)
                dve.reciprocal(RS[:], SD[:]).then_inc(ln_rstd, 1)
                dve.wait_ge(ln_rstd, l + 1)

                def turned(b):
                    n, bank = nth(PJ[f"ln{l}"], 0, 0, b)
                    at = (slice(None), slice(None), slice(b * S, (b + 1) * S))
                    lo((n, bank), HI[f"ln{l}"] + b, XTL[at], pj[bank][:].rearrange("p (c s) -> p c s", c=KC), XTH[at])

                for b in range(B):
                    if b >= 2:
                        dve.wait_ge(pj_full, PJ[f"ln{l}"] + b - 1)
                    dve.tensor_scalar(PR[:, b % 2, :], X[:, b, :], MV[:, b, 0:1], RS[:, b:b + 1],
                                      ALU.subtract, ALU.mult).then_inc(ln_x, 1)
                    if b:
                        turned(b - 1)
                turned(B - 1)

            def dequantise():
                steps = [0]

                def step(ins):
                    steps[0] += 1
                    ins.then_inc(dq, 1)
                    dve.wait_ge(dq, steps[0])

                SHR, SHL, AND, OR = ALU.logical_shift_right, ALU.logical_shift_left, ALU.bitwise_and, ALU.bitwise_or
                step(dve.tensor_copy(QI[:], Q3[:].bitcast(U8).rearrange("p o (n k) -> p o n k", k=3)))
                byte = [QI[:, :, :, k] for k in range(3)]
                fields = [((0, 0, 7),), ((0, 3, 7),), ((0, 6, 3), (1, 1, 2)), ((1, 1, 7),), ((1, 4, 7),),
                          ((1, 7, 1), (2, 3, 1)), ((2, 2, 7),), ((2, 5, 7),)]
                dve.wait_ge(w_ready[0], SLOT["l1x"][0] + 1)
                dve.wait_ge(w_ready[1], SLOT["l1x"][1] + 1)
                w = RAW[:, 0:2, :].rearrange("p s (n v) -> p (s n) v", v=8)
                for v, field in enumerate(fields):
                    k, shift, mask = field[0]
                    step(dve.tensor_scalar(QT[:], byte[k], shift, mask, SHR, AND))
                    if len(field) > 1:
                        k, mask, shift = field[1]
                        step(dve.tensor_scalar(QU[:], byte[k], mask, shift, AND, SHL))
                        step(dve.tensor_tensor(QT[:], QT[:], QU[:], OR))
                    step(dve.tensor_copy(w[:, :, v], QT[:].rearrange("p o n -> p (o n)")))
                norm = QN[:].rearrange("p o g -> p (o g)")
                step(dve.tensor_tensor(QN2[:], norm, norm, ALU.add))
                wf = RAW[:, 0:2, :].rearrange("p s n -> p (s n)")
                wg = RAW[:, 0:2, :].rearrange("p s (g n) -> p (s g) n", n=32)
                step(dve.tensor_scalar(wf, wf, 1.0 / 7.0, None, ALU.mult))
                step(dve.tensor_tensor(wg, wg, QN2[:].unsqueeze(2).broadcast_to((P, 64, 32)), ALU.mult))
                dve.tensor_tensor(wg, wg, norm.unsqueeze(2).broadcast_to((P, 64, 32)), ALU.subtract).then_inc(w_deq, 1)

            dve.sem_inc(sc_done, 2)
            dve.sem_inc(tp_done, 1)
            dve.sem_inc(pv_done, 1)
            dve.sem_inc(sx_nm, B)
            dve.sem_inc(la_lo, 2)
            dve.sem_inc(ff_lo, 1)
            dve.wait_ge(x_in, 32)

            layer_norm(0)
            for hf in range(2):
                up, delta, keep = TY[0], TY[1], TY[2]
                n0, bank0 = nth(PJ["taylor"], 0, 0, 2 * hf)
                dve.wait_ge(pj_full, n0 + 1)
                if hf:
                    dve.wait_ge(ta_lo, TAYLOR)
                dve.tensor_copy(up, pj[bank0][:]).then_inc(ta_t, 1)
                dve.wait_ge(pj_full, n0 + 2)
                dve.wait_ge(ta_t, hf * TAYLOR + 1)
                dve.tensor_scalar(delta, pj[1 - bank0][:], LP[:], None, ALU.subtract).then_inc(ta_d, 1)
                dve.wait_ge(ta_d, hf + 1)
                dve.tensor_scalar(keep, delta, -2.5, None, ALU.is_ge).then_inc(pj_done, 1)
                dve.wait_ge(pj_done, n0 + 1)
                dve.scalar_tensor_tensor(keep, delta, 2.5, keep, ALU.is_le, ALU.mult).then_inc(pj_done, 1)
                for m in range(TAYLOR):
                    if m + 1 < TAYLOR:
                        src, dst = TY[3 * (m % 2)], TY[3 * ((m + 1) % 2)]
                        dve.wait_ge(ta_t, hf * TAYLOR + m + 1)
                        if hf * TAYLOR + m:
                            dve.wait_ge(ta_lo, hf * TAYLOR + m)
                        if m + 1 == 5:
                            dve.tensor_tensor(dst, src, delta, ALU.mult).then_inc(ta_k, 1)
                            dve.wait_ge(ta_k, hf + 1)
                            dve.tensor_tensor(dst, dst, keep, ALU.mult).then_inc(ta_t, 1)
                        else:
                            dve.tensor_tensor(dst, src, delta, ALU.mult).then_inc(ta_t, 1)
                    dve.wait_ge(ta_hi, hf * TAYLOR + m + 1)
                    dve.tensor_tensor(grp(AL, m), TY[3 * (m % 2)], f32(grp(AH, m)), ALU.subtract).then_inc(ta_lo, 1)
                for b in range(HB):
                    n, bank = nth(OU["taylor"], 0, 0, hf * HB + b)
                    add_output(n, bank, X[:, hf * HB + b, :])

            with dve.Fori(0, FG) as i:
                for hf in range(2):
                    for j in range(2):
                        n, bank = nth(PJ["ffn"], i, 8, hf * 4 + 2 * j)
                        dve.wait_ge(ff_sg, i * 4 + (2 * hf + j + 1))
                        dve.wait_ge(ff_lo, i * 4 + (2 * hf + j + 1))
                        dve.tensor_tensor(HF, pj[bank][:], SG, ALU.mult).then_inc(pj_done, 1)
                        dve.wait_ge(pj_full, n + 2)
                        dve.wait_ge(pj_done, n + 1)
                        dve.tensor_tensor(HF, HF, pj[1 - bank][:], ALU.mult).then_inc(pj_done, 1)
                        dve.wait_ge(ff_hi, i * 4 + (2 * hf + j + 1))
                        dve.tensor_tensor(grp(AL, j), HF, f32(grp(AH, j)), ALU.subtract).then_inc(ff_lo, 1)
                    for b in range(HB):
                        n, bank = nth(OU["ffn"], i, B, hf * HB + b)
                        add_output(n, bank, X[:, hf * HB + b, :])

            dve.wait_ge(mask_in, 16)
            dve.tensor_scalar(MF, MI[:].bitcast(U8).rearrange("p b s -> p (b s)"), -1.0, MASKED,
                              ALU.add, ALU.mult).then_inc(m_ready, 1)
            layer_norm(1)
            with dve.Fori(0, HG) as i:
                for hf in range(2):
                    for f in range(8):
                        fill = nth(PJ["l0x"], i, 16, hf * 8 + f)
                        at = i * 16 + (HI["l0x"] + hf * 8 + f)
                        bank = pj[fill[1]]
                        if f < 4:
                            lo(fill, at, qk(AL, f // 2, f % 2), bank[:], qk(AH, f // 2, f % 2), S ** -0.5 if f < 2 else None)
                        else:
                            lo(fill, at, vt(AL, f - 4), bank[:, 0:256], vt(AH, f - 4))

                    def biased_max(j):
                        n, bank = nth(0, i, B, hf * HB + j)
                        dve.wait_ge(fm_ready[hf], i * 2 + 2)
                        dve.wait_ge(sc_full, n + 1)
                        dve.sem_inc(dve_gate, 1)
                        for h in range(2):
                            last = dve.tensor_tensor_reduce(
                                out=PR[:, bank, h * S:(h + 1) * S], in0=sc[bank][:, h * S:(h + 1) * S],
                                in1=FS[:, hf, j, h, :], scale=1.0, scalar=-3e38, op0=ALU.add, op1=ALU.max,
                                accum_out=MX[:, bank, h:h + 1])
                        last.then_inc(sc_done, 1)
                        dve.wait_ge(sc_done, n + 3)
                        dve.tensor_scalar(NM[:, bank, 0:2], MX[:, bank, 0:2], -1.0, MASKED / 10,
                                          ALU.mult, ALU.min).then_inc(sx_nm, 1)

                    def normalise(j):
                        n, bank = nth(0, i, B, hf * HB + j)
                        dve.wait_ge(sx_exp, n + 1)
                        dve.tensor_scalar(SM[:], SU[:, bank, :], 1e-30, None, ALU.max).then_inc(sx_sm, 1)
                        dve.wait_ge(sx_sm, n + 1)
                        dve.reciprocal(RC[:, 0:2], SM[:]).then_inc(sx_rc, 1)
                        dve.wait_ge(sx_rc, n + 1)
                        t = PR[:, bank, 0:256].rearrange("p (h s) -> p h s", h=2)
                        dve.tensor_tensor(t, t, RC[:, 0:2].unsqueeze(2).broadcast_to((P, 2, S)),
                                          ALU.mult).then_inc(sx_pn, 1)

                    def add(j):
                        n, bank = nth(OU["l0x"], i, B, hf * HB + j)
                        add_output(n, bank, X[:, hf * HB + j, :])

                    biased_max(0)
                    normalise(0)
                    for j in range(HB):
                        n, bank = nth(0, i, B, hf * HB + j)
                        if j + 1 < HB:
                            biased_max(j + 1)
                        dve.wait_ge(pt_hi, n + 1)
                        dve.tensor_tensor(tile_a(AL), tp[:, 0:256], f32(tile_a(AH)), ALU.subtract).then_inc(tp_done, 1)
                        if j:
                            add(j - 1)
                        if j + 1 < HB:
                            normalise(j + 1)
                        dve.wait_ge(ct_hi, n + 1)
                        dve.tensor_tensor(tile_b(AL), pv[:, 0:256], f32(tile_b(AH)), ALU.subtract).then_inc(pv_done, 1)
                    add(HB - 1)

            layer_norm(2)
            dve.wait_ge(pj_done, PJ["ln2"] + B)
            for dst, t in ((XM, XTH), (XM2, XTL)):
                dve.tensor_reduce(dst[:].rearrange("p c b -> p (c b)"),
                                  f32(t[:]).rearrange("p c (b s) -> p (c b) s", b=B), axis=AX.X, op=ALU.add).then_inc(lf_sum, 1)
            dve.wait_ge(lf_sum, 2)
            dve.tensor_tensor(XM3[:], XM[:], XM2[:], ALU.add).then_inc(lf_sum, 1)
            for b in range(B):
                n, bank = nth(OU["l0f"], 0, 0, b)
                add_output(n, bank, X[:, b, :])
            dve.wait_ge(lf_pe, 1)
            dve.tensor_scalar(LQT[:], sc[0][:, 0:B], 1.0 / S, None, ALU.mult).then_inc(lf_v, 1)
            dve.wait_ge(lf_pe, 2)
            dve.tensor_reduce(LSM[:, 0:1], sc[1][0:B, 0:E], axis=AX.X, op=ALU.max).then_inc(lf_v, 1)
            dve.wait_ge(lf_v, 2)
            dve.tensor_scalar(LSM[:, 1:2], LSM[:, 0:1], -P ** -0.5, None, ALU.mult).then_inc(lf_v, 1)
            dve.wait_ge(lf_a, 1)
            dve.reciprocal(LSM[:, 3:4], LSM[:, 2:3]).then_inc(lf_v, 1)
            dve.wait_ge(lf_v, 4)
            dve.tensor_scalar(LCO[:], LS[:], LSM[:, 3:4], None, ALU.mult).then_inc(lf_v, 1)
            dve.wait_ge(lf_pe, 3)
            dve.tensor_copy(LCT[:], sc[0][0:E, 0:B]).then_inc(lf_v, 1)
            dve.wait_ge(lf_pe, 4)
            dve.tensor_copy(LCR[:].rearrange("p c b -> p (c b)"), sc[1][:, 0:KC * B]).then_inc(lf_v, 1)
            dve.wait_ge(lf_v, 7)
            for hf in range(2):
                for e in range(KC):
                    n, bank = nth(PJ["l0f"], 0, 0, hf * 4 + e)
                    dve.wait_ge(pj_full, n + 1)
                    dve.tensor_tensor(TY[bank].rearrange("p (b s) -> p b s", b=HB),
                                      pj[bank][:].rearrange("p (b s) -> p b s", b=HB),
                                      LCR[:, e, hf * HB:(hf + 1) * HB].unsqueeze(2).broadcast_to((P, HB, S)),
                                      ALU.mult).then_inc(pj_done, 1)
                    dve.wait_ge(lf_hi, hf * 4 + e + 1)
                    dve.tensor_tensor(grp(AL, e), TY[bank], f32(grp(AH, e)), ALU.subtract).then_inc(lf_lo, 1)
                for b in range(HB):
                    n, bank = nth(OU["l0f"], 0, 0, B + hf * HB + b)
                    add_output(n, bank, X[:, hf * HB + b, :])

            layer_norm(3)
            dve.wait_ge(y_zero, 2)
            with dve.Fori(0, HG) as i:
                for hf in range(2):
                    def silu(f):
                        n, bank = nth(PJ["l1a"], i, 20, hf * 10 + f)
                        dve.wait_ge(la_sg, i * 20 + (hf * 10 + f + 1))
                        if f in (4, 5):
                            g = G[:, f - 4, :]
                            dve.tensor_scalar(g, g, NW[:, bass.ds(i * 2 + (f - 4), 1)], None, ALU.mult).then_inc(pj_done, 1)
                            return
                        x = f if f < 4 else f - 2
                        w = 512 if f < 4 else 256
                        dve.tensor_tensor(F[:, x % 2, 0:w], F[:, x % 2, 0:w], pj[bank][:, 0:w], ALU.mult).then_inc(pj_done, 1)

                    silu(0)
                    for f in range(10):
                        if f < 9:
                            silu(f + 1)
                        if f in (4, 5):
                            continue
                        x = f if f < 4 else f - 2
                        at = (lambda t: qk(t, f // 2, f % 2)) if f < 4 else (lambda t: vt(t, f - 6))
                        dve.wait_ge(la_hi, i * 16 + (hf * 8 + x + 1))
                        dve.tensor_tensor(at(AL), F[:, x % 2, 0:at(AL).shape[1]], f32(at(AH)), ALU.subtract).then_inc(la_lo, 1)

                    def decayed(j):
                        n, bank = nth(SC["l1a"], i, B, hf * HB + j)
                        if hf == 0 and j == 0:
                            dve.wait_ge(dt_in, i * 16 + 16)
                        dve.wait_ge(sc_full, n + 1)
                        dve.tensor_tensor(PR[:, bank, 0:256], sc[bank][:, 0:256], DT[:], ALU.mult).then_inc(sc_done, 1)

                    def add(j):
                        n, bank = nth(OU["l1a"], i, B, hf * HB + j)
                        add_output(n, bank, Y[:, hf * HB + j, :])

                    decayed(0)
                    for j in range(HB):
                        t = i * B + (hf * HB + j + 1)
                        bank, b = j % 2, hf * HB + j
                        if j + 1 < HB:
                            decayed(j + 1)
                        dve.wait_ge(la_sdhi, t)
                        dve.tensor_tensor(tile_a(AL, bank), PR[:, bank, 0:256], f32(tile_a(AH, bank)),
                                          ALU.subtract).then_inc(la_sdlo, 1)
                        dve.wait_ge(la_sq, t)
                        dve.tensor_tensor(GT[bank].rearrange("p (h s) -> p h s", h=2),
                                          pv[:, 0:256].rearrange("p (h s) -> p h s", h=2),
                                          G[:, :, j * S:(j + 1) * S], ALU.mult).then_inc(pv_done, 1)
                        dve.tensor_tensor(SQ[:, b, :], SQ[:, b, :], PR[:, bank, 256:512], ALU.add).then_inc(la_sqa, 1)
                        dve.wait_ge(la_gfhi, t)
                        dve.tensor_tensor(tile_b(AL), GT[bank], f32(tile_b(AH)), ALU.subtract).then_inc(la_gflo, 1)
                        if j:
                            add(j - 1)
                    add(HB - 1)
            dve.wait_ge(la_ss, 1)
            dve.tensor_scalar(SS[:], tp[:, 0:B], 1.0 / (2 * HG * P), EPS, ALU.mult, ALU.add).then_inc(la_v, 1)
            dve.wait_ge(la_a, 1)
            dve.reciprocal(YR[:], SSD[:]).then_inc(la_v, 1)
            dve.wait_ge(la_v, 2)
            for b in range(B):
                dve.scalar_tensor_tensor(X[:, b, :], Y[:, b, :], YR[:, b:b + 1], X[:, b, :],
                                         ALU.mult, ALU.add).then_inc(la_y, 1)

            dve.wait_ge(la_y, B)
            dve.memset(f32(AH[:, V1:PT1]), 1.0).then_inc(v_ones, 1)
            dve.memset(f32(AL[:, V1:PT1]), 0.0).then_inc(v_ones, 1)
            layer_norm(4)
            dve.wait_ge(v_ones, 2)
            for b in range(B):
                fill = nth(PJ["l1xv"], 0, 0, b)
                at = V1 + b * KVH * VW
                part = lambda t: t[:, at:at + KVH * VW].rearrange("p (k w) -> p k w", w=VW)[:, :, 0:HD]
                lo(fill, HI["l1xv"] + b, part(AL), pj[fill[1]][:, 0:P].rearrange("p (k w) -> p k w", w=HD), part(AH))
            dequantise()
            for hf in range(2):
                dve.wait_ge(kr_hi, hf + 1)
                at = slice(hf * HALF, (hf + 1) * HALF)
                for m, bank in enumerate((sc[0], sc[1], ou[0], ou[1])):
                    last = dve.tensor_tensor(CL[:, m, at], bank[:], f32(CH[:, m, at]), ALU.subtract)
                last.then_inc(kr_lo, 1)
            with dve.Fori(0, 4) as i:
                for c in range(KC):
                    fill = nth(PJ["l1x"], i, 6, c)
                    lo(fill, i * 6 + (HI["l1x"] + c), q1(AL, c), pj[fill[1]][:, 0:256], q1(AH, c))

                def row_max(m):
                    n, bank = nth(SC["l1x"], i, 16, m)
                    dve.wait_ge(sc_full, n + 1)
                    dve.tensor_reduce(MX[:, bank, :], sc[bank][:].rearrange("p (h s) -> p h s", h=GQ),
                                      axis=AX.X, op=ALU.max).then_inc(lx_max, 1)
                    dve.wait_ge(lx_max, i * 16 + (m + 1))
                    dve.tensor_scalar(NM[:, bank, :], MX[:, bank, :], -HD ** -0.5, None, ALU.mult).then_inc(lx_nm, 1)

                def heads(k):
                    out = pv[:, 0:2 * GQ * VW].rearrange("p (h w) -> p h w", w=VW)
                    dve.wait_ge(pv_full, i * 16 + (PV["l1x"] + 2 * k + 2))
                    dve.reciprocal(RC[:], out[:, :, HD]).then_inc(lx_rc, 1)
                    dve.wait_ge(lx_rc, i * 8 + (k + 1))
                    dve.tensor_tensor(ONT[:, k // 4, (k % 4) * P:(k % 4 + 1) * P].rearrange("p (h w) -> p h w", w=HD),
                                      out[:, :, 0:HD], RC[:].unsqueeze(2).broadcast_to((P, 2 * GQ, HD)),
                                      ALU.mult).then_inc(pv_done, 1)

                def turned(bb):
                    fill = nth(PJ["l1x"], i, 6, 4 + bb)
                    lo(fill, i * 6 + (HI["l1x"] + 4 + bb), AL[:, ON1:ON1 + 512], pj[fill[1]][:], AH[:, ON1:ON1 + 512])

                def add(bb):
                    n, bank = nth(OU["l1x"], i, 2, bb)
                    add_output(n, bank, X[:, bass.ds(i * 2 + bb, 1), :].rearrange("p a d -> p (a d)"))

                row_max(0)
                for m in range(16):
                    n, bank = nth(TP["l1x"], i, 16, m)
                    if m < 15:
                        row_max(m + 1)
                    dve.wait_ge(pt_hi, n + 1)
                    at = slice(PT1 + bank * 512, PT1 + (bank + 1) * 512)
                    dve.tensor_tensor(AL[:, at], tp[:], f32(AH[:, at]), ALU.subtract).then_inc(tp_done, 1)
                    if m and m % 2 == 0:
                        heads(m // 2 - 1)
                    if m == 10:
                        turned(0)
                    if m == 13:
                        add(0)
                heads(7)
                turned(1)
                add(1)

            for c in range(KC):
                fill = nth(PJ["l1f"], 0, 0, c)
                lo(fill, HI["l1f"] + c, wpair(WL, 0, 512)[:, c, :], pj[fill[1]][:], wpair(WH, 0, 512)[:, c, :])
            layer_norm(5)
            for b in range(B):
                dve.tensor_tensor(X[:, b, :], X[:, b, :], BIAS[:], ALU.add).then_inc(bias_added, 1)
            for b in range(B):
                n, bank = nth(OU["l1f"], 0, 0, b)
                dve.wait_ge(bias_added, b + 1)
                add_output(n, bank, X[:, b, :])


def arr(a):
    return np.ascontiguousarray(a)


def blocks(w):
    return w.reshape(-1, P, w.shape[-1]).transpose(1, 0, 2)


def kernel(**inputs):
    import concourse.bacc as bacc
    from concourse.bass_utils import run_bass_kernel_spmd as run

    g = {k: np.asarray(v) for k, v in inputs.items()}
    L0, L1 = "L0_attn_", "L1_attn_"
    tw = np.zeros((NSLOT, P, PIECE), np.float32)
    tw[0] = blocks(np.concatenate([g[L0 + "up_w"].T, g[L0 + "gate_w"].T], 1)).reshape(P, PIECE)
    terms = [g[L0 + "local_approx_output"].T] + [g[L0 + "fuse_weight"][:, :, m].T for m in range(6)]
    for m, t in enumerate(terms):
        tw[1 + m // 2, :, (m % 2) * 512:(m % 2 + 1) * 512] = t
    fp = [np.zeros((FPAD, D), np.float32) for _ in range(3)]
    for dst, src in zip(fp, (g[L0 + "ffn_gate_w"], g[L0 + "ffn_up_w"], g[L0 + "ffn_down_w"].T)):
        dst[:src.shape[0]] = src

    def in_cols(w):
        return w.reshape(-1, 256, KC, P).transpose(0, 3, 2, 1).reshape(-1, P, PIECE)

    def out_rows(w):
        return w.reshape(-1, 2, P, 512).transpose(0, 2, 1, 3).reshape(-1, P, PIECE)

    def square(w):
        return blocks(w).reshape(P, 2, PIECE).transpose(1, 0, 2)

    ffn = np.stack([in_cols(fp[0]), in_cols(fp[1]), out_rows(fp[2])], 1)
    X0 = "L0_xattn_"
    l0x = np.stack([in_cols(g[X0 + n].T) for n in ("Wq", "Wk", "Wv")] + [out_rows(g[X0 + "Wo"])], 1)
    F0 = "L0_ffn_"
    l0f = np.concatenate([square(g[F0 + "W_org"].T),
                          square(g[F0 + "lora_down"].transpose(1, 0, 2).reshape(D, E * R)),
                          square(g[F0 + "lora_up"].reshape(E * R, D))])
    qkv = g[L1 + "qkv_w"].reshape(2 * HG, 3, P, D).transpose(1, 0, 2, 3).reshape(3, 2 * HG * P, D)
    l1a = np.stack([in_cols(qkv[n]) for n in range(3)] + [in_cols(g[L1 + "gate_w"]), out_rows(g[L1 + "out_w"].T)], 1)
    X1 = "L1_xattn_"
    wk = np.repeat(g[X1 + "Wk"].reshape(D, KVH, 1, HD), GQ, 2).reshape(D, D)
    wv = np.zeros((D, 256), np.float32)
    wv[:, :P] = g[X1 + "Wv"]
    l1x = np.concatenate([square(g[X1 + "Wq"]), square(wk), blocks(wv).reshape(1, P, PIECE), square(g[X1 + "Wo"])])
    side = g["fside_Bx32xSxS2_0"].reshape(2, HB, HG, 2, S, S).transpose(2, 0, 4, 1, 3, 5).reshape(HG, 2, P, 1024)
    q3 = g["L1_ffn_weight_q3"].reshape(D, 16 * 12).view(np.int32).reshape(4, P, 48).transpose(1, 0, 2)
    q3n = g["L1_ffn_weight_norm"].reshape(4, P, 16).transpose(1, 0, 2)
    slope = (1.0 / 2.0 ** (8.0 / 32)) ** (np.arange(32) + 1.0) * (1.0 - 1 / (32 - 1 + 1e-05) + 1e-05)
    diff = np.arange(S)[None, :] - np.arange(S)[:, None]
    decay = np.where(diff >= 0, np.exp(-slope[:, None, None] * np.maximum(diff, 0)), 0.0).astype(np.float32)
    decay = decay.reshape(HG, 2, P, S).transpose(0, 2, 1, 3).reshape(HG, P, 256)
    experts = (np.arange(E * R)[None, :] // R == np.arange(E)[:, None]).astype(np.float32)
    arrays = dict(
        x=g["x"], ctx_t=g["ctx_4096"].reshape(T, KC, P).transpose(1, 2, 0), side=side,
        mask=g["mask_BxSxS2_bk0"].view(np.int32).transpose(1, 0, 2),
        taylor_w=tw, ffn_w=ffn, l0x_w=l0x, l0f_w=l0f, l1a_w=l1a, l1x_w=l1x,
        identity=np.eye(P, dtype=np.float32), local_point=g[L0 + "local_point"].reshape(P, 1),
        discount=np.broadcast_to(g[L0 + "discount_factor"], (P, 6)),
        bias=np.broadcast_to(g["L1_ffn_bias"], (P, D)), lora_keys=g[F0 + "lora_keys"].T,
        lora_wq=blocks(g[F0 + "Wq"].T), expert_rows=experts.reshape(E, KC, P),
        norm_w=g[L1 + "norm_w"].reshape(2 * HG, P).T, one=np.ones((P, 1), np.float32),
        block_mask=(np.arange(P)[:, None] % 64 // HD == np.arange(GQ)[None, :]).astype(np.float32),
        q3=q3, q3_norm=q3n, decay=decay)
    nc = bacc.Bacc("TRN2", target_bir_lowering=False, num_devices=1)
    sent, aps = {}, {}
    for name, v in arrays.items():
        v = arr(v)
        sent["in_" + name] = v
        aps[name] = nc.dram_tensor("in_" + name, v.shape, mybir.dt.from_np(v.dtype), kind="ExternalInput").ap()
    aps["out"] = nc.dram_tensor("out_x", (B, S, D), FP32, kind="ExternalOutput").ap()
    build(nc, aps)
    r = run(nc, [sent], core_ids=[0])
    return r.results[0]["out_x"]
```

```python
import numpy as np
import concourse.bass as bass
from concourse import mybir
from contextlib import ExitStack

FP32 = mybir.dt.float32
F32R = mybir.dt.float32r
I32 = mybir.dt.int32
U8 = mybir.dt.uint8
ACT = mybir.ActivationFunctionType
ALU = mybir.AluOpType
AX = mybir.AxisListType

P = 128
B, S, D = 8, 128, 512
T = B * S
KC = D // P
HALF = T // 2
HB = B // 2
NSLOT, PIECE = 5, 1024
TAYLOR = 7
FG = 5
FPAD = FG * 256
HG = 16
E, R = 8, 64
KVH, GQ, HD = 8, 4, 16
VW = HD + 2
EPS = 1e-5
MASKED = 1e30

PJ_PER = dict(ln=B, taylor=4, ffn=FG * 8, l0x=HG * 16, l0f=8, l1a=HG * 20, l1xv=B, l1x=4 * 6, l1f=4)
PJ_ORDER = ["ln0", "taylor", "ffn", "ln1", "l0x", "ln2", "l0f", "ln3", "l1a", "ln4", "l1xv", "l1x", "l1f", "ln5"]
OU_PER = dict(taylor=B, ffn=FG * B, l0x=HG * B, l0f=2 * B, l1a=HG * B, l1x=B, l1f=B)
OU_ORDER = ["taylor", "ffn", "l0x", "l0f", "l1a", "l1x", "l1f"]


CONSTS_IN = ["identity", "local_point", "discount", "bias", "lora_keys", "lora_wq", "expert_rows", "norm_w",
             "one", "block_mask", "q3", "q3_norm"]


FFN_STEPS = [("F", 0), ("O", 0), ("F", 1), ("O", 1), ("F", 2), ("O", 2), ("F", 3), ("O", 3)]
L0X_STEPS = [("T", 0), ("F", 0), ("V", 0), ("T", 1), ("F", 1), ("O", 0), ("V", 1), ("T", 2), ("F", 2), ("O", 1),
             ("V", 2), ("T", 3), ("F", 3), ("O", 2), ("V", 3), ("F", 4), ("S", 0), ("O", 3), ("F", 5), ("F", 6),
             ("F", 7)]
L1A_STEPS = [("F", 0), ("V", 0), ("F", 1), ("O", 0), ("V", 1), ("F", 2), ("O", 1), ("V", 2), ("F", 3), ("O", 2),
             ("V", 3), ("F", 4), ("O", 3), ("F", 5), ("S", 0), ("F", 6), ("F", 7), ("F", 8), ("F", 9)]


def halves(engine, groups, half):
    last = groups - 1
    half((0, 0), None)
    with engine.Fori(0, last) as i:
        half((i, 1), (i, 0))
        half((i + 1, 0), (i, 1))
    half((last, 1), (last, 0))
    half(None, (last, 1))


def starts(order, per):
    at, out = 0, {}
    for name in order:
        out[name] = at
        at += per["ln" if name[:2] == "ln" else name]
    return out


PJ = starts(PJ_ORDER, PJ_PER)
HI = starts(PJ_ORDER, {k: v if k in ("ln", "l0x", "l1xv", "l1x", "l1f") else 0 for k, v in PJ_PER.items()})
OU = starts(OU_ORDER, OU_PER)
SC = dict(l0x=0, l1a=HG * B, l1x=2 * HG * B)
PV = dict(l0x=0, l1a=HG * B, l1x=2 * HG * B)
TP = dict(l0x=0, l1x=HG * B)
W_T, W_F, W_X, W_L = 0, 1, 1 + FG, 1 + FG + HG
SLOT = dict(
    taylor=[0] * 5,
    ffn=[1, 1, 1],
    l0x=[1 + FG, 1 + FG, 1 + FG, 1],
    l0f=[1 + FG + HG, 1 + FG + HG, 1 + FG + HG, 1 + HG, 1],
    l0f_up=2 + FG + HG,
    l1a=[3 + FG + HG, 2 + FG + HG, 2 + FG + HG, 2 + HG, 2],
    l1x=[3 + FG + 2 * HG, 2 + FG + 2 * HG, 2 + FG + 2 * HG, 2 + 2 * HG, 2 + HG],
    l1x_o=[3 + FG + 2 * HG, 3 + 2 * HG],
)


def build(nc, a):
    ctx = ExitStack()
    with ctx:
        def sb(name, shape, dt=FP32):
            return ctx.enter_context(nc.sbuf_tensor(name, shape, dt))

        def psum(name):
            return ctx.enter_context(nc.psum_tensor(name, [P, 512], FP32))

        def sem(name):
            return ctx.enter_context(nc.semaphore(name))

        RAW = sb("raw", [P, NSLOT, PIECE])
        WH = sb("w_hi", [P, NSLOT, PIECE], F32R)
        WL = sb("w_lo", [P, NSLOT, PIECE], F32R)
        X = sb("x", [P, B, D])
        XTH = sb("xt_hi", [P, KC, T], F32R)
        XTL = sb("xt_lo", [P, KC, T], F32R)
        with ExitStack() as shared:
            Y = shared.enter_context(nc.sbuf_tensor("y", [P, B, D], FP32))
            SQ = shared.enter_context(nc.sbuf_tensor("sumsq", [P, B, 256], FP32))
            G = shared.enter_context(nc.sbuf_tensor("gate", [P, 2, 512], FP32))
            F = shared.enter_context(nc.sbuf_tensor("silu", [P, 2, 512], FP32))
        CH = sb("ctx_hi", [P, KC, T], F32R)
        CL = sb("ctx_lo", [P, KC, T], F32R)
        NA = 3840
        AH = sb("act_hi", [P, NA], F32R)
        AL = sb("act_lo", [P, NA], F32R)
        with ExitStack() as shared:
            FS = shared.enter_context(nc.sbuf_tensor("side", [P, 2, HB, 2, S], FP32))
        KXH = sb("keys_hi", [P, 2, 512], F32R)
        KXL = sb("keys_lo", [P, 2, 512], F32R)
        M = sb("mask_bias", [P, B, S])
        PR = sb("probs", [P, 2, 512])
        DT = sb("decay", [P, 256])
        IDN = sb("identity", [P, P])
        MI = sb("mask_int", [P, B, S // 4], I32)
        BIAS = sb("bias", [P, D])
        Q3 = sb("q3_packed", [P, 4, 16 * 3], I32)
        QN = sb("q3_norm", [P, 4, 16])
        QI = sb("q3_int", [P, 4, 64, 3], I32)
        QT = sb("q3_tmp", [P, 4, 64], I32)
        QU = sb("q3_tmp2", [P, 4, 64], I32)
        QN2 = sb("q3_norm2", [P, 64])
        ST = sb("bn_stats", [P, B, 6])
        MV = sb("bn_mean_var", [P, B, 2])
        VE = sb("var_eps", [P, B])
        SD = sb("std", [P, B])
        RS = sb("rstd", [P, B])
        LP = sb("local_point", [P, 1])
        DC = sb("discount", [P, 6])
        CE = sb("coef_exp", [P, 6])
        MX = sb("row_max", [P, 4, 4])
        NM = sb("neg_max", [P, 4, 4])
        SU = sb("row_sum", [P, 4, 2])
        SM = sb("row_sum_min", [P, 2])
        RC = sb("row_recip", [P, 8])
        KEYS = sb("lora_keys", [P, E])
        LQ = sb("lora_wq", [P, KC, P])
        SEL = sb("expert_rows", [E, KC, P])
        XM = sb("x_sum", [P, KC, B])
        XM2 = sb("x_sum_lo", [P, KC, B])
        XM3 = sb("x_sum_all", [P, KC, B])
        LQT = sb("lora_q", [P, B])
        LS = sb("lora_exp", [B, E])
        LSM = sb("lora_stats", [B, 4])
        LCO = sb("lora_coef", [B, E])
        LCT = sb("lora_coef_t", [E, B])
        LCR = sb("lora_coef_rows", [P, KC, B])
        NW = sb("norm_w", [P, 2 * HG])
        ONE = sb("one", [P, 1])
        BM = sb("block_mask", [P, GQ])
        SS = sb("mean_sq", [P, B])
        SSD = sb("mean_sq_std", [P, B])
        YR = sb("y_scale", [P, B])

        pj = [psum("pj0"), psum("pj1")]
        sc = [psum("sc0"), psum("sc1")]
        tp = psum("tp")
        pv = psum("pv")
        ou = [psum("ou0"), psum("ou1")]

        consts_in, x_in, fs_in, mask_in, out_done = sem("consts_in"), sem("x_in"), [sem("fs_in0"), sem("fs_in1")], sem("mask_in"), sem("out_done")
        dt_in = sem("dt_in")
        w_in = [sem(f"w_in{s}") for s in range(NSLOT)]
        w_scaled = sem("w_scaled")
        w_hi = [sem(f"w_hi{s}") for s in range(NSLOT)]
        w_ready = [sem(f"w_ready{s}") for s in range(NSLOT)]
        pool_gate, dve_gate = sem("pool_gate"), sem("dve_gate")
        c_in, c_hi, c_ready = [sem("c_in0"), sem("c_in1")], sem("c_hi"), sem("c_ready")
        passed = sem("passed")
        ln_stat, ln_aggr, ln_var, ln_std, ln_rstd, ln_x = (sem(n) for n in
            ("ln_stat", "ln_aggr", "ln_var", "ln_std", "ln_rstd", "ln_x"))
        pj_full, pj_hi, pj_done = sem("pj_full"), sem("pj_hi"), sem("pj_done")
        ou_full, x_done = sem("ou_full"), sem("x_done")
        sc_full, sc_done = sem("sc_full"), sem("sc_done")
        tp_full, pt_hi, tp_done = sem("tp_full"), sem("pt_hi"), sem("tp_done")
        pv_full, ct_hi, pv_done = sem("pv_full"), sem("ct_hi"), sem("pv_done")
        ce_ready, ta_u, ta_d, ta_k, ta_t, ta_hi, ta_lo = (sem(n) for n in
            ("ce_ready", "ta_u", "ta_d", "ta_k", "ta_t", "ta_hi", "ta_lo"))
        ff_sg, ff_g, ff_h, ff_hi, ff_lo = (sem(n) for n in ("ff_sg", "ff_g", "ff_h", "ff_hi", "ff_lo"))
        m_ready, fm_ready = sem("m_ready"), [sem("fm_ready0"), sem("fm_ready1")]
        sx_nm, sx_exp, sx_sm, sx_rc, sx_pn = (sem(n) for n in ("sx_nm", "sx_exp", "sx_sm", "sx_rc", "sx_pn"))
        lf_sum, lf_pe, lf_v, lf_a, lf_f, lf_hi, lf_lo = (sem(n) for n in
            ("lf_sum", "lf_pe", "lf_v", "lf_a", "lf_f", "lf_hi", "lf_lo"))
        y_zero, la_sg, la_f, la_hi, la_lo, la_sd, la_sdhi, la_sdlo, la_sq, la_sqa, la_gf, la_gfhi, la_gflo = (
            sem(n) for n in ("y_zero", "la_sg", "la_f", "la_hi", "la_lo", "la_sd", "la_sdhi", "la_sdlo", "la_sq",
                             "la_sqa", "la_gf", "la_gfhi", "la_gflo"))
        la_ss, la_v, la_a, la_y = sem("la_ss"), sem("la_v"), sem("la_a"), sem("la_y")
        v_ones, kr_full, kr_hi, kr_lo, kx_ready, lx_max, lx_nm, lx_exp, lx_rc, lx_on = (sem(n) for n in
            ("v_ones", "kr_full", "kr_hi", "kr_lo", "kx_ready", "lx_max", "lx_nm", "lx_exp", "lx_rc", "lx_on"))
        dq, w_deq, bias_added = sem("dq"), sem("w_deq"), sem("bias_added")

        def f32(ap):
            return ap.bitcast(FP32)

        def wslot(t, s, cols):
            return t[:, s, :].rearrange("p (c n) -> p c n", n=cols)

        def wpair(t, s, cols):
            return t[:, s:s + 2, :].rearrange("p s (c n) -> p (s c) n", n=cols)

        def qk(t, which, h):
            return t[:, (2 * which + h) * 512:(2 * which + h + 1) * 512]

        def vt(t, j):
            return t[:, 2048 + j * 256:2048 + (j + 1) * 256]

        def tile_a(t, n=0):
            return t[:, 3072 + n * 256:3328 + n * 256]

        def tile_b(t):
            return t[:, 3584:3840]

        def grp(t, m):
            return t[:, m * 512:(m + 1) * 512]

        def q1(t, c):
            return t[:, c * 256:(c + 1) * 256]

        V1 = 1024
        PT1 = V1 + B * KVH * VW
        ON1 = PT1 + 1024
        ONT = M[:, :, :].rearrange("p (r c) s -> p r (c s)", r=2)

        FSF = FS[:, :, :, :, :].rearrange("p a b h s -> p (a b h s)")
        TY = [FSF[:, n * 512:(n + 1) * 512] for n in range(4)]
        MF = M[:, :, :].rearrange("p b s -> p (b s)")
        GT = [FSF[:, 0:256], FSF[:, 256:512]]
        SQT = [FSF[:, 512:768], FSF[:, 768:1024]]
        HF = [MF[:, 0:512], MF[:, 512:1024]]
        SG = PR[:, 0, :]

        def part(t, j):
            return t[:, j // 2, (j % 2) * 256:(j % 2 + 1) * 256]

        def score(j):
            return sc[j // 2][:, (j % 2) * 256:(j % 2 + 1) * 256]

        def turned_probs(j):
            return tp[:, (j % 2) * 256:(j % 2 + 1) * 256]

        def nth(base, i, per, j):
            return i * per + (base + j), (base + j) % 2

        block = ctx.enter_context(nc.Block())
        CONSTS = [IDN[:], LP[:], DC[:], BIAS[:], KEYS[:], LQ[:], SEL[:], NW[:], ONE[:], BM[:], Q3[:], QN[:]]

        @block.sync
        def _(sp):
            def load(s, k, src):
                if not isinstance(k, int) or k > 0:
                    sp.wait_ge(w_ready[s], k)
                sp.dma_start(RAW[:, s, :], src).then_inc(w_in[s], 16)

            def load_ctx(n, c):
                if n or c >= 2:
                    sp.wait_ge(c_ready, KC * n + max(c - 1, 0))
                sp.dma_start(FSF[:, (c % 2) * T:(c % 2 + 1) * T], a["ctx_t"][c]).then_inc(c_in[c % 2], 16)

            for n in range(2):
                sp.dma_start(X[:, n * HB:(n + 1) * HB, :],
                             a["x"][n * HB:(n + 1) * HB].rearrange("b p d -> p b d")).then_inc(x_in, 16)
            for dst, name in zip(CONSTS, CONSTS_IN):
                sp.dma_start(dst, a[name]).then_inc(consts_in, 16)
            for s in range(NSLOT):
                load(s, 0, a["taylor_w"][s])
            sp.dma_start(MI[:], a["mask"]).then_inc(mask_in, 16)
            for s in range(3):
                load(s, SLOT["ffn"][s], a["ffn_w"][0, s])
            sp.wait_ge(ta_lo, 2 * TAYLOR)
            load_ctx(0, 0)
            load_ctx(0, 1)
            with sp.Fori(1, FG) as i:
                for s in range(3):
                    load(s, i + SLOT["ffn"][s], a["ffn_w"][bass.ds(i, 1), s].rearrange("a p n -> (a p) n"))
            load_ctx(0, 2)
            load_ctx(0, 3)
            sp.wait_ge(c_ready, KC)
            with sp.Fori(0, HG) as i:
                for s in range(4):
                    load(s, i + SLOT["l0x"][s], a["l0x_w"][bass.ds(i, 1), s].rearrange("a p n -> (a p) n"))
                for hf in range(2):
                    sp.wait_ge(sx_nm, i * B + (hf + 1) * HB)
                    sp.dma_start(FS[:, hf].rearrange("p b h s -> p (b h s)"),
                                 a["side"][bass.ds(i, 1), hf].rearrange("a p n -> (a p) n")).then_inc(fs_in[hf], 16)
            for s in range(NSLOT):
                load(s, SLOT["l0f"][s], a["l0f_w"][s])
            load(0, SLOT["l0f_up"], a["l0f_w"][NSLOT])
            with sp.Fori(0, HG) as i:
                for s in range(NSLOT):
                    load(s, i + SLOT["l1a"][s], a["l1a_w"][bass.ds(i, 1), s].rearrange("a p n -> (a p) n"))
                sp.wait_ge(sc_done, i * B + 2 + SC["l1a"])
                sp.dma_start(DT[:], a["decay"][bass.ds(i, 1)].rearrange("a p n -> (a p) n")).then_inc(dt_in, 16)
            for s in range(NSLOT):
                load(s, SLOT["l1x"][s], a["l1x_w"][s])
            sp.wait_ge(la_gflo, HG * B)
            for c in range(KC):
                load_ctx(1, c)
            for s in range(2):
                load(2 + s, SLOT["l1x_o"][s], a["l1x_w"][NSLOT + s])
            for b in range(B):
                sp.wait_ge(x_done, OU["l1f"] + b + 1)
                sp.dma_start(a["out"][b], X[:, b, :]).then_inc(out_done, 16)
            sp.wait_ge(out_done, 16 * B)

        @block.gpsimd
        def _(pool):
            def hold(*waits):
                for s, v in waits:
                    pool.wait_ge(s, v)
                pool.sem_inc(passed, 1)

            def split(s, k, free=None, scale=None):
                pool.wait_ge(w_in[s], k * 16 + 16)
                if scale is not None:
                    scale()
                hold(*([free] if free else []))
                pool.tensor_tensor(WH[:, s, :], RAW[:, s, :], ONE[:].broadcast_to((P, PIECE)), ALU.mult).then_inc(w_hi[s], 1)
                pool.wait_ge(w_hi[s], k + 1)
                pool.tensor_tensor(WL[:, s, :], RAW[:, s, :], f32(WH[:, s, :]), ALU.subtract).then_inc(w_ready[s], 1)

            def split_ctx(n):
                for c in range(KC):
                    src = FSF[:, (c % 2) * T:(c % 2 + 1) * T]
                    pool.wait_ge(c_in[c % 2], 16 * (2 * n + c // 2 + 1))
                    pool.tensor_tensor(CH[:, c, :], src, ONE[:].broadcast_to((P, T)), ALU.mult).then_inc(c_hi, 1)
                    pool.wait_ge(c_hi, KC * n + c + 1)
                    pool.tensor_tensor(CL[:, c, :], src, f32(CH[:, c, :]), ALU.subtract).then_inc(c_ready, 1)

            def scale_powers(s):
                for j in range(2):
                    m = 2 * (s - 1) + j
                    if 1 <= m < TAYLOR:
                        blk = RAW[:, s, j * 512:(j + 1) * 512]
                        pool.tensor_scalar(blk, blk, CE[:, m - 1:m], None, ALU.mult).then_inc(w_scaled, 1)
                pool.wait_ge(w_scaled, min(2 * s, TAYLOR) - 1)

            pool.wait_ge(consts_in, 16 * len(CONSTS))
            split(0, 0)
            pool.wait_ge(ce_ready, 1)
            for s in range(1, NSLOT):
                split(s, 0, scale=lambda s=s: scale_powers(s))
            for s in range(3):
                split(s, SLOT["ffn"][s], (ou_full, OU["taylor"] + B) if s else (pj_full, PJ["taylor"] + 4))
            with pool.Fori(1, FG) as i:
                split(0, i + SLOT["ffn"][0], (pj_full, i * 8 + (PJ["ffn"] - 1)))
                split(1, i + SLOT["ffn"][1], (pj_full, i * 8 + PJ["ffn"]))
                split(2, i + SLOT["ffn"][2], (ou_full, i * B + OU["ffn"]))
            split_ctx(0)
            pool.wait_ge(m_ready, 1)
            with pool.Fori(0, HG) as i:
                for s, ahead in enumerate((6, 4, 0)):
                    split(s, i + SLOT["l0x"][s], (pj_full, i * 16 + (PJ["l0x"] - ahead)))
                for hf in range(2):
                    pool.wait_ge(fs_in[hf], i * 16 + 16)
                    for h in range(2):
                        pool.tensor_tensor(FS[:, hf, :, h, :], FS[:, hf, :, h, :], M[:, hf * HB:(hf + 1) * HB, :],
                                           ALU.add).then_inc(fm_ready[hf], 1)
                split(3, i + SLOT["l0x"][3], (ou_full, i * B + OU["l0x"]))
            split(0, SLOT["l0f"][0], (pj_full, PJ["l0x"] + HG * 16 - 6))
            split(1, SLOT["l0f"][1], (pj_full, PJ["l0x"] + HG * 16 - 4))
            split(2, SLOT["l0f"][2], (pj_full, PJ["l0x"] + HG * 16))
            split(3, SLOT["l0f"][3], (ou_full, OU["l0x"] + HG * B))
            split(4, SLOT["l0f"][4], (ou_full, OU["taylor"] + B))
            split(0, SLOT["l0f_up"], (ou_full, OU["l0f"] + B))
            pool.memset(Y[:], 0.0).then_inc(y_zero, 1)
            pool.memset(SQ[:], 0.0).then_inc(y_zero, 1)
            pool.wait_ge(ou_full, OU["l0f"] + 2 * B)
            with pool.Fori(0, HG) as i:
                for s, ahead in enumerate((8, 6, 0, 4)):
                    split(s, i + SLOT["l1a"][s], (pj_full, i * 20 + (PJ["l1a"] - ahead)))
                split(4, i + SLOT["l1a"][4], (ou_full, i * B + OU["l1a"]))
            for s, ahead in enumerate((8, 6, 0, 4)):
                split(s, SLOT["l1x"][s], (pj_full, PJ["l1a"] + HG * 20 - ahead))
            split(4, SLOT["l1x"][4], (ou_full, OU["l1a"] + HG * B))
            pool.wait_ge(la_y, B)
            split_ctx(1)
            for s in range(2):
                split(2 + s, SLOT["l1x_o"][s], (kr_full, 2))
            pool.wait_ge(kr_lo, 2)
            with pool.Fori(0, 4) as i:
                for bb in range(2):
                    for c in range(KC):
                        n = bb * KC + c
                        hold((sc_full, i * 16 + (SC["l1x"] + 2 * n - 2)))
                        for t, kx in ((CH, KXH), (CL, KXL)):
                            keys = f32(t[:, c, bass.ds(i * 256 + bb * S, S)])
                            pool.tensor_tensor(kx[:, n % 2, :].rearrange("p (j s) -> p j s", j=GQ),
                                               keys.unsqueeze(1).broadcast_to((P, GQ, S)),
                                               BM[:].unsqueeze(2).broadcast_to((P, GQ, S)),
                                               ALU.mult).then_inc(kx_ready, 1)

        @block.tensor
        def _(pe):
            def mm3(out, w, x, first=True, last=True):
                (wh, wl), (xh, xl) = w, x
                pe.matmul(out, wh, xh, start=first, stop=False)
                pe.matmul(out, wh, xl, start=False, stop=False)
                return pe.matmul(out, wl, xh, start=False, stop=last)

            def pj_free(n):
                if not isinstance(n, int) or n >= 2:
                    pe.wait_ge(pj_done, n - 1)

            def ou_free(n):
                if not isinstance(n, int) or n >= 2:
                    pe.wait_ge(x_done, n - 1)

            def layer_norm(l):
                for b in range(B):
                    n = PJ[f"ln{l}"] + b
                    pe.wait_ge(ln_x, B * l + b + 1)
                    pj_free(n)
                    for c in range(KC):
                        last = pe.transpose(pj[n % 2][:, c * P:(c + 1) * P], PR[:, b % 2, c * P:(c + 1) * P], IDN[:])
                    last.then_inc(pj_full, 1)
                pe.wait_ge(pj_done, PJ[f"ln{l}"] + B)

            def project(fill, w, x, width=512):
                n, bank = fill
                pj_free(n)
                for c in range(KC):
                    last = mm3(pj[bank][:, 0:width], w(c), x(c), c == 0, c == KC - 1)
                last.then_inc(pj_full, 1)

            def both(ts, f):
                return tuple(f(t) for t in ts)

            XT, C, W, A = (XTH, XTL), (CH, CL), (WH, WL), (AH, AL)

            def wide(x, hf):
                return lambda c: both(x, lambda t: t[:, c, hf * HALF:(hf + 1) * HALF])

            def rows(x, b):
                return lambda c: both(x, lambda t: t[:, c, b * S:(b + 1) * S])

            def wcols(s, j, cols=256, width=P):
                return lambda c: both(W, lambda t: wslot(t, s, cols)[:, c, j * width:(j + 1) * width])

            def wrows(s):
                return lambda c: both(W, lambda t: wpair(t, s, 512)[:, c, :])

            def ready(s, k):
                pe.wait_ge(w_ready[s], k + 1)

            pe.wait_ge(consts_in, 16 * len(CONSTS))
            layer_norm(0)
            ready(0, 0)
            for hf in range(2):
                for j in range(2):
                    project(nth(PJ["taylor"], 0, 0, 2 * hf + j), wcols(0, j), wide(XT, hf))
            for s in range(1, NSLOT):
                ready(s, 0)
            for hf in range(2):
                pe.wait_ge(ta_lo, (hf + 1) * TAYLOR)
                for b in range(HB):
                    n, bank = nth(OU["taylor"], 0, 0, hf * HB + b)
                    ou_free(n)
                    for m in range(TAYLOR):
                        w = both(W, lambda t: t[:, 1 + m // 2, (m % 2) * 512:(m % 2 + 1) * 512])
                        x = both(A, lambda t: grp(t, m)[:, b * S:(b + 1) * S])
                        last = mm3(ou[bank][:], x, w, m == 0, m == TAYLOR - 1)
                    last.then_inc(ou_full, 1)

            def ffn_half(now, before):
                for kind, n in FFN_STEPS:
                    if kind == "F" and now:
                        i, hf = now
                        s, j = n % 2, n // 2
                        if hf == 0 and j == 0:
                            ready(s, i + SLOT["ffn"][s])
                        project(nth(PJ["ffn"], i, 8, hf * 4 + n), wcols(s, j), wide(XT, hf))
                    if kind == "O" and before:
                        i, hf = before
                        m, bank = nth(OU["ffn"], i, B, hf * HB + n)
                        if n == 0:
                            if hf == 0:
                                ready(2, i + SLOT["ffn"][2])
                            pe.wait_ge(ff_lo, i * 4 + (2 * hf + 2))
                        ou_free(m)
                        for j in range(2):
                            last = mm3(ou[bank][:], both(A, lambda t: grp(t, 2 * hf + j)[:, n * S:(n + 1) * S]),
                                       wcols(2, 0, 512, 512)(j), j == 0, j == 1)
                        last.then_inc(ou_full, 1)

            halves(pe, FG, ffn_half)

            layer_norm(1)
            pe.wait_ge(c_ready, KC)

            def l0x_half(now, before):
                for kind, n in L0X_STEPS:
                    if kind in "FS" and now:
                        i, hf = now
                    elif kind in "TVO" and before:
                        i, hf = before
                        t = i * B + (hf * HB + n)
                    else:
                        continue
                    if kind == "F" and n < 4:
                        s, x = ((0, XT), (1, C))[n // 2]
                        if hf == 0 and n % 2 == 0:
                            ready(s, i + SLOT["l0x"][s])
                        project(nth(PJ["l0x"], i, 16, hf * 8 + n), wcols(s, n % 2), wide(x, hf))
                    elif kind == "F":
                        if hf == 0 and n == 4:
                            ready(2, i + SLOT["l0x"][2])
                        project(nth(PJ["l0x"], i, 16, hf * 8 + n), rows(C, hf * HB + n - 4), wcols(2, 0, 256, 256), 256)
                    elif kind == "S":
                        pe.wait_ge(pj_done, i * 16 + (PJ["l0x"] + hf * 8 + 4))
                        pe.wait_ge(sc_done, i * B + (hf * HB + 2))
                        for j in range(HB):
                            for h in range(2):
                                last = mm3(score(j)[:, h * S:(h + 1) * S],
                                           both(A, lambda t: qk(t, 0, h)[:, j * S:(j + 1) * S]),
                                           both(A, lambda t: qk(t, 1, h)[:, j * S:(j + 1) * S]))
                            last.then_inc(sc_full, 1)
                    elif kind == "T":
                        pe.wait_ge(sx_pn, t + 1)
                        pe.wait_ge(tp_done, t + 2)
                        for h in range(2):
                            last = pe.transpose(turned_probs(n)[:, h * S:(h + 1) * S],
                                                part(PR, n)[:, h * S:(h + 1) * S], IDN[:])
                        last.then_inc(tp_full, 1)
                    elif kind == "V":
                        if n == 0:
                            pe.wait_ge(pj_done, i * 16 + (PJ["l0x"] + hf * 8 + 8))
                        pe.wait_ge(tp_done, t + 3)
                        pe.wait_ge(pv_done, t + 1)
                        for h in range(2):
                            last = mm3(pv[:, h * S:(h + 1) * S],
                                       both(A, lambda t: vt(t, n)[:, h * S:(h + 1) * S]),
                                       both(A, lambda t: tile_a(t)[:, h * S:(h + 1) * S]))
                        last.then_inc(pv_full, 1)
                    else:
                        m, bank = nth(OU["l0x"], i, B, hf * HB + n)
                        if hf == 0 and n == 0:
                            ready(3, i + SLOT["l0x"][3])
                        pe.wait_ge(pv_done, t + 2)
                        ou_free(m)
                        for h in range(2):
                            last = mm3(ou[bank][:], both(A, lambda t: tile_b(t)[:, h * S:(h + 1) * S]),
                                       wcols(3, 0, 512, 512)(h), h == 0, h == 1)
                        last.then_inc(ou_full, 1)

            halves(pe, HG, l0x_half)

            layer_norm(2)
            for s in range(2):
                ready(s, SLOT["l0f"][s])
            for b in range(B):
                n, bank = nth(OU["l0f"], 0, 0, b)
                ou_free(n)
                for c in range(KC):
                    last = mm3(ou[bank][:], rows(XT, b)(c), wrows(0)(c), c == 0, c == KC - 1)
                last.then_inc(ou_full, 1)
            pe.wait_ge(lf_sum, 3)
            for c in range(KC):
                last = pe.matmul(sc[0][:, 0:B], LQ[:, c, :], XM3[:, c, :], start=c == 0, stop=c == KC - 1)
            last.then_inc(lf_pe, 1)
            pe.wait_ge(lf_v, 1)
            pe.matmul(sc[1][0:B, 0:E], LQT[:], KEYS[:], start=True, stop=True).then_inc(lf_pe, 1)
            pe.wait_ge(lf_v, 5)
            pe.transpose(sc[0][0:E, 0:B], LCO[:], IDN[0:B, 0:B]).then_inc(lf_pe, 1)
            pe.wait_ge(lf_v, 6)
            for c in range(KC):
                last = pe.matmul(sc[1][:, c * B:(c + 1) * B], SEL[:, c, :], LCT[:], start=True, stop=True)
            last.then_inc(lf_pe, 1)
            for s in (2, 3, 4):
                ready(s, SLOT["l0f"][s])
            for hf in range(2):
                for e in range(KC):
                    w = lambda c: both(W, lambda t: wpair(t, 2, 512)[:, c, e * P:(e + 1) * P])
                    project(nth(PJ["l0f"], 0, 0, hf * 4 + e), w, wide(XT, hf))
                pe.wait_ge(lf_lo, 4 * hf + 4)
                if hf == 0:
                    ready(0, SLOT["l0f_up"])
                for b in range(HB):
                    n, bank = nth(OU["l0f"], 0, 0, B + hf * HB + b)
                    ou_free(n)
                    for e in range(KC):
                        s = 4 if e < 2 else 0
                        last = mm3(ou[bank][:], both(A, lambda t: grp(t, e)[:, b * S:(b + 1) * S]),
                                   wcols(s, 0, 512, 512)(e % 2), e == 0, e == KC - 1)
                    last.then_inc(ou_full, 1)

            layer_norm(3)

            def l1a_half(now, before):
                for kind, n in L1A_STEPS:
                    if kind in "FS" and now:
                        i, hf = now
                    elif kind in "VO" and before:
                        i, hf = before
                        t = i * B + (hf * HB + n)
                    else:
                        continue
                    if kind == "F" and n < 6:
                        s = (0, 1, 3)[n // 2]
                        if hf == 0 and n % 2 == 0:
                            ready(s, i + SLOT["l1a"][s])
                        project(nth(PJ["l1a"], i, 20, hf * 10 + n), wcols(s, n % 2), wide(XT, hf))
                    elif kind == "F":
                        if hf == 0 and n == 6:
                            ready(2, i + SLOT["l1a"][2])
                        project(nth(PJ["l1a"], i, 20, hf * 10 + n), rows(XT, hf * HB + n - 6), wcols(2, 0, 256, 256), 256)
                    elif kind == "S":
                        pe.wait_ge(la_lo, i * 16 + (hf * 8 + 6))
                        pe.wait_ge(sc_done, i * B + (SC["l1a"] + hf * HB + 2))
                        for j in range(HB):
                            for h in range(2):
                                last = mm3(score(j)[:, h * S:(h + 1) * S],
                                           both(A, lambda t: qk(t, 1, h)[:, j * S:(j + 1) * S]),
                                           both(A, lambda t: qk(t, 0, h)[:, j * S:(j + 1) * S]))
                            last.then_inc(sc_full, 1)
                    elif kind == "V":
                        if n == 0:
                            pe.wait_ge(la_lo, i * 16 + (hf * 8 + 10))
                        pe.wait_ge(la_sdlo, t + 1)
                        pe.wait_ge(pv_done, t + (PV["l1a"] + 1))
                        for h in range(2):
                            last = mm3(pv[:, h * S:(h + 1) * S],
                                       both(A, lambda t: vt(t, n)[:, h * S:(h + 1) * S]),
                                       both(A, lambda t: tile_a(t, n % 2)[:, h * S:(h + 1) * S]))
                        last.then_inc(pv_full, 1)
                    else:
                        m, bank = nth(OU["l1a"], i, B, hf * HB + n)
                        if hf == 0 and n == 0:
                            ready(4, i + SLOT["l1a"][4])
                        pe.wait_ge(la_gflo, t + 1)
                        ou_free(m)
                        for h in range(2):
                            last = mm3(ou[bank][:], both(A, lambda t: tile_b(t)[:, h * S:(h + 1) * S]),
                                       wcols(4, 0, 512, 512)(h), h == 0, h == 1)
                        last.then_inc(ou_full, 1)

            halves(pe, HG, l1a_half)
            pe.wait_ge(la_sqa, HG * B + 2)
            for b in range(B):
                for h in range(2):
                    last = pe.matmul(tp[:, b:b + 1], SQ[:, b, h * S:(h + 1) * S], ONE[:], start=h == 0, stop=h == 1)
            last.then_inc(la_ss, 1)

            layer_norm(4)
            ready(4, SLOT["l1x"][4])
            pe.wait_ge(c_ready, 2 * KC)
            for b in range(B):
                project(nth(PJ["l1xv"], 0, 0, b), rows(C, b), lambda c: both(W, lambda t: wslot(t, 4, 256)[:, c, 0:P]), P)
            for s in (2, 3):
                ready(s, SLOT["l1x"][s])
            pe.wait_ge(sc_done, 2 + SC["l1x"])
            pe.wait_ge(x_done, OU["l1x"])
            for hf in range(2):
                if hf:
                    pe.wait_ge(kr_lo, 1)
                for m, bank in enumerate((sc[0], sc[1], ou[0], ou[1])):
                    for c in range(KC):
                        w = both(W, lambda t: wpair(t, 2, 512)[:, c, m * P:(m + 1) * P])
                        last = mm3(bank[:], w, wide(C, hf)(c), c == 0, c == KC - 1)
                last.then_inc(kr_full, 1)
            for s in (0, 1):
                ready(s, SLOT["l1x"][s])
            with pe.Fori(0, 4) as i:
                for c4 in range(KC):
                    w = lambda c: both(W, lambda t: wpair(t, 0, 512)[:, c, c4 * P:(c4 + 1) * P])
                    x = lambda c: both(XT, lambda t: t[:, c, bass.ds(i * 256, 256)])
                    project(nth(PJ["l1x"], i, 6, c4), w, x, 256)
                pe.wait_ge(pj_done, i * 6 + (PJ["l1x"] + 4))

                def scores(m):
                    bb, c, u = m // 8, m // 2 % 4, m % 2
                    n, bank = nth(SC["l1x"], i, 16, m)
                    if u == 0:
                        pe.wait_ge(kx_ready, i * 16 + (2 * (m // 2) + 2))
                    pe.wait_ge(lx_exp, i * 16 + (m + 1))
                    r = slice(64 * u, 64 * u + 64)
                    mm3(sc[bank][:], both(A, lambda t: q1(t, c)[r, bb * S:(bb + 1) * S]),
                        both((KXH, KXL), lambda t: t[r, (m // 2) % 2, :])).then_inc(sc_full, 1)

                def transposes(m):
                    n, bank = nth(TP["l1x"], i, 16, m)
                    pe.wait_ge(lx_exp, i * 16 + (m + 3))
                    pe.wait_ge(tp_done, n + 2)
                    for h in range(GQ):
                        last = pe.transpose(tp[:, h * S:(h + 1) * S], PR[:, bank, h * S:(h + 1) * S], IDN[:])
                    last.then_inc(tp_full, 1)

                def values(m):
                    bb, c, u = m // 8, m // 2 % 4, m % 2
                    n, bank = nth(TP["l1x"], i, 16, m)
                    pe.wait_ge(tp_done, n + 3)
                    if u == 0:
                        pe.wait_ge(pv_done, i * 8 + (PV["l1x"] + m // 2 + 1))
                    at = V1 + (2 * c + u) * VW
                    for h in range(GQ):
                        col = (GQ * u + h) * VW
                        last = mm3(pv[:, col:col + VW],
                                   both(A, lambda t: t[:, PT1 + bank * 512 + h * S:PT1 + bank * 512 + (h + 1) * S]),
                                   both(A, lambda t: t[:, bass.ds(i * (2 * KVH * VW) + (at + bb * KVH * VW), VW)]))
                    last.then_inc(pv_full, 1)

                def turn(bb):
                    n, bank = nth(PJ["l1x"], i, 6, 4 + bb)
                    pe.wait_ge(pv_done, i * 8 + (PV["l1x"] + 4 * bb + 5))
                    pj_free(n)
                    for c in range(KC):
                        last = pe.transpose(pj[bank][:, c * P:(c + 1) * P], ONT[:, bb, c * P:(c + 1) * P], IDN[:])
                    last.then_inc(pj_full, 1)

                def output(bb):
                    n, bank = nth(OU["l1x"], i, 2, bb)
                    pe.wait_ge(pj_done, i * 6 + (PJ["l1x"] + 5 + bb))
                    ou_free(n)
                    for c in range(KC):
                        last = mm3(ou[bank][:], both(A, lambda t: t[:, ON1 + c * P:ON1 + (c + 1) * P]),
                                   wrows(2)(c), c == 0, c == KC - 1)
                    last.then_inc(ou_full, 1)

                scores(0)
                for m in range(16):
                    if m < 15:
                        scores(m + 1)
                    transposes(m)
                    if m:
                        values(m - 1)
                    if m == 10:
                        turn(0)
                    if m == 12:
                        pe.wait_ge(w_ready[3], SLOT["l1x_o"][1] + 1)
                        output(0)
                values(15)
                turn(1)
                output(1)

            pe.wait_ge(w_deq, 1)
            for c in range(KC):
                n, bank = nth(PJ["l1f"], 0, 0, c)
                pj_free(n)
                for o in range(KC):
                    last = pe.transpose(pj[bank][:, o * P:(o + 1) * P], RAW[:, 0:2, :].rearrange("p s (o i) -> p (s o) i", i=512)[:, o, c * P:(c + 1) * P], IDN[:])
                last.then_inc(pj_full, 1)
            layer_norm(5)
            for b in range(B):
                n, bank = nth(OU["l1f"], 0, 0, b)
                ou_free(n)
                for c in range(KC):
                    last = mm3(ou[bank][:], rows(XT, b)(c), wrows(0)(c), c == 0, c == KC - 1)
                last.then_inc(ou_full, 1)

        @block.scalar
        def _(act):
            def hi(fill, dst, src, scale=1.0):
                act.wait_ge(pj_full, fill[0] + 1)
                act.activation(dst, src, ACT.Copy, scale=scale).then_inc(pj_hi, 1)

            def layer_norm(l):
                act.wait_ge(ln_var, l + 1)
                act.activation(SD[:], VE[:], ACT.Sqrt).then_inc(ln_std, 1)
                for b in range(B):
                    n, bank = nth(PJ[f"ln{l}"], 0, 0, b)
                    hi((n, bank), XTH[:, :, b * S:(b + 1) * S], pj[bank][:].rearrange("p (c s) -> p c s", c=KC))

            act.sem_inc(lx_exp, 2)
            act.sem_inc(la_sq, 1)
            act.wait_ge(consts_in, 16 * len(CONSTS))
            act.activation(CE[:], DC[:], ACT.Exp, scale=-1.0).then_inc(ce_ready, 1)
            layer_norm(0)
            for hf in range(2):
                if hf:
                    act.wait_ge(ou_full, OU["taylor"] + HB)
                for m in range(TAYLOR):
                    act.wait_ge(ta_t, hf * TAYLOR + m + 1)
                    act.activation(grp(AH, m), TY[3 * (m % 2)], ACT.Copy).then_inc(ta_hi, 1)

            def ffn_half(now, before):
                for kind, f in FFN_STEPS:
                    if kind == "F" and now:
                        i, hf = now
                        j = f // 2
                        n, bank = nth(PJ["ffn"], i, 8, hf * 4 + f)
                        if f % 2 == 0:
                            act.wait_ge(pj_full, n + 1)
                            act.wait_ge(pj_done, n)
                            act.activation(SG, pj[bank][:], ACT.Sigmoid).then_inc(ff_sg, 1)
                        else:
                            act.wait_ge(pj_done, n + 1)
                            if j == 0:
                                act.wait_ge(ou_full, i * B + (OU["ffn"] + hf * HB - HB))
                            act.activation(grp(AH, 2 * hf + j), HF[j], ACT.Copy).then_inc(ff_hi, 1)

            halves(act, FG, ffn_half)

            layer_norm(1)

            def l0x_half(now, before):
                for kind, n in L0X_STEPS:
                    if kind in "FS" and now:
                        i, hf = now
                    elif kind in "TV" and before:
                        i, hf = before
                        t = i * B + (hf * HB + n)
                    else:
                        continue

                    def exps(j):
                        act.wait_ge(sx_nm, i * B + (hf * HB + j + 9))
                        for h in range(2):
                            p = part(PR, j)[:, h * S:(h + 1) * S]
                            last = act.activation(p, p, ACT.Exp, bias=NM[:, j, h:h + 1], accum_out=SU[:, j, h:h + 1])
                        last.then_inc(sx_exp, 1)

                    if kind == "F":
                        fill = nth(PJ["l0x"], i, 16, hf * 8 + n)
                        bank = pj[fill[1]]
                        if n < 4:
                            hi(fill, qk(AH, n // 2, n % 2), bank[:], S ** -0.5 if n < 2 else 1.0)
                        else:
                            hi(fill, vt(AH, n - 4), bank[:, 0:256])
                        if n in (5, 6):
                            exps(n - 3)
                    elif kind == "S":
                        exps(0)
                        exps(1)
                    elif kind == "T":
                        act.wait_ge(tp_full, t + 1)
                        act.activation(tile_a(AH), turned_probs(n), ACT.Copy).then_inc(pt_hi, 1)
                    else:
                        act.wait_ge(pv_full, t + 1)
                        act.wait_ge(ou_full, t + OU["l0x"])
                        act.activation(tile_b(AH), pv[:, 0:256], ACT.Copy).then_inc(ct_hi, 1)

            halves(act, HG, l0x_half)

            layer_norm(2)
            act.wait_ge(lf_v, 3)
            act.activation(LS[:], sc[1][0:B, 0:E], ACT.Exp, bias=LSM[:, 1:2], scale=P ** -0.5,
                           accum_out=LSM[:, 2:3]).then_inc(lf_a, 1)
            for hf in range(2):
                if hf:
                    act.wait_ge(ou_full, OU["l0f"] + B + HB)
                for e in range(KC):
                    n, bank = nth(PJ["l0f"], 0, 0, hf * 4 + e)
                    act.wait_ge(pj_done, n + 1)
                    act.activation(grp(AH, e), TY[bank], ACT.Copy).then_inc(lf_hi, 1)

            layer_norm(3)
            act.wait_ge(y_zero, 2)

            def l1a_half(now, before):
                def tile_hi(i, hf, j):
                    t = i * B + (hf * HB + j)
                    act.wait_ge(sc_done, t + (SC["l1a"] + 3))
                    act.wait_ge(pv_full, t + (PV["l1a"] - 1))
                    act.activation(tile_a(AH, j % 2), part(PR, j), ACT.Copy).then_inc(la_sdhi, 1)

                def fill_hi(i, hf, f):
                    x = f if f < 4 else f - 2
                    act.wait_ge(pj_done, i * 20 + (PJ["l1a"] + hf * 10 + f + 1))
                    dst = qk(AH, f // 2, f % 2) if f < 4 else vt(AH, f - 6)
                    act.activation(dst, F[:, x % 2, 0:dst.shape[1]], ACT.Copy).then_inc(la_hi, 1)

                for kind, n in L1A_STEPS:
                    if kind in "FS" and now:
                        i, hf = now
                    elif kind == "V" and before:
                        i, hf = before
                        t = i * B + (hf * HB + n)
                    else:
                        continue
                    if kind == "F":
                        m, bank = nth(PJ["l1a"], i, 20, hf * 10 + n)
                        act.wait_ge(pj_full, m + 1)
                        if n in (4, 5):
                            act.wait_ge(pv_done, i * B + (PV["l1a"] + hf * HB + 1))
                            act.activation(G[:, n - 4, :], pj[bank][:], ACT.Sigmoid).then_inc(la_sg, 1)
                        else:
                            x = n if n < 4 else n - 2
                            act.wait_ge(la_lo, i * 16 + (hf * 8 + x + 1))
                            w = 512 if n < 4 else 256
                            act.activation(F[:, x % 2, 0:w], pj[bank][:, 0:w], ACT.Sigmoid).then_inc(la_sg, 1)
                        if n not in (0, 5, 6):
                            fill_hi(i, hf, n - 1)
                        if n == 9:
                            fill_hi(i, hf, 9)
                    elif kind == "S":
                        tile_hi(i, hf, 0)
                        tile_hi(i, hf, 1)
                    else:
                        bank = n % 2
                        act.wait_ge(pv_full, t + (PV["l1a"] + 1))
                        act.wait_ge(la_sqa, t + 1)
                        act.activation(SQT[bank], pv[:, 0:256], ACT.Square).then_inc(la_sq, 1)
                        act.wait_ge(pv_done, t + (PV["l1a"] + 2))
                        act.wait_ge(ou_full, t + OU["l1a"])
                        act.activation(tile_b(AH), GT[bank], ACT.Copy).then_inc(la_gfhi, 1)
                        if n < 2:
                            tile_hi(i, hf, n + 2)

            halves(act, HG, l1a_half)
            act.wait_ge(la_v, 1)
            act.activation(SSD[:], SS[:], ACT.Sqrt).then_inc(la_a, 1)

            layer_norm(4)
            act.wait_ge(v_ones, 2)
            for b in range(B):
                fill = nth(PJ["l1xv"], 0, 0, b)
                at = V1 + b * KVH * VW
                hi(fill, AH[:, at:at + KVH * VW].rearrange("p (k w) -> p k w", w=VW)[:, :, 0:HD],
                   pj[fill[1]][:, 0:P].rearrange("p (k w) -> p k w", w=HD))
            for hf in range(2):
                act.wait_ge(kr_full, hf + 1)
                for m, bank in enumerate((sc[0], sc[1], ou[0], ou[1])):
                    last = act.activation(CH[:, m, hf * HALF:(hf + 1) * HALF], bank[:], ACT.Copy)
                last.then_inc(kr_hi, 1)
            with act.Fori(0, 4) as i:
                for c in range(KC):
                    fill = nth(PJ["l1x"], i, 6, c)
                    hi(fill, q1(AH, c), pj[fill[1]][:, 0:256])

                def exps(m):
                    n, bank = nth(0, i, 16, m)
                    act.wait_ge(lx_nm, n + 1)
                    for h in range(GQ):
                        last = act.activation(PR[:, bank, h * S:(h + 1) * S], sc[bank][:, h * S:(h + 1) * S], ACT.Exp,
                                              bias=NM[:, bank, h:h + 1], scale=HD ** -0.5)
                    last.then_inc(lx_exp, 1)

                def turned(bb):
                    fill = nth(PJ["l1x"], i, 6, 4 + bb)
                    act.wait_ge(ou_full, i * 2 + (OU["l1x"] + bb))
                    hi(fill, AH[:, ON1:ON1 + 512], pj[fill[1]][:])

                exps(0)
                for m in range(16):
                    n, bank = nth(TP["l1x"], i, 16, m)
                    act.wait_ge(tp_full, n + 1)
                    act.wait_ge(pv_full, i * 16 + (PV["l1x"] + m - 1))
                    act.activation(AH[:, PT1 + bank * 512:PT1 + (bank + 1) * 512], tp[:], ACT.Copy).then_inc(pt_hi, 1)
                    if m < 15:
                        exps(m + 1)
                    if m == 10:
                        turned(0)
                turned(1)

            for c in range(KC):
                fill = nth(PJ["l1f"], 0, 0, c)
                hi(fill, wpair(WH, 0, 512)[:, c, :], pj[fill[1]][:])
            layer_norm(5)

        @block.vector
        def _(dve):
            def lo(fill, hi_at, dst, src, hi_part, scale=None):
                dve.wait_ge(pj_hi, hi_at + 1)
                if scale is None:
                    dve.tensor_tensor(dst, src, f32(hi_part), ALU.subtract).then_inc(pj_done, 1)
                else:
                    dve.scalar_tensor_tensor(dst, src, scale, f32(hi_part), ALU.mult, ALU.subtract).then_inc(pj_done, 1)

            def add_output(n, bank, dst):
                dve.wait_ge(ou_full, n + 1)
                dve.tensor_tensor(dst, dst, ou[bank][:], ALU.add).then_inc(x_done, 1)

            def layer_norm(l):
                if l == 4:
                    dve.wait_ge(la_y, B)
                elif l:
                    dve.wait_ge(x_done, OU[{1: "l0x", 2: "l0f", 3: "l1a", 5: "l1f"}[l]])
                for b in range(B):
                    last = dve.bn_stats(ST[:, b, :], X[:, b, :])
                last.then_inc(ln_stat, 1)
                dve.wait_ge(ln_stat, l + 1)
                for b in range(B):
                    last = dve.bn_aggr(MV[:, b, :], ST[:, b, :])
                last.then_inc(ln_aggr, 1)
                dve.wait_ge(ln_aggr, l + 1)
                dve.tensor_scalar(VE[:], MV[:, :, 1], EPS, None, ALU.add).then_inc(ln_var, 1)
                dve.wait_ge(ln_std, l + 1)
                dve.reciprocal(RS[:], SD[:]).then_inc(ln_rstd, 1)
                dve.wait_ge(ln_rstd, l + 1)

                def turned(b):
                    n, bank = nth(PJ[f"ln{l}"], 0, 0, b)
                    at = (slice(None), slice(None), slice(b * S, (b + 1) * S))
                    lo((n, bank), HI[f"ln{l}"] + b, XTL[at], pj[bank][:].rearrange("p (c s) -> p c s", c=KC), XTH[at])

                for b in range(B):
                    if b >= 2:
                        dve.wait_ge(pj_full, PJ[f"ln{l}"] + b - 1)
                    dve.tensor_scalar(PR[:, b % 2, :], X[:, b, :], MV[:, b, 0:1], RS[:, b:b + 1],
                                      ALU.subtract, ALU.mult).then_inc(ln_x, 1)
                    if b:
                        turned(b - 1)
                turned(B - 1)

            def dequantise():
                steps = [0]

                def step(ins):
                    steps[0] += 1
                    ins.then_inc(dq, 1)
                    dve.wait_ge(dq, steps[0])

                SHR, SHL, AND, OR = ALU.logical_shift_right, ALU.logical_shift_left, ALU.bitwise_and, ALU.bitwise_or
                step(dve.tensor_copy(QI[:], Q3[:].bitcast(U8).rearrange("p o (n k) -> p o n k", k=3)))
                byte = [QI[:, :, :, k] for k in range(3)]
                fields = [((0, 0, 7),), ((0, 3, 7),), ((0, 6, 3), (1, 1, 2)), ((1, 1, 7),), ((1, 4, 7),),
                          ((1, 7, 1), (2, 3, 1)), ((2, 2, 7),), ((2, 5, 7),)]
                dve.wait_ge(w_ready[0], SLOT["l1x"][0] + 1)
                dve.wait_ge(w_ready[1], SLOT["l1x"][1] + 1)
                w = RAW[:, 0:2, :].rearrange("p s (n v) -> p (s n) v", v=8)
                for v, field in enumerate(fields):
                    k, shift, mask = field[0]
                    step(dve.tensor_scalar(QT[:], byte[k], shift, mask, SHR, AND))
                    if len(field) > 1:
                        k, mask, shift = field[1]
                        step(dve.tensor_scalar(QU[:], byte[k], mask, shift, AND, SHL))
                        step(dve.tensor_tensor(QT[:], QT[:], QU[:], OR))
                    step(dve.tensor_copy(w[:, :, v], QT[:].rearrange("p o n -> p (o n)")))
                norm = QN[:].rearrange("p o g -> p (o g)")
                step(dve.tensor_tensor(QN2[:], norm, norm, ALU.add))
                wf = RAW[:, 0:2, :].rearrange("p s n -> p (s n)")
                wg = RAW[:, 0:2, :].rearrange("p s (g n) -> p (s g) n", n=32)
                step(dve.tensor_scalar(wf, wf, 1.0 / 7.0, None, ALU.mult))
                step(dve.tensor_tensor(wg, wg, QN2[:].unsqueeze(2).broadcast_to((P, 64, 32)), ALU.mult))
                dve.tensor_tensor(wg, wg, norm.unsqueeze(2).broadcast_to((P, 64, 32)), ALU.subtract).then_inc(w_deq, 1)

            dve.sem_inc(sc_done, 2)
            dve.sem_inc(tp_done, 2)
            dve.sem_inc(pv_done, 1)
            dve.sem_inc(sx_nm, B)
            dve.sem_inc(la_lo, 2)
            dve.sem_inc(la_sqa, 2)
            dve.wait_ge(x_in, 32)

            layer_norm(0)
            for hf in range(2):
                up, delta, keep = TY[0], TY[1], TY[2]
                n0, bank0 = nth(PJ["taylor"], 0, 0, 2 * hf)
                dve.wait_ge(pj_full, n0 + 1)
                if hf:
                    dve.wait_ge(ta_lo, TAYLOR)
                dve.tensor_copy(up, pj[bank0][:]).then_inc(ta_t, 1)
                dve.wait_ge(pj_full, n0 + 2)
                dve.wait_ge(ta_t, hf * TAYLOR + 1)
                dve.tensor_scalar(delta, pj[1 - bank0][:], LP[:], None, ALU.subtract).then_inc(ta_d, 1)
                dve.wait_ge(ta_d, hf + 1)
                dve.tensor_scalar(keep, delta, -2.5, None, ALU.is_ge).then_inc(pj_done, 1)
                dve.wait_ge(pj_done, n0 + 1)
                dve.scalar_tensor_tensor(keep, delta, 2.5, keep, ALU.is_le, ALU.mult).then_inc(pj_done, 1)
                for m in range(TAYLOR):
                    if m + 1 < TAYLOR:
                        src, dst = TY[3 * (m % 2)], TY[3 * ((m + 1) % 2)]
                        dve.wait_ge(ta_t, hf * TAYLOR + m + 1)
                        if hf * TAYLOR + m:
                            dve.wait_ge(ta_lo, hf * TAYLOR + m)
                        if m + 1 == 5:
                            dve.tensor_tensor(dst, src, delta, ALU.mult).then_inc(ta_k, 1)
                            dve.wait_ge(ta_k, hf + 1)
                            dve.tensor_tensor(dst, dst, keep, ALU.mult).then_inc(ta_t, 1)
                        else:
                            dve.tensor_tensor(dst, src, delta, ALU.mult).then_inc(ta_t, 1)
                    dve.wait_ge(ta_hi, hf * TAYLOR + m + 1)
                    dve.tensor_tensor(grp(AL, m), TY[3 * (m % 2)], f32(grp(AH, m)), ALU.subtract).then_inc(ta_lo, 1)
                for b in range(HB):
                    n, bank = nth(OU["taylor"], 0, 0, hf * HB + b)
                    add_output(n, bank, X[:, hf * HB + b, :])

            def ffn_half(now, before):
                def chunk_lo(i, hf, j):
                    dve.wait_ge(ff_hi, i * 4 + (2 * hf + j + 1))
                    g = 2 * hf + j
                    dve.tensor_tensor(grp(AL, g), HF[j], f32(grp(AH, g)), ALU.subtract).then_inc(ff_lo, 1)

                for kind, f in FFN_STEPS:
                    if kind == "F" and now:
                        i, hf = now
                        j = f // 2
                        n, bank = nth(PJ["ffn"], i, 8, hf * 4 + f)
                        if f % 2 == 0:
                            dve.wait_ge(ff_sg, i * 4 + (2 * hf + j + 1))
                            dve.wait_ge(pj_done, n)
                            dve.tensor_tensor(HF[j], pj[bank][:], SG, ALU.mult).then_inc(pj_done, 1)
                            if j:
                                chunk_lo(i, hf, 0)
                        else:
                            dve.wait_ge(pj_full, n + 1)
                            dve.wait_ge(pj_done, n)
                            dve.tensor_tensor(HF[j], HF[j], pj[bank][:], ALU.mult).then_inc(pj_done, 1)
                    if kind == "O" and before:
                        i, hf = before
                        m, bank = nth(OU["ffn"], i, B, hf * HB + f)
                        add_output(m, bank, X[:, hf * HB + f, :])
                if now:
                    chunk_lo(*now, 1)

            halves(dve, FG, ffn_half)

            dve.wait_ge(mask_in, 16)
            dve.tensor_scalar(MF, MI[:].bitcast(U8).rearrange("p b s -> p (b s)"), -1.0, MASKED,
                              ALU.add, ALU.mult).then_inc(m_ready, 1)
            layer_norm(1)

            def l0x_half(now, before):
                def biased_max(i, hf, j):
                    t = i * B + (hf * HB + j)
                    dve.wait_ge(fm_ready[hf], i * 2 + 2)
                    dve.wait_ge(sc_full, i * B + (hf * HB + 2 * (j // 2) + 2))
                    dve.sem_inc(dve_gate, 1)
                    for h in range(2):
                        last = dve.tensor_tensor_reduce(
                            out=part(PR, j)[:, h * S:(h + 1) * S], in0=score(j)[:, h * S:(h + 1) * S],
                            in1=FS[:, hf, j, h, :], scale=1.0, scalar=-3e38, op0=ALU.add, op1=ALU.max,
                            accum_out=MX[:, j, h:h + 1])
                    last.then_inc(sc_done, 1)
                    dve.wait_ge(sc_done, t + 3)
                    dve.tensor_scalar(NM[:, j, 0:2], MX[:, j, 0:2], -1.0, MASKED / 10,
                                      ALU.mult, ALU.min).then_inc(sx_nm, 1)

                def normalise(i, hf, j):
                    t = i * B + (hf * HB + j)
                    dve.wait_ge(sx_exp, t + 1)
                    dve.tensor_scalar(SM[:], SU[:, j, :], 1e-30, None, ALU.max).then_inc(sx_sm, 1)
                    dve.wait_ge(sx_sm, t + 1)
                    dve.reciprocal(RC[:, 0:2], SM[:]).then_inc(sx_rc, 1)
                    dve.wait_ge(sx_rc, t + 1)
                    p = part(PR, j).rearrange("p (h s) -> p h s", h=2)
                    dve.tensor_tensor(p, p, RC[:, 0:2].unsqueeze(2).broadcast_to((P, 2, S)), ALU.mult).then_inc(sx_pn, 1)

                for kind, n in L0X_STEPS:
                    if kind in "FS" and now:
                        i, hf = now
                    elif kind in "TVO" and before:
                        i, hf = before
                        t = i * B + (hf * HB + n)
                    else:
                        continue
                    if kind == "F":
                        fill = nth(PJ["l0x"], i, 16, hf * 8 + n)
                        at = i * 16 + (HI["l0x"] + hf * 8 + n)
                        bank = pj[fill[1]]
                        if n < 4:
                            lo(fill, at, qk(AL, n // 2, n % 2), bank[:], qk(AH, n // 2, n % 2), S ** -0.5 if n < 2 else None)
                        else:
                            lo(fill, at, vt(AL, n - 4), bank[:, 0:256], vt(AH, n - 4))
                        if n in (5, 6):
                            biased_max(i, hf, n - 3)
                    elif kind == "S":
                        biased_max(i, hf, 0)
                        biased_max(i, hf, 1)
                        normalise(i, hf, 0)
                    elif kind == "T":
                        dve.wait_ge(pt_hi, t + 1)
                        dve.tensor_tensor(tile_a(AL), turned_probs(n), f32(tile_a(AH)), ALU.subtract).then_inc(tp_done, 1)
                        if n + 1 < HB:
                            normalise(i, hf, n + 1)
                    elif kind == "V":
                        dve.wait_ge(ct_hi, t + 1)
                        dve.tensor_tensor(tile_b(AL), pv[:, 0:256], f32(tile_b(AH)), ALU.subtract).then_inc(pv_done, 1)
                    else:
                        m, bank = nth(OU["l0x"], i, B, hf * HB + n)
                        add_output(m, bank, X[:, hf * HB + n, :])

            halves(dve, HG, l0x_half)

            layer_norm(2)
            dve.wait_ge(pj_done, PJ["ln2"] + B)
            for dst, t in ((XM, XTH), (XM2, XTL)):
                dve.tensor_reduce(dst[:].rearrange("p c b -> p (c b)"),
                                  f32(t[:]).rearrange("p c (b s) -> p (c b) s", b=B), axis=AX.X, op=ALU.add).then_inc(lf_sum, 1)
            dve.wait_ge(lf_sum, 2)
            dve.tensor_tensor(XM3[:], XM[:], XM2[:], ALU.add).then_inc(lf_sum, 1)
            for b in range(B):
                n, bank = nth(OU["l0f"], 0, 0, b)
                add_output(n, bank, X[:, b, :])
            dve.wait_ge(lf_pe, 1)
            dve.tensor_scalar(LQT[:], sc[0][:, 0:B], 1.0 / S, None, ALU.mult).then_inc(lf_v, 1)
            dve.wait_ge(lf_pe, 2)
            dve.tensor_reduce(LSM[:, 0:1], sc[1][0:B, 0:E], axis=AX.X, op=ALU.max).then_inc(lf_v, 1)
            dve.wait_ge(lf_v, 2)
            dve.tensor_scalar(LSM[:, 1:2], LSM[:, 0:1], -P ** -0.5, None, ALU.mult).then_inc(lf_v, 1)
            dve.wait_ge(lf_a, 1)
            dve.reciprocal(LSM[:, 3:4], LSM[:, 2:3]).then_inc(lf_v, 1)
            dve.wait_ge(lf_v, 4)
            dve.tensor_scalar(LCO[:], LS[:], LSM[:, 3:4], None, ALU.mult).then_inc(lf_v, 1)
            dve.wait_ge(lf_pe, 3)
            dve.tensor_copy(LCT[:], sc[0][0:E, 0:B]).then_inc(lf_v, 1)
            dve.wait_ge(lf_pe, 4)
            dve.tensor_copy(LCR[:].rearrange("p c b -> p (c b)"), sc[1][:, 0:KC * B]).then_inc(lf_v, 1)
            dve.wait_ge(lf_v, 7)
            for hf in range(2):
                for e in range(KC):
                    n, bank = nth(PJ["l0f"], 0, 0, hf * 4 + e)
                    dve.wait_ge(pj_full, n + 1)
                    dve.tensor_tensor(TY[bank].rearrange("p (b s) -> p b s", b=HB),
                                      pj[bank][:].rearrange("p (b s) -> p b s", b=HB),
                                      LCR[:, e, hf * HB:(hf + 1) * HB].unsqueeze(2).broadcast_to((P, HB, S)),
                                      ALU.mult).then_inc(pj_done, 1)
                    dve.wait_ge(lf_hi, hf * 4 + e + 1)
                    dve.tensor_tensor(grp(AL, e), TY[bank], f32(grp(AH, e)), ALU.subtract).then_inc(lf_lo, 1)
                for b in range(HB):
                    n, bank = nth(OU["l0f"], 0, 0, B + hf * HB + b)
                    add_output(n, bank, X[:, hf * HB + b, :])

            layer_norm(3)
            dve.wait_ge(y_zero, 2)

            def l1a_half(now, before):
                def fill_lo(i, hf, f):
                    x = f if f < 4 else f - 2
                    at = (lambda t: qk(t, f // 2, f % 2)) if f < 4 else (lambda t: vt(t, f - 6))
                    dve.wait_ge(la_hi, i * 16 + (hf * 8 + x + 1))
                    dve.tensor_tensor(at(AL), F[:, x % 2, 0:at(AL).shape[1]], f32(at(AH)), ALU.subtract).then_inc(la_lo, 1)

                def decayed(i, hf, j):
                    t = i * B + (hf * HB + j)
                    if hf == 0 and j == 0:
                        dve.wait_ge(dt_in, i * 16 + 16)
                    dve.wait_ge(sc_full, i * B + (SC["l1a"] + hf * HB + 2 * (j // 2) + 2))
                    dve.tensor_tensor(part(PR, j), score(j), DT[:], ALU.mult).then_inc(sc_done, 1)

                def tile_lo(i, hf, j):
                    t = i * B + (hf * HB + j)
                    dve.wait_ge(la_sdhi, t + 1)
                    dve.tensor_tensor(tile_a(AL, j % 2), part(PR, j), f32(tile_a(AH, j % 2)),
                                      ALU.subtract).then_inc(la_sdlo, 1)

                for kind, n in L1A_STEPS:
                    if kind in "FS" and now:
                        i, hf = now
                    elif kind in "VO" and before:
                        i, hf = before
                        t = i * B + (hf * HB + n)
                    else:
                        continue
                    if kind == "F":
                        m, bank = nth(PJ["l1a"], i, 20, hf * 10 + n)
                        dve.wait_ge(la_sg, m + (1 - PJ["l1a"]))
                        if n in (4, 5):
                            g = G[:, n - 4, :]
                            dve.tensor_scalar(g, g, NW[:, bass.ds(i * 2 + (n - 4), 1)], None, ALU.mult).then_inc(pj_done, 1)
                        else:
                            x = n if n < 4 else n - 2
                            w = 512 if n < 4 else 256
                            dve.tensor_tensor(F[:, x % 2, 0:w], F[:, x % 2, 0:w], pj[bank][:, 0:w],
                                              ALU.mult).then_inc(pj_done, 1)
                        if n not in (0, 5, 6):
                            fill_lo(i, hf, n - 1)
                        if n in (6, 7):
                            tile_lo(i, hf, n - 6)
                            decayed(i, hf, n - 4)
                        if n == 9:
                            fill_lo(i, hf, 9)
                    elif kind == "S":
                        decayed(i, hf, 0)
                        decayed(i, hf, 1)
                    elif kind == "V":
                        bank, b = n % 2, hf * HB + n
                        dve.wait_ge(la_sq, t + 2)
                        dve.tensor_tensor(GT[bank].rearrange("p (h s) -> p h s", h=2),
                                          pv[:, 0:256].rearrange("p (h s) -> p h s", h=2),
                                          G[:, :, n * S:(n + 1) * S], ALU.mult).then_inc(pv_done, 1)
                        dve.tensor_tensor(SQ[:, b, :], SQ[:, b, :], SQT[bank], ALU.add).then_inc(la_sqa, 1)
                        dve.wait_ge(la_gfhi, t + 1)
                        dve.tensor_tensor(tile_b(AL), GT[bank], f32(tile_b(AH)), ALU.subtract).then_inc(la_gflo, 1)
                        if n < 2:
                            tile_lo(i, hf, n + 2)
                    else:
                        m, bank = nth(OU["l1a"], i, B, hf * HB + n)
                        add_output(m, bank, Y[:, hf * HB + n, :])

            halves(dve, HG, l1a_half)
            dve.wait_ge(la_ss, 1)
            dve.tensor_scalar(SS[:], tp[:, 0:B], 1.0 / (2 * HG * P), EPS, ALU.mult, ALU.add).then_inc(la_v, 1)
            dve.wait_ge(la_a, 1)
            dve.reciprocal(YR[:], SSD[:]).then_inc(la_v, 1)
            dve.wait_ge(la_v, 2)
            for b in range(B):
                dve.scalar_tensor_tensor(X[:, b, :], Y[:, b, :], YR[:, b:b + 1], X[:, b, :],
                                         ALU.mult, ALU.add).then_inc(la_y, 1)

            dve.wait_ge(la_y, B)
            dve.memset(f32(AH[:, V1:PT1]), 1.0).then_inc(v_ones, 1)
            dve.memset(f32(AL[:, V1:PT1]), 0.0).then_inc(v_ones, 1)
            layer_norm(4)
            dve.wait_ge(v_ones, 2)
            for b in range(B):
                fill = nth(PJ["l1xv"], 0, 0, b)
                at = V1 + b * KVH * VW
                vcols = lambda t: t[:, at:at + KVH * VW].rearrange("p (k w) -> p k w", w=VW)[:, :, 0:HD]
                lo(fill, HI["l1xv"] + b, vcols(AL), pj[fill[1]][:, 0:P].rearrange("p (k w) -> p k w", w=HD), vcols(AH))
            dequantise()
            for hf in range(2):
                dve.wait_ge(kr_hi, hf + 1)
                at = slice(hf * HALF, (hf + 1) * HALF)
                for m, bank in enumerate((sc[0], sc[1], ou[0], ou[1])):
                    last = dve.tensor_tensor(CL[:, m, at], bank[:], f32(CH[:, m, at]), ALU.subtract)
                last.then_inc(kr_lo, 1)
            with dve.Fori(0, 4) as i:
                for c in range(KC):
                    fill = nth(PJ["l1x"], i, 6, c)
                    lo(fill, i * 6 + (HI["l1x"] + c), q1(AL, c), pj[fill[1]][:, 0:256], q1(AH, c))

                def row_max(m):
                    n, bank = nth(SC["l1x"], i, 16, m)
                    dve.wait_ge(sc_full, n + 1)
                    dve.tensor_reduce(MX[:, bank, :], sc[bank][:].rearrange("p (h s) -> p h s", h=GQ),
                                      axis=AX.X, op=ALU.max).then_inc(lx_max, 1)
                    dve.wait_ge(lx_max, i * 16 + (m + 1))
                    dve.tensor_scalar(NM[:, bank, :], MX[:, bank, :], -HD ** -0.5, None, ALU.mult).then_inc(lx_nm, 1)

                def heads(k):
                    out = pv[:, 0:2 * GQ * VW].rearrange("p (h w) -> p h w", w=VW)
                    dve.wait_ge(pv_full, i * 16 + (PV["l1x"] + 2 * k + 2))
                    dve.reciprocal(RC[:], out[:, :, HD]).then_inc(lx_rc, 1)
                    dve.wait_ge(lx_rc, i * 8 + (k + 1))
                    dve.tensor_tensor(ONT[:, k // 4, (k % 4) * P:(k % 4 + 1) * P].rearrange("p (h w) -> p h w", w=HD),
                                      out[:, :, 0:HD], RC[:].unsqueeze(2).broadcast_to((P, 2 * GQ, HD)),
                                      ALU.mult).then_inc(pv_done, 1)

                def turned(bb):
                    fill = nth(PJ["l1x"], i, 6, 4 + bb)
                    lo(fill, i * 6 + (HI["l1x"] + 4 + bb), AL[:, ON1:ON1 + 512], pj[fill[1]][:], AH[:, ON1:ON1 + 512])

                def add(bb):
                    n, bank = nth(OU["l1x"], i, 2, bb)
                    add_output(n, bank, X[:, bass.ds(i * 2 + bb, 1), :].rearrange("p a d -> p (a d)"))

                row_max(0)
                for m in range(16):
                    n, bank = nth(TP["l1x"], i, 16, m)
                    if m < 15:
                        row_max(m + 1)
                    dve.wait_ge(pt_hi, n + 1)
                    at = slice(PT1 + bank * 512, PT1 + (bank + 1) * 512)
                    dve.tensor_tensor(AL[:, at], tp[:], f32(AH[:, at]), ALU.subtract).then_inc(tp_done, 1)
                    if m and m % 2 == 0:
                        heads(m // 2 - 1)
                    if m == 10:
                        turned(0)
                    if m == 13:
                        add(0)
                heads(7)
                turned(1)
                add(1)

            for c in range(KC):
                fill = nth(PJ["l1f"], 0, 0, c)
                lo(fill, HI["l1f"] + c, wpair(WL, 0, 512)[:, c, :], pj[fill[1]][:], wpair(WH, 0, 512)[:, c, :])
            layer_norm(5)
            for b in range(B):
                dve.tensor_tensor(X[:, b, :], X[:, b, :], BIAS[:], ALU.add).then_inc(bias_added, 1)
            for b in range(B):
                n, bank = nth(OU["l1f"], 0, 0, b)
                dve.wait_ge(bias_added, b + 1)
                add_output(n, bank, X[:, b, :])


def arr(a):
    return np.ascontiguousarray(a)


def blocks(w):
    return w.reshape(-1, P, w.shape[-1]).transpose(1, 0, 2)


def kernel(**inputs):
    import concourse.bacc as bacc
    from concourse.bass_utils import run_bass_kernel_spmd as run

    g = {k: np.asarray(v) for k, v in inputs.items()}
    L0, L1 = "L0_attn_", "L1_attn_"
    tw = np.zeros((NSLOT, P, PIECE), np.float32)
    tw[0] = blocks(np.concatenate([g[L0 + "up_w"].T, g[L0 + "gate_w"].T], 1)).reshape(P, PIECE)
    terms = [g[L0 + "local_approx_output"].T] + [g[L0 + "fuse_weight"][:, :, m].T for m in range(6)]
    for m, t in enumerate(terms):
        tw[1 + m // 2, :, (m % 2) * 512:(m % 2 + 1) * 512] = t
    fp = [np.zeros((FPAD, D), np.float32) for _ in range(3)]
    for dst, src in zip(fp, (g[L0 + "ffn_gate_w"], g[L0 + "ffn_up_w"], g[L0 + "ffn_down_w"].T)):
        dst[:src.shape[0]] = src

    def in_cols(w):
        return w.reshape(-1, 256, KC, P).transpose(0, 3, 2, 1).reshape(-1, P, PIECE)

    def out_rows(w):
        return w.reshape(-1, 2, P, 512).transpose(0, 2, 1, 3).reshape(-1, P, PIECE)

    def square(w):
        return blocks(w).reshape(P, 2, PIECE).transpose(1, 0, 2)

    ffn = np.stack([in_cols(fp[0]), in_cols(fp[1]), out_rows(fp[2])], 1)
    X0 = "L0_xattn_"
    l0x = np.stack([in_cols(g[X0 + n].T) for n in ("Wq", "Wk", "Wv")] + [out_rows(g[X0 + "Wo"])], 1)
    F0 = "L0_ffn_"
    l0f = np.concatenate([square(g[F0 + "W_org"].T),
                          square(g[F0 + "lora_down"].transpose(1, 0, 2).reshape(D, E * R)),
                          square(g[F0 + "lora_up"].reshape(E * R, D))])
    qkv = g[L1 + "qkv_w"].reshape(2 * HG, 3, P, D).transpose(1, 0, 2, 3).reshape(3, 2 * HG * P, D)
    l1a = np.stack([in_cols(qkv[n]) for n in range(3)] + [in_cols(g[L1 + "gate_w"]), out_rows(g[L1 + "out_w"].T)], 1)
    X1 = "L1_xattn_"
    wk = np.repeat(g[X1 + "Wk"].reshape(D, KVH, 1, HD), GQ, 2).reshape(D, D)
    wv = np.zeros((D, 256), np.float32)
    wv[:, :P] = g[X1 + "Wv"]
    l1x = np.concatenate([square(g[X1 + "Wq"]), square(wk), blocks(wv).reshape(1, P, PIECE), square(g[X1 + "Wo"])])
    side = g["fside_Bx32xSxS2_0"].reshape(2, HB, HG, 2, S, S).transpose(2, 0, 4, 1, 3, 5).reshape(HG, 2, P, 1024)
    q3 = g["L1_ffn_weight_q3"].reshape(D, 16 * 12).view(np.int32).reshape(4, P, 48).transpose(1, 0, 2)
    q3n = g["L1_ffn_weight_norm"].reshape(4, P, 16).transpose(1, 0, 2)
    slope = (1.0 / 2.0 ** (8.0 / 32)) ** (np.arange(32) + 1.0) * (1.0 - 1 / (32 - 1 + 1e-05) + 1e-05)
    diff = np.arange(S)[None, :] - np.arange(S)[:, None]
    decay = np.where(diff >= 0, np.exp(-slope[:, None, None] * np.maximum(diff, 0)), 0.0).astype(np.float32)
    decay = decay.reshape(HG, 2, P, S).transpose(0, 2, 1, 3).reshape(HG, P, 256)
    experts = (np.arange(E * R)[None, :] // R == np.arange(E)[:, None]).astype(np.float32)
    arrays = dict(
        x=g["x"], ctx_t=g["ctx_4096"].reshape(T, KC, P).transpose(1, 2, 0), side=side,
        mask=g["mask_BxSxS2_bk0"].view(np.int32).transpose(1, 0, 2),
        taylor_w=tw, ffn_w=ffn, l0x_w=l0x, l0f_w=l0f, l1a_w=l1a, l1x_w=l1x,
        identity=np.eye(P, dtype=np.float32), local_point=g[L0 + "local_point"].reshape(P, 1),
        discount=np.broadcast_to(g[L0 + "discount_factor"], (P, 6)),
        bias=np.broadcast_to(g["L1_ffn_bias"], (P, D)), lora_keys=g[F0 + "lora_keys"].T,
        lora_wq=blocks(g[F0 + "Wq"].T), expert_rows=experts.reshape(E, KC, P),
        norm_w=g[L1 + "norm_w"].reshape(2 * HG, P).T, one=np.ones((P, 1), np.float32),
        block_mask=(np.arange(P)[:, None] % 64 // HD == np.arange(GQ)[None, :]).astype(np.float32),
        q3=q3, q3_norm=q3n, decay=decay)
    nc = bacc.Bacc("TRN2", target_bir_lowering=False, num_devices=1)
    sent, aps = {}, {}
    for name, v in arrays.items():
        v = arr(v)
        sent["in_" + name] = v
        aps[name] = nc.dram_tensor("in_" + name, v.shape, mybir.dt.from_np(v.dtype), kind="ExternalInput").ap()
    aps["out"] = nc.dram_tensor("out_x", (B, S, D), FP32, kind="ExternalOutput").ap()
    build(nc, aps)
    r = run(nc, [sent], core_ids=[0])
    return r.results[0]["out_x"]
```

```python
import numpy as np
import concourse.bass as bass
from concourse import mybir
from contextlib import ExitStack

FP32 = mybir.dt.float32
F32R = mybir.dt.float32r
I32 = mybir.dt.int32
U8 = mybir.dt.uint8
ACT = mybir.ActivationFunctionType
ALU = mybir.AluOpType
AX = mybir.AxisListType

P = 128
B, S, D = 8, 128, 512
T = B * S
KC = D // P
HALF = T // 2
HB = B // 2
NSLOT, PIECE = 5, 1024
TAYLOR = 7
FG = 5
FPAD = FG * 256
HG = 16
E, R = 8, 64
KVH, GQ, HD = 8, 4, 16
EPS = 1e-5
MASKED = 1e30

PJ_PER = dict(ln=B, taylor=4, ffn=FG * 8, l0x=HG * 16, l0f=8, l1a=HG * 20, l1xv=4, l1x=4 * KC, l1f=4)
PJ_ORDER = ["ln0", "taylor", "ffn", "ln1", "l0x", "ln2", "l0f", "ln3", "l1a", "ln4", "l1xv", "l1x", "l1f", "ln5"]
OU_PER = dict(taylor=B, ffn=FG * B, l0x=HG * B, l0f=2 * B, l1a=HG * B, l1x=B, l1f=B)
OU_ORDER = ["taylor", "ffn", "l0x", "l0f", "l1a", "l1x", "l1f"]


CONSTS_IN = ["identity", "local_point", "discount", "bias", "lora_keys", "lora_wq", "expert_rows", "norm_w",
             "one", "block_mask", "q3", "q3_norm"]


FFN_STEPS = [("F", 0), ("F", 1), ("O", 0), ("F", 2), ("O", 1), ("F", 3), ("O", 2), ("O", 3)]
L0X_STEPS = [("T", 0), ("F", 0), ("V", 0), ("T", 1), ("F", 1), ("O", 0), ("V", 1), ("T", 2), ("F", 2), ("O", 1),
             ("V", 2), ("T", 3), ("F", 3), ("O", 2), ("V", 3), ("F", 4), ("S", 0), ("O", 3), ("F", 5), ("F", 6),
             ("F", 7)]
L1A_STEPS = [("F", 0), ("V", 0), ("F", 1), ("O", 0), ("V", 1), ("F", 2), ("O", 1), ("V", 2), ("F", 3), ("O", 2),
             ("V", 3), ("F", 4), ("O", 3), ("F", 5), ("S", 0), ("F", 6), ("F", 7), ("F", 8), ("F", 9)]


def halves(engine, groups, half):
    last = groups - 1
    half((0, 0), None)
    with engine.Fori(0, last) as i:
        half((i, 1), (i, 0))
        half((i + 1, 0), (i, 1))
    half((last, 1), (last, 0))
    half(None, (last, 1))


def pairs(engine, pair):
    pair(0, True, False)
    with engine.Fori(1, B // 2 - 1) as i:
        pair(i, False, False)
    pair(B // 2 - 1, False, True)


def starts(order, per):
    at, out = 0, {}
    for name in order:
        out[name] = at
        at += per["ln" if name[:2] == "ln" else name]
    return out


PJ = starts(PJ_ORDER, PJ_PER)
HI = starts(PJ_ORDER, {k: v if k in ("ln", "l0x", "l1x", "l1f") else 2 if k == "l1xv" else 0 for k, v in PJ_PER.items()})
OU = starts(OU_ORDER, OU_PER)
SC = dict(l0x=0, l1a=HG * B, l1x=2 * HG * B)
PV = dict(l0x=0, l1a=HG * B, l1x=2 * HG * B)
TP = dict(l0x=0, l1x=HG * B)
SLOT = dict(
    taylor=[0] * 5,
    ffn=[1, 1, 1],
    l0x=[1 + FG, 1 + FG, 1 + FG, 1],
    l0f=[1 + FG + HG, 1 + FG + HG, 1 + FG + HG, 1 + HG, 1],
    l0f_up=2 + FG + HG,
    l1a=[3 + FG + HG, 2 + FG + HG, 2 + FG + HG, 2 + HG, 2],
    l1x=[3 + FG + 2 * HG, 2 + FG + 2 * HG, 2 + FG + 2 * HG, 2 + 2 * HG, 2 + HG],
    l1x_o=[3 + FG + 2 * HG, 3 + 2 * HG],
)


def build(nc, a):
    ctx = ExitStack()
    with ctx:
        def sb(name, shape, dt=FP32):
            return ctx.enter_context(nc.sbuf_tensor(name, shape, dt))

        def psum(name):
            return ctx.enter_context(nc.psum_tensor(name, [P, 512], FP32))

        def sem(name):
            return ctx.enter_context(nc.semaphore(name))

        RAW = sb("raw", [P, NSLOT, PIECE])
        WH = sb("w_hi", [P, NSLOT, PIECE], F32R)
        WL = sb("w_lo", [P, NSLOT, PIECE], F32R)
        X = sb("x", [P, B, D])
        XTH = sb("xt_hi", [P, KC, T], F32R)
        XTL = sb("xt_lo", [P, KC, T], F32R)
        with ExitStack() as shared:
            Y = shared.enter_context(nc.sbuf_tensor("y", [P, B, D], FP32))
            SQ = shared.enter_context(nc.sbuf_tensor("sumsq", [P, B, 256], FP32))
            G = shared.enter_context(nc.sbuf_tensor("gate", [P, 2, 512], FP32))
            F = shared.enter_context(nc.sbuf_tensor("silu", [P, 2, 512], FP32))
        CH = sb("ctx_hi", [P, KC, T], F32R)
        CL = sb("ctx_lo", [P, KC, T], F32R)
        NA = 3840
        AH = sb("act_hi", [P, NA], F32R)
        AL = sb("act_lo", [P, NA], F32R)
        with ExitStack() as shared:
            FS = shared.enter_context(nc.sbuf_tensor("side", [P, 2, HB, 2, S], FP32))
        KXH = sb("keys_hi", [P, 2, 512], F32R)
        KXL = sb("keys_lo", [P, 2, 512], F32R)
        with ExitStack() as shared:
            M = shared.enter_context(nc.sbuf_tensor("mask_bias", [P, B, S], FP32))
            MI = shared.enter_context(nc.sbuf_tensor("mask_int", [P, B, S // 4], I32))
            QI = shared.enter_context(nc.sbuf_tensor("q3_int", [P, 4, 64, 3], I32))
        VP = sb("values_padded", [P, 2, PIECE], F32R)
        PR = sb("probs", [P, 2, 512])
        DT = sb("decay", [P, 256])
        IDN = sb("identity", [P, P])
        BIAS = sb("bias", [P, D])
        Q3 = sb("q3_packed", [P, 4, 16 * 3], I32)
        QN = sb("q3_norm", [P, 4, 16])
        QT = sb("q3_tmp", [P, 4, 64], I32)
        QU = sb("q3_tmp2", [P, 4, 64], I32)
        QN2 = sb("q3_norm2", [P, 64])
        ST = sb("bn_stats", [P, B, 6])
        MV = sb("bn_mean_var", [P, B, 2])
        VE = sb("var_eps", [P, B])
        SD = sb("std", [P, B])
        RS = sb("rstd", [P, B])
        LP = sb("local_point", [P, 1])
        DC = sb("discount", [P, 6])
        CE = sb("coef_exp", [P, 6])
        MX = sb("row_max", [P, 4, 4])
        NM = sb("neg_max", [P, 4, 4])
        SU = sb("row_sum", [P, 4, 2])
        SM = sb("row_sum_min", [P, 2])
        RC = sb("row_recip", [P, 8])
        KEYS = sb("lora_keys", [P, E])
        LQ = sb("lora_wq", [P, KC, P])
        SEL = sb("expert_rows", [E, KC, P])
        XM = sb("x_sum", [P, KC, B])
        XM2 = sb("x_sum_lo", [P, KC, B])
        XM3 = sb("x_sum_all", [P, KC, B])
        LQT = sb("lora_q", [P, B])
        LS = sb("lora_exp", [B, E])
        LSM = sb("lora_stats", [B, 4])
        LCO = sb("lora_coef", [B, E])
        LCT = sb("lora_coef_t", [E, B])
        LCR = sb("lora_coef_rows", [P, KC, B])
        NW = sb("norm_w", [P, 2 * HG])
        ONE = sb("one", [P, 1])
        BM = sb("block_mask", [P, GQ])
        SS = sb("mean_sq", [P, B])
        SSD = sb("mean_sq_std", [P, B])
        YR = sb("y_scale", [P, B])

        pj = [psum("pj0"), psum("pj1")]
        sc = [psum("sc0"), psum("sc1")]
        tp = psum("tp")
        pv = psum("pv")
        ou = [psum("ou0"), psum("ou1")]

        consts_in, x_in, fs_in, mask_in = sem("consts_in"), sem("x_in"), [sem("fs_in0"), sem("fs_in1")], sem("mask_in")
        dt_in, out_done = sem("dt_in"), sem("out_done")
        w_in = [sem(f"w_in{s}") for s in range(NSLOT)]
        ta_used = sem("ta_used")
        w_hi = [sem(f"w_hi{s}") for s in range(NSLOT)]
        w_ready = [sem(f"w_ready{s}") for s in range(NSLOT)]
        dve_gate = sem("dve_gate")
        c_in, c_hi, c_ready = [sem("c_in0"), sem("c_in1")], sem("c_hi"), sem("c_ready")
        passed = sem("passed")
        ln_stat, ln_aggr, ln_var, ln_std, ln_rstd, ln_x = (sem(n) for n in
            ("ln_stat", "ln_aggr", "ln_var", "ln_std", "ln_rstd", "ln_x"))
        pj_full, pj_hi, pj_done = sem("pj_full"), sem("pj_hi"), sem("pj_done")
        ou_full, x_done = sem("ou_full"), sem("x_done")
        sc_full, sc_done = sem("sc_full"), sem("sc_done")
        tp_full, pt_hi, tp_done = sem("tp_full"), sem("pt_hi"), sem("tp_done")
        pv_full, ct_hi, pv_done = sem("pv_full"), sem("ct_hi"), sem("pv_done")
        ce_ready, ta_d, ta_k, ta_t, ta_hi, ta_lo = (sem(n) for n in
            ("ce_ready", "ta_d", "ta_k", "ta_t", "ta_hi", "ta_lo"))
        ff_sg, ff_hi, ff_lo = (sem(n) for n in ("ff_sg", "ff_hi", "ff_lo"))
        m_ready, fm_ready = sem("m_ready"), [sem("fm_ready0"), sem("fm_ready1")]
        sx_nm, sx_exp, sx_sm, sx_rc, sx_pn = (sem(n) for n in ("sx_nm", "sx_exp", "sx_sm", "sx_rc", "sx_pn"))
        lf_sum, lf_pe, lf_v, lf_a, lf_hi, lf_lo = (sem(n) for n in
            ("lf_sum", "lf_pe", "lf_v", "lf_a", "lf_hi", "lf_lo"))
        y_zero, la_sg, la_hi, la_lo, la_sdhi, la_sdlo, la_sq, la_sqa, la_gfhi, la_gflo = (
            sem(n) for n in ("y_zero", "la_sg", "la_hi", "la_lo", "la_sdhi", "la_sdlo", "la_sq",
                             "la_sqa", "la_gfhi", "la_gflo"))
        la_ss, la_v, la_a, la_y = sem("la_ss"), sem("la_v"), sem("la_a"), sem("la_y")
        pads_zero, pad_ready, on_done, lx_pn = (sem(n) for n in ("pads_zero", "pad_ready", "on_done", "lx_pn"))
        kr_full, kr_hi, kr_lo, kx_ready, lx_max, lx_nm, lx_exp, lx_rc, lx_on = (sem(n) for n in
            ("kr_full", "kr_hi", "kr_lo", "kx_ready", "lx_max", "lx_nm", "lx_exp", "lx_rc", "lx_on"))
        dq, w_deq, bias_added = sem("dq"), sem("w_deq"), sem("bias_added")

        def f32(ap):
            return ap.bitcast(FP32)

        def wslot(t, s, cols):
            return t[:, s, :].rearrange("p (c n) -> p c n", n=cols)

        def wpair(t, s, cols):
            return t[:, s:s + 2, :].rearrange("p s (c n) -> p (s c) n", n=cols)

        def qk(t, which, h):
            return t[:, (2 * which + h) * 512:(2 * which + h + 1) * 512]

        def vt(t, j):
            return t[:, 2048 + j * 256:2048 + (j + 1) * 256]

        def tile_a(t, n=0):
            return t[:, 3072 + n * 256:3328 + n * 256]

        def tile_b(t):
            return t[:, 3584:3840]

        def grp(t, m):
            return t[:, m * 512:(m + 1) * 512]

        def q1(t, c):
            return t[:, c * 256:(c + 1) * 256]

        V1 = 1024
        PT1 = V1 + B * P
        ON1 = PT1 + 1024
        SUMS = SU[:, :, :].rearrange("p a b -> p (a b)")
        PADS = [(WH[:, 4, :], WL[:, 4, :]), (VP[:, 0, :], VP[:, 1, :])]


        FSF = FS[:, :, :, :, :].rearrange("p a b h s -> p (a b h s)")
        TY = [FSF[:, n * 512:(n + 1) * 512] for n in range(4)]
        MF = M[:, :, :].rearrange("p b s -> p (b s)")
        GT = [FSF[:, 0:256], FSF[:, 256:512]]
        SQT = [FSF[:, 512:768], FSF[:, 768:1024]]
        HF = [MF[:, 0:512], MF[:, 512:1024]]
        SG = PR[:, 0, :]

        def part(t, j):
            return t[:, j // 2, (j % 2) * 256:(j % 2 + 1) * 256]

        def score(j):
            return sc[j // 2][:, (j % 2) * 256:(j % 2 + 1) * 256]

        def turned_probs(j):
            return tp[:, (j % 2) * 256:(j % 2 + 1) * 256]

        def nth(base, i, per, j):
            return i * per + (base + j), (base + j) % 2

        taylor_banks = [[ou[0], ou[1], sc[0], sc[1]], [tp, pv, ou[0], ou[1]]]

        key_banks = [[sc[0], sc[1], ou[0], ou[1]], [tp, pv, sc[0], sc[1]]]

        block = ctx.enter_context(nc.Block())
        CONSTS = [IDN[:], LP[:], DC[:], BIAS[:], KEYS[:], LQ[:], SEL[:], NW[:], ONE[:], BM[:], Q3[:], QN[:]]

        @block.sync
        def _(sp):
            def load(s, k, src):
                if not isinstance(k, int) or k > 0:
                    sp.wait_ge(w_ready[s], k)
                sp.dma_start(RAW[:, s, :], src).then_inc(w_in[s], 16)

            def load_ctx(n, c):
                if n or c >= 2:
                    sp.wait_ge(c_ready, KC * n + max(c - 1, 0))
                sp.dma_start(FSF[:, (c % 2) * T:(c % 2 + 1) * T], a["ctx_t"][c]).then_inc(c_in[c % 2], 16)

            for n in range(2):
                sp.dma_start(X[:, n * HB:(n + 1) * HB, :],
                             a["x"][n * HB:(n + 1) * HB].rearrange("b p d -> p b d")).then_inc(x_in, 16)
            for dst, name in zip(CONSTS, CONSTS_IN):
                sp.dma_start(dst, a[name]).then_inc(consts_in, 16)
            for s in range(NSLOT):
                load(s, 0, a["taylor_w"][s])
            sp.dma_start(MI[:], a["mask"]).then_inc(mask_in, 16)
            for s in range(3):
                load(s, SLOT["ffn"][s], a["ffn_w"][0, s])
            sp.wait_ge(ta_lo, 2 * TAYLOR)
            load_ctx(0, 0)
            load_ctx(0, 1)
            with sp.Fori(1, FG) as i:
                for s in range(3):
                    load(s, i + SLOT["ffn"][s], a["ffn_w"][bass.ds(i, 1), s].rearrange("a p n -> (a p) n"))
            load_ctx(0, 2)
            load_ctx(0, 3)
            sp.wait_ge(c_ready, KC)
            with sp.Fori(0, HG) as i:
                for s in range(4):
                    load(s, i + SLOT["l0x"][s], a["l0x_w"][bass.ds(i, 1), s].rearrange("a p n -> (a p) n"))
                for hf in range(2):
                    sp.wait_ge(sx_nm, i * B + (hf + 1) * HB)
                    sp.dma_start(FS[:, hf].rearrange("p b h s -> p (b h s)"),
                                 a["side"][bass.ds(i, 1), hf].rearrange("a p n -> (a p) n")).then_inc(fs_in[hf], 16)
            for s in range(NSLOT):
                load(s, SLOT["l0f"][s], a["l0f_w"][s])
            load(0, SLOT["l0f_up"], a["l0f_w"][NSLOT])
            with sp.Fori(0, HG) as i:
                for s in range(NSLOT):
                    load(s, i + SLOT["l1a"][s], a["l1a_w"][bass.ds(i, 1), s].rearrange("a p n -> (a p) n"))
                sp.wait_ge(sc_done, i * B + 2 + SC["l1a"])
                sp.dma_start(DT[:], a["decay"][bass.ds(i, 1)].rearrange("a p n -> (a p) n")).then_inc(dt_in, 16)
            for s in range(NSLOT):
                load(s, SLOT["l1x"][s], a["l1x_w"][s])
            sp.wait_ge(la_gflo, HG * B)
            for c in range(KC):
                load_ctx(1, c)
            for s in range(2):
                load(2 + s, SLOT["l1x_o"][s], a["l1x_w"][NSLOT + s])
            for b in range(B):
                sp.wait_ge(x_done, OU["l1f"] + b + 1)
                sp.dma_start(a["out"][b], X[:, b, :]).then_inc(out_done, 16)
            sp.wait_ge(out_done, 16 * B)

        @block.gpsimd
        def _(pool):
            def hold(*waits):
                for s, v in waits:
                    pool.wait_ge(s, v)
                pool.sem_inc(passed, 1)

            def split(s, k, free=None):
                pool.wait_ge(w_in[s], k * 16 + 16)
                hold(*([free] if free else []))
                pool.tensor_tensor(WH[:, s, :], RAW[:, s, :], ONE[:].broadcast_to((P, PIECE)), ALU.mult).then_inc(w_hi[s], 1)
                pool.wait_ge(w_hi[s], k + 1)
                pool.tensor_tensor(WL[:, s, :], RAW[:, s, :], f32(WH[:, s, :]), ALU.subtract).then_inc(w_ready[s], 1)

            def split_ctx(n):
                for c in range(KC):
                    src = FSF[:, (c % 2) * T:(c % 2 + 1) * T]
                    pool.wait_ge(c_in[c % 2], 16 * (2 * n + c // 2 + 1))
                    pool.tensor_tensor(CH[:, c, :], src, ONE[:].broadcast_to((P, T)), ALU.mult).then_inc(c_hi, 1)
                    pool.wait_ge(c_hi, KC * n + c + 1)
                    pool.tensor_tensor(CL[:, c, :], src, f32(CH[:, c, :]), ALU.subtract).then_inc(c_ready, 1)

            pool.wait_ge(consts_in, 16 * len(CONSTS))
            for s in range(NSLOT):
                split(s, 0)
            for s in range(3):
                split(s, SLOT["ffn"][s], (ou_full, OU["taylor"] + B) if s else (pj_full, PJ["taylor"] + 4))
            with pool.Fori(1, FG) as i:
                split(0, i + SLOT["ffn"][0], (pj_full, i * 8 + (PJ["ffn"] - 1)))
                split(1, i + SLOT["ffn"][1], (pj_full, i * 8 + PJ["ffn"]))
                split(2, i + SLOT["ffn"][2], (ou_full, i * B + OU["ffn"]))
            split_ctx(0)
            pool.wait_ge(m_ready, 1)
            with pool.Fori(0, HG) as i:
                for s, ahead in enumerate((6, 4, 0)):
                    split(s, i + SLOT["l0x"][s], (pj_full, i * 16 + (PJ["l0x"] - ahead)))
                for hf in range(2):
                    pool.wait_ge(fs_in[hf], i * 16 + 16)
                    for h in range(2):
                        pool.tensor_tensor(FS[:, hf, :, h, :], FS[:, hf, :, h, :], M[:, hf * HB:(hf + 1) * HB, :],
                                           ALU.add).then_inc(fm_ready[hf], 1)
                split(3, i + SLOT["l0x"][3], (ou_full, i * B + OU["l0x"]))
            split(0, SLOT["l0f"][0], (pj_full, PJ["l0x"] + HG * 16 - 6))
            split(1, SLOT["l0f"][1], (pj_full, PJ["l0x"] + HG * 16 - 4))
            split(2, SLOT["l0f"][2], (pj_full, PJ["l0x"] + HG * 16))
            split(3, SLOT["l0f"][3], (ou_full, OU["l0x"] + HG * B))
            split(4, SLOT["l0f"][4], (ou_full, OU["taylor"] + B))
            split(0, SLOT["l0f_up"], (ou_full, OU["l0f"] + B))
            pool.memset(Y[:], 0.0).then_inc(y_zero, 1)
            pool.memset(SQ[:], 0.0).then_inc(y_zero, 1)
            pool.wait_ge(ou_full, OU["l0f"] + 2 * B)
            with pool.Fori(0, HG) as i:
                for s, ahead in enumerate((8, 6, 0, 4)):
                    split(s, i + SLOT["l1a"][s], (pj_full, i * 20 + (PJ["l1a"] - ahead)))
                split(4, i + SLOT["l1a"][4], (ou_full, i * B + OU["l1a"]))
            for s, ahead in enumerate((8, 6, 0, 4)):
                split(s, SLOT["l1x"][s], (pj_full, PJ["l1a"] + HG * 20 - ahead))
            split(4, SLOT["l1x"][4], (ou_full, OU["l1a"] + HG * B))
            pool.wait_ge(la_y, B)
            split_ctx(1)
            pool.wait_ge(pj_full, PJ["l1xv"] + 4)
            for pads in PADS:
                pool.wait_ge(w_deq, 1)
                for t in pads:
                    pool.memset(f32(t), 0.0).then_inc(pads_zero, 1)
            pool.wait_ge(pads_zero, 4)
            pool.wait_ge(pj_done, PJ["l1xv"] + 4)
            pool.wait_ge(kr_lo, 2 * KC)

            def pair(i, first, last):
                def pad_values(bb):
                    hold((pv_full, i * 16 + (PV["l1x"] + 8 * bb - 8)))
                    for t, pad in zip((AH, AL), PADS[bb % 2]):
                        src = f32(t[:, bass.ds(i * 256 + (V1 + bb * P), P)]).rearrange("p (k w) -> p k w", w=HD)
                        pool.tensor_tensor(pad.rearrange("p (k w) -> p k w", w=P)[:, :, 0:HD], src,
                                           ONE[:].unsqueeze(2).broadcast_to((P, KVH, HD)), ALU.mult).then_inc(pad_ready, 1)

                def block_keys(n, part):
                    t, kx = ((CH, KXH), (CL, KXL))[part]
                    if part == 0:
                        hold((sc_full, i * 16 + (SC["l1x"] + 2 * n - 2)))
                    keys = f32(t[:, n % KC, bass.ds(i * 256 + n // KC * S, S)])
                    pool.tensor_tensor(kx[:, n % 2, :].rearrange("p (j s) -> p j s", j=GQ),
                                       keys.unsqueeze(1).broadcast_to((P, GQ, S)),
                                       BM[:].unsqueeze(2).broadcast_to((P, GQ, S)), ALU.mult).then_inc(kx_ready, 1)

                if first:
                    for n in range(2):
                        block_keys(n, 0)
                        block_keys(n, 1)
                    pad_values(0)
                for m in range(16):
                    hold((lx_rc, i * 16 + (m + 1)))
                    p = PR[:, m % 2, :].rearrange("p (h s) -> p h s", h=GQ)
                    pool.tensor_tensor(p, p, RC[:, m % 2 * GQ:(m % 2 + 1) * GQ].unsqueeze(2).broadcast_to((P, GQ, S)),
                                       ALU.mult).then_inc(lx_pn, 1)
                    if not (last and m >= 12):
                        block_keys(m // 2 + 2, m % 2)
                    if m == 6:
                        pad_values(1)
                    if m == 14 and not last:
                        pad_values(2)

            pairs(pool, pair)

        @block.tensor
        def _(pe):
            def mm3(out, w, x, first=True, last=True):
                (wh, wl), (xh, xl) = w, x
                pe.matmul(out, wh, xh, start=first, stop=False)
                pe.matmul(out, wh, xl, start=False, stop=False)
                return pe.matmul(out, wl, xh, start=False, stop=last)

            def pj_free(n):
                if not isinstance(n, int) or n >= 2:
                    pe.wait_ge(pj_done, n - 1)

            def ou_free(n):
                if not isinstance(n, int) or n >= 2:
                    pe.wait_ge(x_done, n - 1)

            def layer_norm(l):
                for b in range(B):
                    n = PJ[f"ln{l}"] + b
                    pe.wait_ge(ln_x, B * l + b + 1)
                    pj_free(n)
                    for c in range(KC):
                        last = pe.transpose(pj[n % 2][:, c * P:(c + 1) * P], PR[:, b % 2, c * P:(c + 1) * P], IDN[:])
                    last.then_inc(pj_full, 1)

            def project(fill, w, x, width=512):
                n, bank = fill
                pj_free(n)
                for c in range(KC):
                    last = mm3(pj[bank][:, 0:width], w(c), x(c), c == 0, c == KC - 1)
                last.then_inc(pj_full, 1)

            def both(ts, f):
                return tuple(f(t) for t in ts)

            XT, C, W, A = (XTH, XTL), (CH, CL), (WH, WL), (AH, AL)

            def wide(x, hf):
                return lambda c: both(x, lambda t: t[:, c, hf * HALF:(hf + 1) * HALF])

            def rows(x, b):
                return lambda c: both(x, lambda t: t[:, c, b * S:(b + 1) * S])

            def wcols(s, j, cols=256, width=P):
                return lambda c: both(W, lambda t: wslot(t, s, cols)[:, c, j * width:(j + 1) * width])

            def wrows(s):
                return lambda c: both(W, lambda t: wpair(t, s, 512)[:, c, :])

            def ready(s, k):
                pe.wait_ge(w_ready[s], k + 1)

            pe.wait_ge(consts_in, 16 * len(CONSTS))
            layer_norm(0)
            ready(0, 0)
            for hf in range(2):
                for j in range(2):
                    project(nth(PJ["taylor"], 0, 0, 2 * hf + j), wcols(0, j), wide(XT, hf))
            for hf in range(2):
                for m in range(TAYLOR):
                    if hf == 0 and m % 2 == 0:
                        ready(1 + m // 2, 0)
                    pe.wait_ge(ta_lo, hf * TAYLOR + m + 1)
                    for b in range(HB):
                        if hf and m == 0 and b >= 2:
                            pe.wait_ge(x_done, b - 1)
                        w = both(W, lambda t: t[:, 1 + m // 2, (m % 2) * 512:(m % 2 + 1) * 512])
                        x = both(A, lambda t: grp(t, m)[:, b * S:(b + 1) * S])
                        last = mm3(taylor_banks[hf][b][:], x, w, m == 0, m == TAYLOR - 1)
                        if m == TAYLOR - 1:
                            last.then_inc(ou_full, 1)
                    if m < TAYLOR - 1:
                        last.then_inc(ta_used, 1)

            def ffn_half(now, before):
                for kind, n in FFN_STEPS:
                    if kind == "F" and now:
                        i, hf = now
                        s, j = n % 2, n // 2
                        if hf == 0 and j == 0:
                            ready(s, i + SLOT["ffn"][s])
                        project(nth(PJ["ffn"], i, 8, hf * 4 + n), wcols(s, j), wide(XT, hf))
                    if kind == "O" and before:
                        i, hf = before
                        m, bank = nth(OU["ffn"], i, B, hf * HB + n)
                        if n == 0:
                            if hf == 0:
                                ready(2, i + SLOT["ffn"][2])
                            pe.wait_ge(ff_lo, i * 4 + (2 * hf + 2))
                        ou_free(m)
                        for j in range(2):
                            last = mm3(ou[bank][:], both(A, lambda t: grp(t, 2 * hf + j)[:, n * S:(n + 1) * S]),
                                       wcols(2, 0, 512, 512)(j), j == 0, j == 1)
                        last.then_inc(ou_full, 1)

            halves(pe, FG, ffn_half)

            layer_norm(1)
            pe.wait_ge(c_ready, KC)

            def l0x_half(now, before):
                for kind, n in L0X_STEPS:
                    if kind in "FS" and now:
                        i, hf = now
                    elif kind in "TVO" and before:
                        i, hf = before
                        t = i * B + (hf * HB + n)
                    else:
                        continue
                    if kind == "F" and n < 4:
                        s, x = ((0, XT), (1, C))[n // 2]
                        if hf == 0 and n % 2 == 0:
                            ready(s, i + SLOT["l0x"][s])
                        project(nth(PJ["l0x"], i, 16, hf * 8 + n), wcols(s, n % 2), wide(x, hf))
                    elif kind == "F":
                        if hf == 0 and n == 4:
                            ready(2, i + SLOT["l0x"][2])
                        project(nth(PJ["l0x"], i, 16, hf * 8 + n), rows(C, hf * HB + n - 4), wcols(2, 0, 256, 256), 256)
                    elif kind == "S":
                        pe.wait_ge(pj_done, i * 16 + (PJ["l0x"] + hf * 8 + 4))
                        pe.wait_ge(sc_done, i * B + (hf * HB + 2))
                        for j in range(HB):
                            for h in range(2):
                                last = mm3(score(j)[:, h * S:(h + 1) * S],
                                           both(A, lambda t: qk(t, 0, h)[:, j * S:(j + 1) * S]),
                                           both(A, lambda t: qk(t, 1, h)[:, j * S:(j + 1) * S]))
                            last.then_inc(sc_full, 1)
                    elif kind == "T":
                        pe.wait_ge(sx_pn, t + 1)
                        pe.wait_ge(tp_done, t + 2)
                        for h in range(2):
                            last = pe.transpose(turned_probs(n)[:, h * S:(h + 1) * S],
                                                part(PR, n)[:, h * S:(h + 1) * S], IDN[:])
                        last.then_inc(tp_full, 1)
                    elif kind == "V":
                        if n == 0:
                            pe.wait_ge(pj_done, i * 16 + (PJ["l0x"] + hf * 8 + 8))
                        pe.wait_ge(tp_done, t + 3)
                        pe.wait_ge(pv_done, t + 1)
                        for h in range(2):
                            last = mm3(pv[:, h * S:(h + 1) * S],
                                       both(A, lambda t: vt(t, n)[:, h * S:(h + 1) * S]),
                                       both(A, lambda t: tile_a(t)[:, h * S:(h + 1) * S]))
                        last.then_inc(pv_full, 1)
                    else:
                        m, bank = nth(OU["l0x"], i, B, hf * HB + n)
                        if hf == 0 and n == 0:
                            ready(3, i + SLOT["l0x"][3])
                        pe.wait_ge(pv_done, t + 2)
                        ou_free(m)
                        for h in range(2):
                            last = mm3(ou[bank][:], both(A, lambda t: tile_b(t)[:, h * S:(h + 1) * S]),
                                       wcols(3, 0, 512, 512)(h), h == 0, h == 1)
                        last.then_inc(ou_full, 1)

            halves(pe, HG, l0x_half)

            layer_norm(2)
            for s in range(2):
                ready(s, SLOT["l0f"][s])
            for b in range(B):
                n, bank = nth(OU["l0f"], 0, 0, b)
                pe.wait_ge(pj_done, PJ["ln2"] + b + 1)
                ou_free(n)
                for c in range(KC):
                    last = mm3(ou[bank][:], rows(XT, b)(c), wrows(0)(c), c == 0, c == KC - 1)
                last.then_inc(ou_full, 1)
            pe.wait_ge(lf_sum, 3)
            for c in range(KC):
                last = pe.matmul(sc[0][:, 0:B], LQ[:, c, :], XM3[:, c, :], start=c == 0, stop=c == KC - 1)
            last.then_inc(lf_pe, 1)
            pe.wait_ge(lf_v, 1)
            pe.matmul(sc[1][0:B, 0:E], LQT[:], KEYS[:], start=True, stop=True).then_inc(lf_pe, 1)
            pe.wait_ge(lf_v, 5)
            pe.transpose(sc[0][0:E, 0:B], LCO[:], IDN[0:B, 0:B]).then_inc(lf_pe, 1)
            pe.wait_ge(lf_v, 6)
            for c in range(KC):
                last = pe.matmul(sc[1][:, c * B:(c + 1) * B], SEL[:, c, :], LCT[:], start=True, stop=True)
            last.then_inc(lf_pe, 1)
            for s in (2, 3, 4):
                ready(s, SLOT["l0f"][s])
            for hf in range(2):
                for e in range(KC):
                    w = lambda c: both(W, lambda t: wpair(t, 2, 512)[:, c, e * P:(e + 1) * P])
                    project(nth(PJ["l0f"], 0, 0, hf * 4 + e), w, wide(XT, hf))
                pe.wait_ge(lf_lo, 4 * hf + 4)
                if hf == 0:
                    ready(0, SLOT["l0f_up"])
                for b in range(HB):
                    n, bank = nth(OU["l0f"], 0, 0, B + hf * HB + b)
                    ou_free(n)
                    for e in range(KC):
                        s = 4 if e < 2 else 0
                        last = mm3(ou[bank][:], both(A, lambda t: grp(t, e)[:, b * S:(b + 1) * S]),
                                   wcols(s, 0, 512, 512)(e % 2), e == 0, e == KC - 1)
                    last.then_inc(ou_full, 1)

            layer_norm(3)

            def l1a_half(now, before):
                for kind, n in L1A_STEPS:
                    if kind in "FS" and now:
                        i, hf = now
                    elif kind in "VO" and before:
                        i, hf = before
                        t = i * B + (hf * HB + n)
                    else:
                        continue
                    if kind == "F" and n < 6:
                        s = (0, 1, 3)[n // 2]
                        if hf == 0 and n % 2 == 0:
                            ready(s, i + SLOT["l1a"][s])
                        project(nth(PJ["l1a"], i, 20, hf * 10 + n), wcols(s, n % 2), wide(XT, hf))
                    elif kind == "F":
                        if hf == 0 and n == 6:
                            ready(2, i + SLOT["l1a"][2])
                        project(nth(PJ["l1a"], i, 20, hf * 10 + n), rows(XT, hf * HB + n - 6), wcols(2, 0, 256, 256), 256)
                    elif kind == "S":
                        pe.wait_ge(la_lo, i * 16 + (hf * 8 + 6))
                        pe.wait_ge(sc_done, i * B + (SC["l1a"] + hf * HB + 2))
                        for j in range(HB):
                            for h in range(2):
                                last = mm3(score(j)[:, h * S:(h + 1) * S],
                                           both(A, lambda t: qk(t, 1, h)[:, j * S:(j + 1) * S]),
                                           both(A, lambda t: qk(t, 0, h)[:, j * S:(j + 1) * S]))
                            last.then_inc(sc_full, 1)
                    elif kind == "V":
                        if n == 0:
                            pe.wait_ge(la_lo, i * 16 + (hf * 8 + 10))
                        pe.wait_ge(la_sdlo, t + 1)
                        pe.wait_ge(pv_done, t + (PV["l1a"] + 1))
                        for h in range(2):
                            last = mm3(pv[:, h * S:(h + 1) * S],
                                       both(A, lambda t: vt(t, n)[:, h * S:(h + 1) * S]),
                                       both(A, lambda t: tile_a(t, n % 2)[:, h * S:(h + 1) * S]))
                        last.then_inc(pv_full, 1)
                    else:
                        m, bank = nth(OU["l1a"], i, B, hf * HB + n)
                        if hf == 0 and n == 0:
                            ready(4, i + SLOT["l1a"][4])
                        pe.wait_ge(la_gflo, t + 1)
                        ou_free(m)
                        for h in range(2):
                            last = mm3(ou[bank][:], both(A, lambda t: tile_b(t)[:, h * S:(h + 1) * S]),
                                       wcols(4, 0, 512, 512)(h), h == 0, h == 1)
                        last.then_inc(ou_full, 1)

            halves(pe, HG, l1a_half)
            pe.wait_ge(la_sqa, HG * B + 2)
            for b in range(B):
                for h in range(2):
                    last = pe.matmul(tp[:, b:b + 1], SQ[:, b, h * S:(h + 1) * S], ONE[:], start=h == 0, stop=h == 1)
            last.then_inc(la_ss, 1)

            layer_norm(4)
            ready(4, SLOT["l1x"][4])
            pe.wait_ge(c_ready, 2 * KC)
            for hf in range(2):
                project(nth(PJ["l1xv"], 0, 0, hf), wcols(4, 0), wide(C, hf))
            for s in (2, 3):
                ready(s, SLOT["l1x"][s])
            pe.wait_ge(sc_done, 2 + SC["l1x"])
            pe.wait_ge(x_done, OU["l1x"])
            for hf in range(2):
                if hf:
                    for f in range(2):
                        n, bank = nth(PJ["l1xv"], 0, 0, 2 + f)
                        pj_free(n)
                        for b in range(HB):
                            last = pe.transpose(pj[bank][:, b * S:(b + 1) * S], TY[f][:, b * S:(b + 1) * S], IDN[:])
                        last.then_inc(pj_full, 1)
                for m, bank in enumerate(key_banks[hf]):
                    if hf and m >= 2:
                        pe.wait_ge(kr_lo, m - 1)
                    for c in range(KC):
                        w = both(W, lambda t: wpair(t, 2, 512)[:, c, m * P:(m + 1) * P])
                        last = mm3(bank[:], w, wide(C, hf)(c), c == 0, c == KC - 1)
                last.then_inc(kr_full, 1)
            for s in (0, 1):
                ready(s, SLOT["l1x"][s])

            def pair(i, first, last):
                def queries(f):
                    w = lambda c: both(W, lambda t: wpair(t, 0, 512)[:, c, f % KC * P:(f % KC + 1) * P])
                    x = lambda c: both(XT, lambda t: t[:, c, bass.ds(i * 256 + f // KC * 256, 256)])
                    project(nth(PJ["l1x"], i, KC, f), w, x, 256)

                def scores(m):
                    bb, c, u = m // 8 % 2, m // 2 % 4, m % 2
                    n, bank = nth(SC["l1x"], i, 16, m)
                    if m % 16 in (0, 2, 4, 6):
                        pe.wait_ge(pj_done, i * KC + (PJ["l1x"] + m // 16 * KC + c + 1))
                    if u == 0:
                        pe.wait_ge(kx_ready, i * 16 + (2 * (m // 2) + 2))
                    pe.wait_ge(lx_exp, i * 16 + (m + 1))
                    r = slice(64 * u, 64 * u + 64)
                    mm3(sc[bank][:], both(A, lambda t: q1(t, c)[r, bb * S:(bb + 1) * S]),
                        both((KXH, KXL), lambda t: t[r, (m // 2) % 2, :])).then_inc(sc_full, 1)

                def transposes(m):
                    n, bank = nth(TP["l1x"], i, 16, m)
                    pe.wait_ge(lx_pn, i * 16 + (m + 1))
                    pe.wait_ge(tp_done, n + 2)
                    for h in range(GQ):
                        done = pe.transpose(tp[:, h * S:(h + 1) * S], PR[:, bank, h * S:(h + 1) * S], IDN[:])
                    done.then_inc(tp_full, 1)

                def values(m):
                    bb, k = m // 8, m % 8
                    out = (pv, ou[1])[bb % 2]
                    n, bank = nth(TP["l1x"], i, 16, m)
                    if k == 0:
                        pe.wait_ge(pad_ready, i * 4 + (2 * bb + 2))
                        if not (first and bb == 0):
                            pe.wait_ge(on_done, i * 2 + bb)
                    pe.wait_ge(tp_done, n + 3)
                    mm3(out[:], tuple(t[:, 112 * k:112 * k + P] for t in PADS[bb % 2]),
                        both(A, lambda t: t[:, PT1 + bank * 512:PT1 + (bank + 1) * 512]),
                        k == 0, k == 7).then_inc(pv_full, 1)

                def output(bb):
                    pe.wait_ge(on_done, i * 2 + (2 + bb))
                    pe.wait_ge(x_done, i * 2 + (OU["l1x"] + bb))
                    for c in range(KC):
                        done = mm3(ou[0][:], both(A, lambda t: t[:, ON1 + c * P:ON1 + (c + 1) * P]),
                                   wrows(2)(c), c == 0, c == KC - 1)
                    done.then_inc(ou_full, 1)

                if first:
                    for c in range(KC):
                        queries(c)
                    scores(0)
                    scores(1)
                for m in range(16):
                    if not (last and m >= 14):
                        scores(m + 2)
                    transposes(m)
                    if not (first and m == 0):
                        values(m - 1)
                    if m == 3 and not first:
                        output(-1)
                    if m == 11:
                        if first:
                            pe.wait_ge(w_ready[3], SLOT["l1x_o"][1] + 1)
                        output(0)
                    if m >= 9 and m % 2 and not last:
                        queries(KC + (m - 9) // 2)
                if last:
                    values(15)
                    output(1)

            pairs(pe, pair)

            pe.wait_ge(w_deq, 1)
            for c in range(KC):
                n, bank = nth(PJ["l1f"], 0, 0, c)
                pj_free(n)
                for o in range(KC):
                    last = pe.transpose(pj[bank][:, o * P:(o + 1) * P], RAW[:, 0:2, :].rearrange("p s (o i) -> p (s o) i", i=512)[:, o, c * P:(c + 1) * P], IDN[:])
                last.then_inc(pj_full, 1)
            layer_norm(5)
            for b in range(B):
                n, bank = nth(OU["l1f"], 0, 0, b)
                pe.wait_ge(pj_done, PJ["ln5"] + b + 1)
                ou_free(n)
                for c in range(KC):
                    last = mm3(ou[bank][:], rows(XT, b)(c), wrows(0)(c), c == 0, c == KC - 1)
                last.then_inc(ou_full, 1)

        @block.scalar
        def _(act):
            def hi(fill, dst, src, scale=1.0):
                act.wait_ge(pj_full, fill[0] + 1)
                act.activation(dst, src, ACT.Copy, scale=scale).then_inc(pj_hi, 1)

            def layer_norm(l):
                act.wait_ge(ln_var, l + 1)
                act.activation(SD[:], VE[:], ACT.Sqrt).then_inc(ln_std, 1)
                for b in range(B):
                    n, bank = nth(PJ[f"ln{l}"], 0, 0, b)
                    hi((n, bank), XTH[:, :, b * S:(b + 1) * S], pj[bank][:].rearrange("p (c s) -> p c s", c=KC))

            act.sem_inc(lx_exp, 2)
            act.sem_inc(la_sq, 1)
            act.wait_ge(consts_in, 16 * len(CONSTS))
            act.activation(CE[:], DC[:], ACT.Exp, scale=-1.0).then_inc(ce_ready, 1)
            layer_norm(0)
            for hf in range(2):
                for m in range(TAYLOR):
                    if hf:
                        act.wait_ge(*((ta_used, m + 1) if m < TAYLOR - 1 else (ou_full, OU["taylor"] + HB)))
                    act.wait_ge(ta_t, hf * TAYLOR + m + 1)
                    act.activation(grp(AH, m), TY[3 * (m % 2)], ACT.Copy,
                                   scale=CE[:, m - 1:m] if m else 1.0).then_inc(ta_hi, 1)

            def ffn_half(now, before):
                for kind, f in FFN_STEPS:
                    if kind == "F" and now:
                        i, hf = now
                        j = f // 2
                        n, bank = nth(PJ["ffn"], i, 8, hf * 4 + f)
                        if f % 2 == 0:
                            act.wait_ge(pj_full, n + 1)
                            act.wait_ge(pj_done, n)
                            act.activation(SG, pj[bank][:], ACT.Sigmoid).then_inc(ff_sg, 1)
                        else:
                            act.wait_ge(pj_done, n + 1)
                            if j == 0:
                                act.wait_ge(ou_full, i * B + (OU["ffn"] + hf * HB - HB))
                            act.activation(grp(AH, 2 * hf + j), HF[j], ACT.Copy).then_inc(ff_hi, 1)

            halves(act, FG, ffn_half)

            layer_norm(1)

            def l0x_half(now, before):
                for kind, n in L0X_STEPS:
                    if kind in "FS" and now:
                        i, hf = now
                    elif kind in "TV" and before:
                        i, hf = before
                        t = i * B + (hf * HB + n)
                    else:
                        continue

                    def exps(j):
                        act.wait_ge(sx_nm, i * B + (hf * HB + j + 9))
                        for h in range(2):
                            p = part(PR, j)[:, h * S:(h + 1) * S]
                            last = act.activation(p, p, ACT.Exp, bias=NM[:, j, h:h + 1], accum_out=SU[:, j, h:h + 1])
                        last.then_inc(sx_exp, 1)

                    if kind == "F":
                        fill = nth(PJ["l0x"], i, 16, hf * 8 + n)
                        bank = pj[fill[1]]
                        if n < 4:
                            hi(fill, qk(AH, n // 2, n % 2), bank[:], S ** -0.5 if n < 2 else 1.0)
                        else:
                            hi(fill, vt(AH, n - 4), bank[:, 0:256])
                        if n in (6, 7):
                            exps(n - 4)
                    elif kind == "S":
                        exps(0)
                        exps(1)
                    elif kind == "T":
                        act.wait_ge(tp_full, t + 1)
                        act.activation(tile_a(AH), turned_probs(n), ACT.Copy).then_inc(pt_hi, 1)
                    else:
                        act.wait_ge(pv_full, t + 1)
                        act.wait_ge(ou_full, t + OU["l0x"])
                        act.activation(tile_b(AH), pv[:, 0:256], ACT.Copy).then_inc(ct_hi, 1)

            halves(act, HG, l0x_half)

            layer_norm(2)
            act.wait_ge(lf_v, 3)
            act.activation(LS[:], sc[1][0:B, 0:E], ACT.Exp, bias=LSM[:, 1:2], scale=P ** -0.5,
                           accum_out=LSM[:, 2:3]).then_inc(lf_a, 1)
            for hf in range(2):
                if hf:
                    act.wait_ge(ou_full, OU["l0f"] + B + HB)
                for e in range(KC):
                    n, bank = nth(PJ["l0f"], 0, 0, hf * 4 + e)
                    act.wait_ge(pj_done, n + 1)
                    act.activation(grp(AH, e), TY[bank], ACT.Copy).then_inc(lf_hi, 1)

            layer_norm(3)
            act.wait_ge(y_zero, 2)

            def l1a_half(now, before):
                def tile_hi(i, hf, j):
                    t = i * B + (hf * HB + j)
                    act.wait_ge(sc_done, t + (SC["l1a"] + 3))
                    act.wait_ge(pv_full, t + (PV["l1a"] - 1))
                    act.activation(tile_a(AH, j % 2), part(PR, j), ACT.Copy).then_inc(la_sdhi, 1)

                def fill_hi(i, hf, f):
                    x = f if f < 4 else f - 2
                    act.wait_ge(pj_done, i * 20 + (PJ["l1a"] + hf * 10 + f + 1))
                    dst = qk(AH, f // 2, f % 2) if f < 4 else vt(AH, f - 6)
                    act.activation(dst, F[:, x % 2, 0:dst.shape[1]], ACT.Copy).then_inc(la_hi, 1)

                for kind, n in L1A_STEPS:
                    if kind in "FS" and now:
                        i, hf = now
                    elif kind == "V" and before:
                        i, hf = before
                        t = i * B + (hf * HB + n)
                    else:
                        continue
                    if kind == "F":
                        m, bank = nth(PJ["l1a"], i, 20, hf * 10 + n)
                        act.wait_ge(pj_full, m + 1)
                        if n in (4, 5):
                            act.wait_ge(pv_done, i * B + (PV["l1a"] + hf * HB + 1))
                            act.activation(G[:, n - 4, :], pj[bank][:], ACT.Sigmoid).then_inc(la_sg, 1)
                        else:
                            x = n if n < 4 else n - 2
                            act.wait_ge(la_lo, i * 16 + (hf * 8 + x + 1))
                            w = 512 if n < 4 else 256
                            act.activation(F[:, x % 2, 0:w], pj[bank][:, 0:w], ACT.Sigmoid).then_inc(la_sg, 1)
                        if n not in (0, 5, 6):
                            fill_hi(i, hf, n - 1)
                        if n == 9:
                            fill_hi(i, hf, 9)
                    elif kind == "S":
                        tile_hi(i, hf, 0)
                        tile_hi(i, hf, 1)
                    else:
                        bank = n % 2
                        act.wait_ge(pv_full, t + (PV["l1a"] + 1))
                        act.wait_ge(la_sqa, t + 1)
                        act.activation(SQT[bank], pv[:, 0:256], ACT.Square).then_inc(la_sq, 1)
                        act.wait_ge(pv_done, t + (PV["l1a"] + 2))
                        act.wait_ge(ou_full, t + OU["l1a"])
                        act.activation(tile_b(AH), GT[bank], ACT.Copy).then_inc(la_gfhi, 1)
                        if n < 2:
                            tile_hi(i, hf, n + 2)

            halves(act, HG, l1a_half)
            act.wait_ge(la_v, 1)
            act.activation(SSD[:], SS[:], ACT.Sqrt).then_inc(la_a, 1)

            layer_norm(4)
            for hf in range(2):
                if hf:
                    for f in range(2):
                        fill = nth(PJ["l1xv"], 0, 0, 2 + f)
                        hi(fill, AH[:, V1 + f * HALF:V1 + (f + 1) * HALF], pj[fill[1]][:])
                act.wait_ge(kr_full, hf + 1)
                for m, bank in enumerate(key_banks[hf]):
                    act.activation(CH[:, m, hf * HALF:(hf + 1) * HALF], bank[:], ACT.Copy).then_inc(kr_hi, 1)
            for s in range(2, 4):
                act.wait_ge(w_in[s], (SLOT["l1x_o"][s - 2] + 1) * 16)
                act.activation(WH[:, s, :], RAW[:, s, :], ACT.Copy).then_inc(w_hi[s], 1)

            def pair(i, first, last):
                def queries(f):
                    fill = nth(PJ["l1x"], i, KC, f)
                    hi(fill, q1(AH, f % KC), pj[fill[1]][:, 0:256])

                def exps(m):
                    n, bank = nth(0, i, 16, m)
                    act.wait_ge(lx_nm, n + 1)
                    for h in range(GQ):
                        at = bank * GQ + h
                        done = act.activation(PR[:, bank, h * S:(h + 1) * S], sc[bank][:, h * S:(h + 1) * S], ACT.Exp,
                                              bias=NM[:, bank, h:h + 1], scale=HD ** -0.5,
                                              accum_out=SUMS[:, at:at + 1])
                    done.then_inc(lx_exp, 1)

                def heads(bb):
                    act.wait_ge(pv_full, i * 16 + (PV["l1x"] + 8 * bb + 8))
                    act.wait_ge(ou_full, i * 2 + (OU["l1x"] + bb))
                    act.activation(AH[:, ON1:ON1 + 512], (pv, ou[1])[bb % 2][:], ACT.Copy).then_inc(lx_on, 1)

                if first:
                    for c in range(KC):
                        queries(c)
                    exps(0)
                for m in range(16):
                    n, bank = nth(TP["l1x"], i, 16, m)
                    if not (last and m == 15):
                        exps(m + 1)
                    if m == 0 and not first:
                        queries(3)
                    if m in (10, 12, 14) and not last:
                        queries(KC + (m - 10) // 2)
                    act.wait_ge(tp_full, n + 1)
                    act.wait_ge(pv_full, i * 16 + (PV["l1x"] + m - 1))
                    act.activation(AH[:, PT1 + bank * 512:PT1 + (bank + 1) * 512], tp[:], ACT.Copy).then_inc(pt_hi, 1)
                    if m == 1 and not first:
                        heads(-1)
                    if m == 9:
                        heads(0)
                if last:
                    heads(1)

            pairs(act, pair)

            for c in range(KC):
                fill = nth(PJ["l1f"], 0, 0, c)
                hi(fill, wpair(WH, 0, 512)[:, c, :], pj[fill[1]][:])
            layer_norm(5)

        @block.vector
        def _(dve):
            def lo(fill, hi_at, dst, src, hi_part, scale=None):
                dve.wait_ge(pj_hi, hi_at + 1)
                if scale is None:
                    dve.tensor_tensor(dst, src, f32(hi_part), ALU.subtract).then_inc(pj_done, 1)
                else:
                    dve.scalar_tensor_tensor(dst, src, scale, f32(hi_part), ALU.mult, ALU.subtract).then_inc(pj_done, 1)

            def add_output(n, bank, dst):
                dve.wait_ge(ou_full, n + 1)
                dve.tensor_tensor(dst, dst, ou[bank][:], ALU.add).then_inc(x_done, 1)

            def add_output_b(n, bank, b):
                add_output(n, bank, X[:, b, :])

            def add_last(n, bank, b):
                add_output(n, bank, X[:, b, :])
                dve.wait_ge(x_done, n + 1)
                dve.bn_stats(ST[:, b, :], X[:, b, :]).then_inc(ln_stat, 1)

            def layer_norm(l):
                if l == 4:
                    dve.wait_ge(la_y, B)
                elif l:
                    dve.wait_ge(x_done, OU[{1: "l0x", 2: "l0f", 3: "l1a", 5: "l1f"}[l]])
                if l in (0, 4):
                    for b in range(B):
                        dve.bn_stats(ST[:, b, :], X[:, b, :]).then_inc(ln_stat, 1)
                dve.wait_ge(ln_stat, B * (l + 1))
                for b in range(B):
                    last = dve.bn_aggr(MV[:, b, :], ST[:, b, :])
                last.then_inc(ln_aggr, 1)
                dve.wait_ge(ln_aggr, l + 1)
                dve.tensor_scalar(VE[:], MV[:, :, 1], EPS, None, ALU.add).then_inc(ln_var, 1)
                dve.wait_ge(ln_std, l + 1)
                dve.reciprocal(RS[:], SD[:]).then_inc(ln_rstd, 1)
                dve.wait_ge(ln_rstd, l + 1)

                def turned(b):
                    n, bank = nth(PJ[f"ln{l}"], 0, 0, b)
                    at = (slice(None), slice(None), slice(b * S, (b + 1) * S))
                    lo((n, bank), HI[f"ln{l}"] + b, XTL[at], pj[bank][:].rearrange("p (c s) -> p c s", c=KC), XTH[at])

                for b in range(B):
                    if b >= 2:
                        dve.wait_ge(pj_full, PJ[f"ln{l}"] + b - 1)
                    dve.tensor_scalar(PR[:, b % 2, :], X[:, b, :], MV[:, b, 0:1], RS[:, b:b + 1],
                                      ALU.subtract, ALU.mult).then_inc(ln_x, 1)
                    if b >= 2:
                        turned(b - 2)
                turned(B - 2)
                turned(B - 1)

            def dequantise():
                steps = [0]

                def step(ins):
                    steps[0] += 1
                    ins.then_inc(dq, 1)
                    dve.wait_ge(dq, steps[0])

                SHR, SHL, AND, OR = ALU.logical_shift_right, ALU.logical_shift_left, ALU.bitwise_and, ALU.bitwise_or
                step(dve.tensor_copy(QI[:], Q3[:].bitcast(U8).rearrange("p o (n k) -> p o n k", k=3)))
                byte = [QI[:, :, :, k] for k in range(3)]
                fields = [((0, 0, 7),), ((0, 3, 7),), ((0, 6, 3), (1, 1, 2)), ((1, 1, 7),), ((1, 4, 7),),
                          ((1, 7, 1), (2, 3, 1)), ((2, 2, 7),), ((2, 5, 7),)]
                dve.wait_ge(w_ready[0], SLOT["l1x"][0] + 1)
                dve.wait_ge(w_ready[1], SLOT["l1x"][1] + 1)
                w = RAW[:, 0:2, :].rearrange("p s (n v) -> p (s n) v", v=8)
                for v, field in enumerate(fields):
                    k, shift, mask = field[0]
                    step(dve.tensor_scalar(QT[:], byte[k], shift, mask, SHR, AND))
                    if len(field) > 1:
                        k, mask, shift = field[1]
                        step(dve.tensor_scalar(QU[:], byte[k], mask, shift, AND, SHL))
                        step(dve.tensor_tensor(QT[:], QT[:], QU[:], OR))
                    step(dve.tensor_copy(w[:, :, v], QT[:].rearrange("p o n -> p (o n)")))
                norm = QN[:].rearrange("p o g -> p (o g)")
                step(dve.tensor_tensor(QN2[:], norm, norm, ALU.add))
                wf = RAW[:, 0:2, :].rearrange("p s n -> p (s n)")
                wg = RAW[:, 0:2, :].rearrange("p s (g n) -> p (s g) n", n=32)
                step(dve.tensor_scalar(wf, wf, 1.0 / 7.0, None, ALU.mult))
                step(dve.tensor_tensor(wg, wg, QN2[:].unsqueeze(2).broadcast_to((P, 64, 32)), ALU.mult))
                dve.tensor_tensor(wg, wg, norm.unsqueeze(2).broadcast_to((P, 64, 32)), ALU.subtract).then_inc(w_deq, 1)

            dve.sem_inc(sc_done, 2)
            dve.sem_inc(tp_done, 2)
            dve.sem_inc(pv_done, 1)
            dve.sem_inc(sx_nm, B)
            dve.sem_inc(la_lo, 2)
            dve.sem_inc(la_sqa, 2)
            dve.sem_inc(on_done, 1)
            dve.wait_ge(x_in, 32)

            dve.wait_ge(ce_ready, 1)
            layer_norm(0)

            def taylor_outputs(hf):
                for b in range(HB):
                    dve.wait_ge(ou_full, OU["taylor"] + hf * HB + b + 1)
                    xb = X[:, hf * HB + b, :]
                    dve.tensor_tensor(xb, xb, taylor_banks[hf][b][:], ALU.add).then_inc(x_done, 1)

            for hf in range(2):
                up, delta, keep = TY[0], TY[1], TY[2]
                n0, bank0 = nth(PJ["taylor"], 0, 0, 2 * hf)
                dve.wait_ge(pj_full, n0 + 1)
                if hf:
                    dve.wait_ge(ta_lo, TAYLOR)
                dve.tensor_copy(up, pj[bank0][:]).then_inc(ta_t, 1)
                dve.wait_ge(pj_full, n0 + 2)
                dve.wait_ge(ta_t, hf * TAYLOR + 1)
                dve.tensor_scalar(delta, pj[1 - bank0][:], LP[:], None, ALU.subtract).then_inc(ta_d, 1)
                dve.wait_ge(ta_d, hf + 1)
                dve.tensor_scalar(keep, delta, -2.5, None, ALU.is_ge).then_inc(pj_done, 1)
                dve.wait_ge(pj_done, n0 + 1)
                dve.scalar_tensor_tensor(keep, delta, 2.5, keep, ALU.is_le, ALU.mult).then_inc(pj_done, 1)
                if hf:
                    taylor_outputs(0)
                for m in range(TAYLOR):
                    if m + 1 < TAYLOR:
                        src, dst = TY[3 * (m % 2)], TY[3 * ((m + 1) % 2)]
                        dve.wait_ge(ta_t, hf * TAYLOR + m + 1)
                        if hf * TAYLOR + m:
                            dve.wait_ge(ta_lo, hf * TAYLOR + m)
                        if m + 1 == 5:
                            dve.tensor_tensor(dst, src, delta, ALU.mult).then_inc(ta_k, 1)
                            dve.wait_ge(ta_k, hf + 1)
                            dve.tensor_tensor(dst, dst, keep, ALU.mult).then_inc(ta_t, 1)
                        else:
                            dve.tensor_tensor(dst, src, delta, ALU.mult).then_inc(ta_t, 1)
                    dve.wait_ge(ta_hi, hf * TAYLOR + m + 1)
                    if m:
                        dve.scalar_tensor_tensor(grp(AL, m), TY[3 * (m % 2)], CE[:, m - 1:m], f32(grp(AH, m)),
                                                 ALU.mult, ALU.subtract).then_inc(ta_lo, 1)
                    else:
                        dve.tensor_tensor(grp(AL, m), TY[0], f32(grp(AH, m)), ALU.subtract).then_inc(ta_lo, 1)
                if hf:
                    taylor_outputs(1)

            def ffn_half(now, before):
                def chunk_lo(i, hf, j):
                    dve.wait_ge(ff_hi, i * 4 + (2 * hf + j + 1))
                    g = 2 * hf + j
                    dve.tensor_tensor(grp(AL, g), HF[j], f32(grp(AH, g)), ALU.subtract).then_inc(ff_lo, 1)

                for kind, f in FFN_STEPS:
                    if kind == "F" and now:
                        i, hf = now
                        j = f // 2
                        n, bank = nth(PJ["ffn"], i, 8, hf * 4 + f)
                        if f % 2 == 0:
                            dve.wait_ge(ff_sg, i * 4 + (2 * hf + j + 1))
                            dve.wait_ge(pj_done, n)
                            dve.tensor_tensor(HF[j], pj[bank][:], SG, ALU.mult).then_inc(pj_done, 1)
                            if j:
                                chunk_lo(i, hf, 0)
                        else:
                            dve.wait_ge(pj_full, n + 1)
                            dve.wait_ge(pj_done, n)
                            dve.tensor_tensor(HF[j], HF[j], pj[bank][:], ALU.mult).then_inc(pj_done, 1)
                    if kind == "O" and before:
                        if now and f == 2:
                            chunk_lo(*now, 1)
                        i, hf = before
                        m, bank = nth(OU["ffn"], i, B, hf * HB + f)
                        (add_last if isinstance(i, int) and i == FG - 1 else add_output_b)(m, bank, hf * HB + f)
                if now and not before:
                    chunk_lo(*now, 1)

            halves(dve, FG, ffn_half)

            dve.wait_ge(mask_in, 16)
            dve.tensor_scalar(MF, MI[:].bitcast(U8).rearrange("p b s -> p (b s)"), -1.0, MASKED,
                              ALU.add, ALU.mult).then_inc(m_ready, 1)
            layer_norm(1)

            def l0x_half(now, before):
                def biased_max(i, hf, j):
                    t = i * B + (hf * HB + j)
                    dve.wait_ge(fm_ready[hf], i * 2 + 2)
                    dve.wait_ge(sc_full, i * B + (hf * HB + 2 * (j // 2) + 2))
                    dve.sem_inc(dve_gate, 1)
                    for h in range(2):
                        last = dve.tensor_tensor_reduce(
                            out=part(PR, j)[:, h * S:(h + 1) * S], in0=score(j)[:, h * S:(h + 1) * S],
                            in1=FS[:, hf, j, h, :], scale=1.0, scalar=-3e38, op0=ALU.add, op1=ALU.max,
                            accum_out=MX[:, j, h:h + 1])
                    last.then_inc(sc_done, 1)
                    dve.wait_ge(sc_done, t + 3)
                    dve.tensor_scalar(NM[:, j, 0:2], MX[:, j, 0:2], -1.0, MASKED / 10,
                                      ALU.mult, ALU.min).then_inc(sx_nm, 1)

                def normalise(i, hf, j):
                    t = i * B + (hf * HB + j)
                    dve.wait_ge(sx_exp, t + 1)
                    dve.tensor_scalar(SM[:], SU[:, j, :], 1e-30, None, ALU.max).then_inc(sx_sm, 1)
                    dve.wait_ge(sx_sm, t + 1)
                    dve.reciprocal(RC[:, 0:2], SM[:]).then_inc(sx_rc, 1)
                    dve.wait_ge(sx_rc, t + 1)
                    p = part(PR, j).rearrange("p (h s) -> p h s", h=2)
                    dve.tensor_tensor(p, p, RC[:, 0:2].unsqueeze(2).broadcast_to((P, 2, S)), ALU.mult).then_inc(sx_pn, 1)

                for kind, n in L0X_STEPS:
                    if kind in "FS" and now:
                        i, hf = now
                    elif kind in "TVO" and before:
                        i, hf = before
                        t = i * B + (hf * HB + n)
                    else:
                        continue
                    if kind == "F":
                        fill = nth(PJ["l0x"], i, 16, hf * 8 + n)
                        at = i * 16 + (HI["l0x"] + hf * 8 + n)
                        bank = pj[fill[1]]
                        if n < 4:
                            lo(fill, at, qk(AL, n // 2, n % 2), bank[:], qk(AH, n // 2, n % 2), S ** -0.5 if n < 2 else None)
                        else:
                            lo(fill, at, vt(AL, n - 4), bank[:, 0:256], vt(AH, n - 4))
                        if n in (5, 6):
                            biased_max(i, hf, n - 3)
                    elif kind == "S":
                        biased_max(i, hf, 0)
                        biased_max(i, hf, 1)
                        normalise(i, hf, 0)
                    elif kind == "T":
                        dve.wait_ge(pt_hi, t + 1)
                        dve.tensor_tensor(tile_a(AL), turned_probs(n), f32(tile_a(AH)), ALU.subtract).then_inc(tp_done, 1)
                        if n + 1 < HB:
                            normalise(i, hf, n + 1)
                    elif kind == "V":
                        dve.wait_ge(ct_hi, t + 1)
                        dve.tensor_tensor(tile_b(AL), pv[:, 0:256], f32(tile_b(AH)), ALU.subtract).then_inc(pv_done, 1)
                    else:
                        m, bank = nth(OU["l0x"], i, B, hf * HB + n)
                        (add_last if isinstance(i, int) and i == HG - 1 else add_output_b)(m, bank, hf * HB + n)

            halves(dve, HG, l0x_half)

            layer_norm(2)
            dve.wait_ge(pj_done, PJ["ln2"] + B)
            for dst, t in ((XM, XTH), (XM2, XTL)):
                dve.tensor_reduce(dst[:].rearrange("p c b -> p (c b)"),
                                  f32(t[:]).rearrange("p c (b s) -> p (c b) s", b=B), axis=AX.X, op=ALU.add).then_inc(lf_sum, 1)
            dve.wait_ge(lf_sum, 2)
            dve.tensor_tensor(XM3[:], XM[:], XM2[:], ALU.add).then_inc(lf_sum, 1)
            for b in range(B):
                n, bank = nth(OU["l0f"], 0, 0, b)
                add_output(n, bank, X[:, b, :])
            dve.wait_ge(lf_pe, 1)
            dve.tensor_scalar(LQT[:], sc[0][:, 0:B], 1.0 / S, None, ALU.mult).then_inc(lf_v, 1)
            dve.wait_ge(lf_pe, 2)
            dve.tensor_reduce(LSM[:, 0:1], sc[1][0:B, 0:E], axis=AX.X, op=ALU.max).then_inc(lf_v, 1)
            dve.wait_ge(lf_v, 2)
            dve.tensor_scalar(LSM[:, 1:2], LSM[:, 0:1], -P ** -0.5, None, ALU.mult).then_inc(lf_v, 1)
            dve.wait_ge(lf_a, 1)
            dve.reciprocal(LSM[:, 3:4], LSM[:, 2:3]).then_inc(lf_v, 1)
            dve.wait_ge(lf_v, 4)
            dve.tensor_scalar(LCO[:], LS[:], LSM[:, 3:4], None, ALU.mult).then_inc(lf_v, 1)
            dve.wait_ge(lf_pe, 3)
            dve.tensor_copy(LCT[:], sc[0][0:E, 0:B]).then_inc(lf_v, 1)
            dve.wait_ge(lf_pe, 4)
            dve.tensor_copy(LCR[:].rearrange("p c b -> p (c b)"), sc[1][:, 0:KC * B]).then_inc(lf_v, 1)
            dve.wait_ge(lf_v, 7)
            for hf in range(2):
                for e in range(KC):
                    n, bank = nth(PJ["l0f"], 0, 0, hf * 4 + e)
                    dve.wait_ge(pj_full, n + 1)
                    dve.tensor_tensor(TY[bank].rearrange("p (b s) -> p b s", b=HB),
                                      pj[bank][:].rearrange("p (b s) -> p b s", b=HB),
                                      LCR[:, e, hf * HB:(hf + 1) * HB].unsqueeze(2).broadcast_to((P, HB, S)),
                                      ALU.mult).then_inc(pj_done, 1)
                    dve.wait_ge(lf_hi, hf * 4 + e + 1)
                    dve.tensor_tensor(grp(AL, e), TY[bank], f32(grp(AH, e)), ALU.subtract).then_inc(lf_lo, 1)
                for b in range(HB):
                    n, bank = nth(OU["l0f"], 0, 0, B + hf * HB + b)
                    add_last(n, bank, hf * HB + b)

            layer_norm(3)
            dve.wait_ge(y_zero, 2)

            def l1a_half(now, before):
                def fill_lo(i, hf, f):
                    x = f if f < 4 else f - 2
                    at = (lambda t: qk(t, f // 2, f % 2)) if f < 4 else (lambda t: vt(t, f - 6))
                    dve.wait_ge(la_hi, i * 16 + (hf * 8 + x + 1))
                    dve.tensor_tensor(at(AL), F[:, x % 2, 0:at(AL).shape[1]], f32(at(AH)), ALU.subtract).then_inc(la_lo, 1)

                def decayed(i, hf, j):
                    t = i * B + (hf * HB + j)
                    if hf == 0 and j == 0:
                        dve.wait_ge(dt_in, i * 16 + 16)
                    dve.wait_ge(sc_full, i * B + (SC["l1a"] + hf * HB + 2 * (j // 2) + 2))
                    dve.tensor_tensor(part(PR, j), score(j), DT[:], ALU.mult).then_inc(sc_done, 1)

                def tile_lo(i, hf, j):
                    t = i * B + (hf * HB + j)
                    dve.wait_ge(la_sdhi, t + 1)
                    dve.tensor_tensor(tile_a(AL, j % 2), part(PR, j), f32(tile_a(AH, j % 2)),
                                      ALU.subtract).then_inc(la_sdlo, 1)

                for kind, n in L1A_STEPS:
                    if kind in "FS" and now:
                        i, hf = now
                    elif kind in "VO" and before:
                        i, hf = before
                        t = i * B + (hf * HB + n)
                    else:
                        continue
                    if kind == "F":
                        m, bank = nth(PJ["l1a"], i, 20, hf * 10 + n)
                        dve.wait_ge(la_sg, m + (1 - PJ["l1a"]))
                        if n in (4, 5):
                            g = G[:, n - 4, :]
                            dve.tensor_scalar(g, g, NW[:, bass.ds(i * 2 + (n - 4), 1)], None, ALU.mult).then_inc(pj_done, 1)
                        else:
                            x = n if n < 4 else n - 2
                            w = 512 if n < 4 else 256
                            dve.tensor_tensor(F[:, x % 2, 0:w], F[:, x % 2, 0:w], pj[bank][:, 0:w],
                                              ALU.mult).then_inc(pj_done, 1)
                        if n not in (0, 5, 6):
                            fill_lo(i, hf, n - 1)
                        if n in (6, 7):
                            tile_lo(i, hf, n - 6)
                            decayed(i, hf, n - 4)
                        if n == 9:
                            fill_lo(i, hf, 9)
                    elif kind == "S":
                        decayed(i, hf, 0)
                        decayed(i, hf, 1)
                    elif kind == "V":
                        bank, b = n % 2, hf * HB + n
                        dve.wait_ge(la_sq, t + 2)
                        dve.tensor_tensor(GT[bank].rearrange("p (h s) -> p h s", h=2),
                                          pv[:, 0:256].rearrange("p (h s) -> p h s", h=2),
                                          G[:, :, n * S:(n + 1) * S], ALU.mult).then_inc(pv_done, 1)
                        dve.tensor_tensor(SQ[:, b, :], SQ[:, b, :], SQT[bank], ALU.add).then_inc(la_sqa, 1)
                        dve.wait_ge(la_gfhi, t + 1)
                        dve.tensor_tensor(tile_b(AL), GT[bank], f32(tile_b(AH)), ALU.subtract).then_inc(la_gflo, 1)
                        if n < 2:
                            tile_lo(i, hf, n + 2)
                    else:
                        m, bank = nth(OU["l1a"], i, B, hf * HB + n)
                        add_output(m, bank, Y[:, hf * HB + n, :])

            halves(dve, HG, l1a_half)
            dve.wait_ge(la_ss, 1)
            dve.tensor_scalar(SS[:], tp[:, 0:B], 1.0 / (2 * HG * P), EPS, ALU.mult, ALU.add).then_inc(la_v, 1)
            dve.wait_ge(la_a, 1)
            dve.reciprocal(YR[:], SSD[:]).then_inc(la_v, 1)
            dve.wait_ge(la_v, 2)
            for b in range(B):
                dve.scalar_tensor_tensor(X[:, b, :], Y[:, b, :], YR[:, b:b + 1], X[:, b, :],
                                         ALU.mult, ALU.add).then_inc(la_y, 1)

            layer_norm(4)
            for hf in range(2):
                n, bank = nth(PJ["l1xv"], 0, 0, hf)
                dve.wait_ge(pj_full, n + 1)
                dve.tensor_copy(TY[hf], pj[bank][:]).then_inc(pj_done, 1)
            dequantise()
            for hf in range(2):
                if hf:
                    for f in range(2):
                        fill = nth(PJ["l1xv"], 0, 0, 2 + f)
                        at = slice(V1 + f * HALF, V1 + (f + 1) * HALF)
                        lo(fill, HI["l1xv"] + f, AL[:, at], pj[fill[1]][:], AH[:, at])
                at = slice(hf * HALF, (hf + 1) * HALF)
                for m, bank in enumerate(key_banks[hf]):
                    dve.wait_ge(kr_hi, hf * KC + m + 1)
                    dve.tensor_tensor(CL[:, m, at], bank[:], f32(CH[:, m, at]), ALU.subtract).then_inc(kr_lo, 1)
            for s in range(2, 4):
                dve.wait_ge(w_hi[s], SLOT["l1x_o"][s - 2] + 1)
                dve.tensor_tensor(WL[:, s, :], RAW[:, s, :], f32(WH[:, s, :]), ALU.subtract).then_inc(w_ready[s], 1)

            def pair(i, first, last):
                def queries(f):
                    fill = nth(PJ["l1x"], i, KC, f)
                    lo(fill, i * KC + (HI["l1x"] + f), q1(AL, f % KC), pj[fill[1]][:, 0:256], q1(AH, f % KC))

                def row_max(m):
                    n, bank = nth(SC["l1x"], i, 16, m)
                    dve.wait_ge(sc_full, n + 1)
                    dve.tensor_reduce(MX[:, bank, :], sc[bank][:].rearrange("p (h s) -> p h s", h=GQ),
                                      axis=AX.X, op=ALU.max).then_inc(lx_max, 1)
                    dve.wait_ge(lx_max, i * 16 + (m + 1))
                    dve.tensor_scalar(NM[:, bank, :], MX[:, bank, :], -HD ** -0.5, None, ALU.mult).then_inc(lx_nm, 1)

                def row_recip(m):
                    dve.wait_ge(lx_exp, i * 16 + (m + 3))
                    at = slice(m % 2 * GQ, (m % 2 + 1) * GQ)
                    dve.reciprocal(RC[:, at], SUMS[:, at]).then_inc(lx_rc, 1)

                def turned_lo(m):
                    n, bank = nth(TP["l1x"], i, 16, m)
                    dve.wait_ge(pt_hi, n + 1)
                    at = slice(PT1 + bank * 512, PT1 + (bank + 1) * 512)
                    dve.tensor_tensor(AL[:, at], tp[:], f32(AH[:, at]), ALU.subtract).then_inc(tp_done, 1)

                def heads(bb):
                    dve.wait_ge(lx_on, i * 2 + (bb + 1))
                    at = slice(ON1, ON1 + 512)
                    dve.tensor_tensor(AL[:, at], (pv, ou[1])[bb % 2][:], f32(AH[:, at]), ALU.subtract).then_inc(on_done, 1)

                def add(bb):
                    n = i * 2 + (OU["l1x"] + bb)
                    rows = X[:, bass.ds(i * 2 + bb, 1), :].rearrange("p a d -> p (a d)")
                    add_output(n, 0, rows)
                    dve.wait_ge(x_done, n + 1)
                    dve.bn_stats(ST[:, bass.ds(i * 2 + bb, 1), :].rearrange("p a d -> p (a d)"), rows).then_inc(ln_stat, 1)

                if first:
                    for c in range(KC):
                        queries(c)
                    row_max(0)
                for m in range(16):
                    if not (last and m == 15):
                        row_max(m + 1)
                    row_recip(m)
                    if not (first and m == 0):
                        turned_lo(m - 1)
                    if m == 0 and not first:
                        queries(3)
                    if m in (10, 12, 14) and not last:
                        queries(KC + (m - 10) // 2)
                    if m == 2 and not first:
                        heads(-1)
                    if m == 10:
                        heads(0)
                    if m == 5 and not first:
                        add(-1)
                    if m == 13:
                        add(0)
                if last:
                    turned_lo(15)
                    heads(1)
                    add(1)

            pairs(dve, pair)

            for c in range(KC):
                fill = nth(PJ["l1f"], 0, 0, c)
                lo(fill, HI["l1f"] + c, wpair(WL, 0, 512)[:, c, :], pj[fill[1]][:], wpair(WH, 0, 512)[:, c, :])
            layer_norm(5)
            for b in range(B):
                dve.tensor_tensor(X[:, b, :], X[:, b, :], BIAS[:], ALU.add).then_inc(bias_added, 1)
            for b in range(B):
                n, bank = nth(OU["l1f"], 0, 0, b)
                dve.wait_ge(bias_added, b + 1)
                add_output(n, bank, X[:, b, :])


def arr(a):
    return np.ascontiguousarray(a)


def blocks(w):
    return w.reshape(-1, P, w.shape[-1]).transpose(1, 0, 2)


def kernel(**inputs):
    import concourse.bacc as bacc
    from concourse.bass_utils import run_bass_kernel_spmd as run

    g = {k: np.asarray(v) for k, v in inputs.items()}
    L0, L1 = "L0_attn_", "L1_attn_"
    tw = np.zeros((NSLOT, P, PIECE), np.float32)
    tw[0] = blocks(np.concatenate([g[L0 + "up_w"].T, g[L0 + "gate_w"].T], 1)).reshape(P, PIECE)
    terms = [g[L0 + "local_approx_output"].T] + [g[L0 + "fuse_weight"][:, :, m].T for m in range(6)]
    for m, t in enumerate(terms):
        tw[1 + m // 2, :, (m % 2) * 512:(m % 2 + 1) * 512] = t
    fp = [np.zeros((FPAD, D), np.float32) for _ in range(3)]
    for dst, src in zip(fp, (g[L0 + "ffn_gate_w"], g[L0 + "ffn_up_w"], g[L0 + "ffn_down_w"].T)):
        dst[:src.shape[0]] = src

    def in_cols(w):
        return w.reshape(-1, 256, KC, P).transpose(0, 3, 2, 1).reshape(-1, P, PIECE)

    def out_rows(w):
        return w.reshape(-1, 2, P, 512).transpose(0, 2, 1, 3).reshape(-1, P, PIECE)

    def square(w):
        return blocks(w).reshape(P, 2, PIECE).transpose(1, 0, 2)

    ffn = np.stack([in_cols(fp[0]), in_cols(fp[1]), out_rows(fp[2])], 1)
    X0 = "L0_xattn_"
    l0x = np.stack([in_cols(g[X0 + n].T) for n in ("Wq", "Wk", "Wv")] + [out_rows(g[X0 + "Wo"])], 1)
    F0 = "L0_ffn_"
    l0f = np.concatenate([square(g[F0 + "W_org"].T),
                          square(g[F0 + "lora_down"].transpose(1, 0, 2).reshape(D, E * R)),
                          square(g[F0 + "lora_up"].reshape(E * R, D))])
    qkv = g[L1 + "qkv_w"].reshape(2 * HG, 3, P, D).transpose(1, 0, 2, 3).reshape(3, 2 * HG * P, D)
    l1a = np.stack([in_cols(qkv[n]) for n in range(3)] + [in_cols(g[L1 + "gate_w"]), out_rows(g[L1 + "out_w"].T)], 1)
    X1 = "L1_xattn_"
    wk = np.repeat(g[X1 + "Wk"].reshape(D, KVH, 1, HD), GQ, 2).reshape(D, D)
    wv = np.zeros((D, 256), np.float32)
    wv[:, :P] = g[X1 + "Wv"]
    wo = g[X1 + "Wo"].reshape(KVH, GQ, HD, D).transpose(1, 0, 2, 3).reshape(D, D)
    l1x = np.concatenate([square(g[X1 + "Wq"]), square(wk), blocks(wv).reshape(1, P, PIECE), square(wo)])
    side = g["fside_Bx32xSxS2_0"].reshape(2, HB, HG, 2, S, S).transpose(2, 0, 4, 1, 3, 5).reshape(HG, 2, P, 1024)
    q3 = g["L1_ffn_weight_q3"].reshape(D, 16 * 12).view(np.int32).reshape(4, P, 48).transpose(1, 0, 2)
    q3n = g["L1_ffn_weight_norm"].reshape(4, P, 16).transpose(1, 0, 2)
    slope = (1.0 / 2.0 ** (8.0 / 32)) ** (np.arange(32) + 1.0) * (1.0 - 1 / (32 - 1 + 1e-05) + 1e-05)
    diff = np.arange(S)[None, :] - np.arange(S)[:, None]
    decay = np.where(diff >= 0, np.exp(-slope[:, None, None] * np.maximum(diff, 0)), 0.0).astype(np.float32)
    decay = decay.reshape(HG, 2, P, S).transpose(0, 2, 1, 3).reshape(HG, P, 256)
    experts = (np.arange(E * R)[None, :] // R == np.arange(E)[:, None]).astype(np.float32)
    arrays = dict(
        x=g["x"], ctx_t=g["ctx_4096"].reshape(T, KC, P).transpose(1, 2, 0), side=side,
        mask=g["mask_BxSxS2_bk0"].view(np.int32).transpose(1, 0, 2),
        taylor_w=tw, ffn_w=ffn, l0x_w=l0x, l0f_w=l0f, l1a_w=l1a, l1x_w=l1x,
        identity=np.eye(P, dtype=np.float32), local_point=g[L0 + "local_point"].reshape(P, 1),
        discount=np.broadcast_to(g[L0 + "discount_factor"], (P, 6)),
        bias=np.broadcast_to(g["L1_ffn_bias"], (P, D)), lora_keys=g[F0 + "lora_keys"].T,
        lora_wq=blocks(g[F0 + "Wq"].T), expert_rows=experts.reshape(E, KC, P),
        norm_w=g[L1 + "norm_w"].reshape(2 * HG, P).T, one=np.ones((P, 1), np.float32),
        block_mask=(np.arange(P)[:, None] % 64 // HD == np.arange(GQ)[None, :]).astype(np.float32),
        q3=q3, q3_norm=q3n, decay=decay)
    nc = bacc.Bacc("TRN2", target_bir_lowering=False, num_devices=1)
    sent, aps = {}, {}
    for name, v in arrays.items():
        v = arr(v)
        sent["in_" + name] = v
        aps[name] = nc.dram_tensor("in_" + name, v.shape, mybir.dt.from_np(v.dtype), kind="ExternalInput").ap()
    aps["out"] = nc.dram_tensor("out_x", (B, S, D), FP32, kind="ExternalOutput").ap()
    build(nc, aps)
    r = run(nc, [sent], core_ids=[0])
    return r.results[0]["out_x"]
```
